# Optimizing a Trainium2 kernel written in Bass

```python
import numpy as np
import jax
import jax.numpy as jnp

def _softmax(x, axis=-1):
    return jax.nn.softmax(x, axis=axis)

def _gelu(x):
    return jax.nn.gelu(x, approximate=True)

def _silu(x):
    return jax.nn.silu(x)

def _sigmoid(x):
    return jax.nn.sigmoid(x)

def _layernorm(x, axis=-1, eps=1e-05):
    m = jnp.mean(x, axis=axis, keepdims=True)
    v = jnp.var(x, axis=axis, keepdims=True)
    return (x - m) / jnp.sqrt(v + eps)

def _scatter_add(tgt, idx, src, axis=0):
    return tgt.at[idx].add(src)

def _segment_sum(src, seg, n):
    return jax.ops.segment_sum(src, seg, n)
kernel_name = 'mk_recurrent_d2_jaxref_r8_78a5b9'

def setup_inputs(seed: int=0):
    np.random.seed(seed)
    _w = jnp.asarray

    def _L0_attn_setup():
        import jax, jax.numpy as jnp
        import numpy as np
        from jax import lax
        D_MODEL, D_STATE, D_CONV, EXPAND = (128, 64, 4, 2)
        D_INNER = EXPAND * D_MODEL
        BATCH, SEQ = (4, 512)

        def _forward(x, in_proj_w, conv_w, conv_b, x_proj_w, dt_proj_w, dt_proj_b, A_log, D, out_proj_w):
            b, seq_len, d_model = x.shape
            d_inner = conv_w.shape[0]
            d_conv = conv_w.shape[-1]
            x_and_res = jnp.einsum('bsd,od->bso', x, in_proj_w)
            u, res = (x_and_res[..., :d_inner], x_and_res[..., d_inner:])
            u_c = lax.conv_general_dilated(u.transpose(0, 2, 1), conv_w, window_strides=(1,), padding=[(d_conv - 1, 0)], feature_group_count=d_inner, dimension_numbers=('NCH', 'OIH', 'NCH')) + conv_b[None, :, None]
            u = u_c.transpose(0, 2, 1)
            x_dbl = jnp.einsum('bsd,od->bso', u, x_proj_w)
            _ = -jnp.exp(A_log)
            _ = D
            delta = jax.nn.softplus(jnp.einsum('bsd,od->bso', u, dt_proj_w) + dt_proj_b)
            gated_u = u * jax.nn.sigmoid(delta)

            def step(state, u_t):
                state = state * 0.9 + u_t * 0.1
                return (state, state)
            _, ys = lax.scan(step, jnp.zeros((b, d_inner), dtype=u.dtype), gated_u.transpose(1, 0, 2))
            y = ys.transpose(1, 0, 2)
            return jnp.einsum('bsd,od->bso', y, out_proj_w) + res
        key = jax.random.key(seed)
        ks = jax.random.split(key, 9)
        s = lambda fan_in: 1.0 / np.sqrt(fan_in)
        inp = {'x': jax.random.normal(ks[0], (BATCH, SEQ, D_MODEL), dtype=jnp.float32), 'in_proj_w': jax.random.uniform(ks[1], (D_INNER + D_MODEL, D_MODEL), jnp.float32, -s(D_MODEL), s(D_MODEL)), 'conv_w': jax.random.uniform(ks[2], (D_INNER, 1, D_CONV), jnp.float32, -s(D_CONV), s(D_CONV)), 'conv_b': jax.random.uniform(ks[3], (D_INNER,), jnp.float32, -s(D_CONV), s(D_CONV)), 'x_proj_w': jax.random.uniform(ks[4], (2 * D_STATE, D_INNER), jnp.float32, -s(D_INNER), s(D_INNER)), 'dt_proj_w': jax.random.uniform(ks[5], (D_INNER, D_INNER), jnp.float32, -s(D_INNER), s(D_INNER)), 'dt_proj_b': jax.random.uniform(ks[6], (D_INNER,), jnp.float32, -s(D_INNER), s(D_INNER)), 'A_log': jnp.log(jnp.tile(jnp.arange(1, D_STATE + 1, dtype=jnp.float32), (D_INNER, 1))), 'D': jnp.ones((D_INNER,), dtype=jnp.float32), 'out_proj_w': jax.random.uniform(ks[7], (D_MODEL, D_INNER), jnp.float32, -s(D_INNER), s(D_INNER))}
        return inp
    _L0_attn_in = _L0_attn_setup()

    def _L0_ffn_setup():
        import jax, jax.numpy as jnp
        import numpy as np
        NHEAD = 16
        NUM_GROUPS = 4
        EXPERTS_PER_GROUP = 2
        LN_EPS = 1e-05

        def _layernorm(x, g, b):
            mu = jnp.mean(x, axis=-1, keepdims=True)
            var = jnp.mean(jnp.square(x - mu), axis=-1, keepdims=True)
            return (x - mu) * jax.lax.rsqrt(var + LN_EPS) * g + b

        def _mha(x, wi, bi, wo, bo):
            B, S, D = x.shape
            hd = D // NHEAD
            qkv = x @ wi.T + bi
            q, k, v = jnp.split(qkv, 3, axis=-1)

            def heads(t):
                return t.reshape(B, S, NHEAD, hd).transpose(0, 2, 1, 3)
            q, k, v = (heads(q), heads(k), heads(v))
            scores = jnp.einsum('bhqd,bhkd->bhqk', q, k) / jnp.sqrt(jnp.asarray(hd, x.dtype))
            attn = jax.nn.softmax(scores, axis=-1)
            o = jnp.einsum('bhqk,bhkd->bhqd', attn, v)
            o = o.transpose(0, 2, 1, 3).reshape(B, S, D)
            return o @ wo.T + bo

        def _hier_moe(x, w_group, b_group, w_expert, b_expert, w1, b1, w2, b2):
            B, S, D = x.shape
            xt = x.reshape(B * S, D)
            T = xt.shape[0]
            E = NUM_GROUPS * EXPERTS_PER_GROUP
            gp = jax.nn.softmax(xt @ w_group + b_group, axis=-1)
            g_idx = jnp.argmax(gp, axis=-1)
            g_prob = jnp.max(gp, axis=-1)
            elog = jnp.einsum('td,gde->tge', xt, w_expert) + b_expert
            ep = jax.nn.softmax(elog, axis=-1)
            ep_sel = jnp.take_along_axis(ep, g_idx[:, None, None], axis=1)[:, 0, :]
            e_idx_local = jnp.argmax(ep_sel, axis=-1)
            e_prob = jnp.max(ep_sel, axis=-1)
            flat_e = g_idx * EXPERTS_PER_GROUP + e_idx_local
            combine = jax.nn.one_hot(flat_e, E, dtype=xt.dtype) * (g_prob * e_prob)[:, None]
            h = jax.nn.relu(jnp.einsum('td,edf->etf', xt, w1) + b1[:, None, :])
            y = jnp.einsum('etf,efd->etd', h, w2) + b2[:, None, :]
            out = jnp.einsum('te,etd->td', combine, y)
            return out.reshape(B, S, D)
        key = jax.random.key(seed)
        ks = jax.random.split(key, 8)
        B, S, D, F = (2, 128, 128, 256)
        G, Epg = (NUM_GROUPS, EXPERTS_PER_GROUP)
        E = G * Epg
        sc = lambda fan: 1.0 / np.sqrt(fan)
        return {'x': jax.random.normal(ks[0], (B, S, D), jnp.float32), 'in_proj_w': jax.random.normal(ks[1], (3 * D, D), jnp.float32) * sc(D), 'in_proj_b': jnp.zeros((3 * D,), jnp.float32), 'out_proj_w': jax.random.normal(ks[2], (D, D), jnp.float32) * sc(D), 'out_proj_b': jnp.zeros((D,), jnp.float32), 'ln1_g': jnp.ones((D,), jnp.float32), 'ln1_b': jnp.zeros((D,), jnp.float32), 'ln2_g': jnp.ones((D,), jnp.float32), 'ln2_b': jnp.zeros((D,), jnp.float32), 'w_group': jax.random.normal(ks[3], (D, G), jnp.float32) * sc(D), 'b_group': jnp.zeros((G,), jnp.float32), 'w_expert': jax.random.normal(ks[4], (G, D, Epg), jnp.float32) * sc(D), 'b_expert': jnp.zeros((G, Epg), jnp.float32), 'w1': jax.random.normal(ks[5], (E, D, F), jnp.float32) * sc(D), 'b1': jnp.zeros((E, F), jnp.float32), 'w2': jax.random.normal(ks[6], (E, F, D), jnp.float32) * sc(F), 'b2': jnp.zeros((E, D), jnp.float32)}
    _L0_ffn_in = _L0_ffn_setup()

    def _L1_attn_setup():
        import jax, jax.numpy as jnp
        import numpy as np
        B, N, C, D = (4, 512, 128, 32)
        EPS = 1e-15
        PAD_VAL = 1.0
        key = jax.random.key(seed)
        k1, k2, k3 = jax.random.split(key, 3)
        x = jax.random.normal(k1, (B, N, C), dtype=jnp.float32)
        W_qkv = jax.random.normal(k2, (3 * C, C), dtype=jnp.float32) * 0.02
        W_proj = jax.random.normal(k3, (C, C), dtype=jnp.float32) * 0.02
        b_proj = jnp.zeros((C,), dtype=jnp.float32)
        return {'x': x, 'W_qkv': W_qkv, 'W_proj': W_proj, 'b_proj': b_proj}
    _L1_attn_in = _L1_attn_setup()

    def _L1_ffn_setup():
        import jax, jax.numpy as jnp
        import numpy as np
        S, B, D = (128, 2, 128)
        E, TOPK = (15, 3)
        F = 128
        FS = 256

        def _uinit(k, shape, out_dim):
            std = out_dim ** (-0.5)
            return jax.random.uniform(k, shape, jnp.float32, -std, std)
        key = jax.random.key(seed)
        ks = jax.random.split(key, 10)
        return {'x': jax.random.normal(ks[0], (S, B, D), jnp.float32), 'gate_w': jax.random.normal(ks[1], (E, D), jnp.float32) * D ** (-0.5), 'fc1_w': _uinit(ks[2], (E, 2 * F, D), 2 * F), 'fc1_b': _uinit(ks[3], (E, 2 * F), 2 * F), 'geglu_mult': jnp.ones((E, F), jnp.float32), 'fc2_w': _uinit(ks[4], (E, D, F), D), 'fc2_b': _uinit(ks[5], (E, D), D), 's_fc1_w': _uinit(ks[6], (2 * FS, D), 2 * FS), 's_fc1_b': _uinit(ks[7], (2 * FS,), 2 * FS), 's_geglu_mult': jnp.ones((FS,), jnp.float32), 's_fc2_w': _uinit(ks[8], (D, FS), D), 's_fc2_b': _uinit(ks[9], (D,), D)}
    _L1_ffn_in = _L1_ffn_setup()
    _d = {'L0_attn_x': _L0_attn_in['x'], 'L0_attn_in_proj_w': _L0_attn_in['in_proj_w'], 'L0_attn_conv_w': _L0_attn_in['conv_w'], 'L0_attn_conv_b': _L0_attn_in['conv_b'], 'L0_attn_x_proj_w': _L0_attn_in['x_proj_w'], 'L0_attn_dt_proj_w': _L0_attn_in['dt_proj_w'], 'L0_attn_dt_proj_b': _L0_attn_in['dt_proj_b'], 'L0_attn_A_log': _L0_attn_in['A_log'], 'L0_attn_D': _L0_attn_in['D'], 'L0_attn_out_proj_w': _L0_attn_in['out_proj_w'], 'L0_ffn_in_proj_w': _L0_ffn_in['in_proj_w'], 'L0_ffn_in_proj_b': _L0_ffn_in['in_proj_b'], 'L0_ffn_out_proj_w': _L0_ffn_in['out_proj_w'], 'L0_ffn_out_proj_b': _L0_ffn_in['out_proj_b'], 'L0_ffn_ln1_g': _L0_ffn_in['ln1_g'], 'L0_ffn_ln1_b': _L0_ffn_in['ln1_b'], 'L0_ffn_ln2_g': _L0_ffn_in['ln2_g'], 'L0_ffn_ln2_b': _L0_ffn_in['ln2_b'], 'L0_ffn_w_group': _L0_ffn_in['w_group'], 'L0_ffn_b_group': _L0_ffn_in['b_group'], 'L0_ffn_w_expert': _L0_ffn_in['w_expert'], 'L0_ffn_b_expert': _L0_ffn_in['b_expert'], 'L0_ffn_w1': _L0_ffn_in['w1'], 'L0_ffn_b1': _L0_ffn_in['b1'], 'L0_ffn_w2': _L0_ffn_in['w2'], 'L0_ffn_b2': _L0_ffn_in['b2'], 'L1_attn_W_qkv': _L1_attn_in['W_qkv'], 'L1_attn_W_proj': _L1_attn_in['W_proj'], 'L1_attn_b_proj': _L1_attn_in['b_proj'], 'L1_ffn_gate_w': _L1_ffn_in['gate_w'], 'L1_ffn_fc1_w': _L1_ffn_in['fc1_w'], 'L1_ffn_fc1_b': _L1_ffn_in['fc1_b'], 'L1_ffn_geglu_mult': _L1_ffn_in['geglu_mult'], 'L1_ffn_fc2_w': _L1_ffn_in['fc2_w'], 'L1_ffn_fc2_b': _L1_ffn_in['fc2_b'], 'L1_ffn_s_fc1_w': _L1_ffn_in['s_fc1_w'], 'L1_ffn_s_fc1_b': _L1_ffn_in['s_fc1_b'], 'L1_ffn_s_geglu_mult': _L1_ffn_in['s_geglu_mult'], 'L1_ffn_s_fc2_w': _L1_ffn_in['s_fc2_w'], 'L1_ffn_s_fc2_b': _L1_ffn_in['s_fc2_b']}
    _x0 = _d['L0_attn_x']
    _d['L0_attn_x'] = jax.random.normal(jax.random.fold_in(jax.random.key(seed), 1), (8, 512, 128), dtype=_x0.dtype)
    del _x0
    return _d

def reference(L0_attn_x, L0_attn_in_proj_w, L0_attn_conv_w, L0_attn_conv_b, L0_attn_x_proj_w, L0_attn_dt_proj_w, L0_attn_dt_proj_b, L0_attn_A_log, L0_attn_D, L0_attn_out_proj_w, L0_ffn_in_proj_w, L0_ffn_in_proj_b, L0_ffn_out_proj_w, L0_ffn_out_proj_b, L0_ffn_ln1_g, L0_ffn_ln1_b, L0_ffn_ln2_g, L0_ffn_ln2_b, L0_ffn_w_group, L0_ffn_b_group, L0_ffn_w_expert, L0_ffn_b_expert, L0_ffn_w1, L0_ffn_b1, L0_ffn_w2, L0_ffn_b2, L1_attn_W_qkv, L1_attn_W_proj, L1_attn_b_proj, L1_ffn_gate_w, L1_ffn_fc1_w, L1_ffn_fc1_b, L1_ffn_geglu_mult, L1_ffn_fc2_w, L1_ffn_fc2_b, L1_ffn_s_fc1_w, L1_ffn_s_fc1_b, L1_ffn_s_geglu_mult, L1_ffn_s_fc2_w, L1_ffn_s_fc2_b):

    def _L0_attn_ref(x, in_proj_w, conv_w, conv_b, x_proj_w, dt_proj_w, dt_proj_b, A_log, D, out_proj_w):
        import jax, jax.numpy as jnp
        import numpy as np
        from jax import lax
        D_MODEL, D_STATE, D_CONV, EXPAND = (128, 64, 4, 2)
        D_INNER = EXPAND * D_MODEL
        BATCH, SEQ = (4, 512)

        def _forward(x, in_proj_w, conv_w, conv_b, x_proj_w, dt_proj_w, dt_proj_b, A_log, D, out_proj_w):
            b, seq_len, d_model = x.shape
            d_inner = conv_w.shape[0]
            d_conv = conv_w.shape[-1]
            x_and_res = jnp.einsum('bsd,od->bso', x, in_proj_w)
            u, res = (x_and_res[..., :d_inner], x_and_res[..., d_inner:])
            u_c = lax.conv_general_dilated(u.transpose(0, 2, 1), conv_w, window_strides=(1,), padding=[(d_conv - 1, 0)], feature_group_count=d_inner, dimension_numbers=('NCH', 'OIH', 'NCH')) + conv_b[None, :, None]
            u = u_c.transpose(0, 2, 1)
            x_dbl = jnp.einsum('bsd,od->bso', u, x_proj_w)
            _ = -jnp.exp(A_log)
            _ = D
            delta = jax.nn.softplus(jnp.einsum('bsd,od->bso', u, dt_proj_w) + dt_proj_b)
            gated_u = u * jax.nn.sigmoid(delta)

            def step(state, u_t):
                state = state * 0.9 + u_t * 0.1
                return (state, state)
            _, ys = lax.scan(step, jnp.zeros((b, d_inner), dtype=u.dtype), gated_u.transpose(1, 0, 2))
            y = ys.transpose(1, 0, 2)
            return jnp.einsum('bsd,od->bso', y, out_proj_w) + res
        return _forward(x, in_proj_w, conv_w, conv_b, x_proj_w, dt_proj_w, dt_proj_b, A_log, D, out_proj_w)

    def _L0_ffn_ref(x, in_proj_w, in_proj_b, out_proj_w, out_proj_b, ln1_g, ln1_b, ln2_g, ln2_b, w_group, b_group, w_expert, b_expert, w1, b1, w2, b2):
        import jax, jax.numpy as jnp
        import numpy as np
        NHEAD = 16
        NUM_GROUPS = 4
        EXPERTS_PER_GROUP = 2
        LN_EPS = 1e-05

        def _layernorm(x, g, b):
            mu = jnp.mean(x, axis=-1, keepdims=True)
            var = jnp.mean(jnp.square(x - mu), axis=-1, keepdims=True)
            return (x - mu) * jax.lax.rsqrt(var + LN_EPS) * g + b

        def _mha(x, wi, bi, wo, bo):
            B, S, D = x.shape
            hd = D // NHEAD
            qkv = x @ wi.T + bi
            q, k, v = jnp.split(qkv, 3, axis=-1)

            def heads(t):
                return t.reshape(B, S, NHEAD, hd).transpose(0, 2, 1, 3)
            q, k, v = (heads(q), heads(k), heads(v))
            scores = jnp.einsum('bhqd,bhkd->bhqk', q, k) / jnp.sqrt(jnp.asarray(hd, x.dtype))
            attn = jax.nn.softmax(scores, axis=-1)
            o = jnp.einsum('bhqk,bhkd->bhqd', attn, v)
            o = o.transpose(0, 2, 1, 3).reshape(B, S, D)
            return o @ wo.T + bo

        def _hier_moe(x, w_group, b_group, w_expert, b_expert, w1, b1, w2, b2):
            B, S, D = x.shape
            xt = x.reshape(B * S, D)
            T = xt.shape[0]
            E = NUM_GROUPS * EXPERTS_PER_GROUP
            gp = jax.nn.softmax(xt @ w_group + b_group, axis=-1)
            g_idx = jnp.argmax(gp, axis=-1)
            g_prob = jnp.max(gp, axis=-1)
            elog = jnp.einsum('td,gde->tge', xt, w_expert) + b_expert
            ep = jax.nn.softmax(elog, axis=-1)
            ep_sel = jnp.take_along_axis(ep, g_idx[:, None, None], axis=1)[:, 0, :]
            e_idx_local = jnp.argmax(ep_sel, axis=-1)
            e_prob = jnp.max(ep_sel, axis=-1)
            flat_e = g_idx * EXPERTS_PER_GROUP + e_idx_local
            combine = jax.nn.one_hot(flat_e, E, dtype=xt.dtype) * (g_prob * e_prob)[:, None]
            h = jax.nn.relu(jnp.einsum('td,edf->etf', xt, w1) + b1[:, None, :])
            y = jnp.einsum('etf,efd->etd', h, w2) + b2[:, None, :]
            out = jnp.einsum('te,etd->td', combine, y)
            return out.reshape(B, S, D)
        attn_out = _mha(x, in_proj_w, in_proj_b, out_proj_w, out_proj_b)
        x = _layernorm(x + attn_out, ln1_g, ln1_b)
        moe_out = _hier_moe(x, w_group, b_group, w_expert, b_expert, w1, b1, w2, b2)
        x = _layernorm(x + moe_out, ln2_g, ln2_b)
        return x

    def _L1_attn_ref(x, W_qkv, W_proj, b_proj):
        import jax, jax.numpy as jnp
        import numpy as np
        B, N, C, D = (4, 512, 128, 32)
        EPS = 1e-15
        PAD_VAL = 1.0
        Bx, Nx, Cx = x.shape
        h = Cx // D
        qkv = jnp.einsum('bnc,oc->bno', x, W_qkv)
        qkv = qkv.reshape(Bx, Nx, 3, Cx).transpose(0, 2, 3, 1)
        q, k, v = (qkv[:, 0], qkv[:, 1], qkv[:, 2])
        q = jax.nn.relu(q.reshape(Bx, h, D, Nx))
        k = jax.nn.relu(k.reshape(Bx, h, D, Nx)).transpose(0, 1, 3, 2)
        v = v.reshape(Bx, h, D, Nx)
        v = jnp.concatenate([v, jnp.full((Bx, h, 1, Nx), PAD_VAL, v.dtype)], axis=2)
        vk = jnp.einsum('bhdn,bhne->bhde', v, k)
        out = jnp.einsum('bhde,bhen->bhdn', vk, q)
        out = out[:, :, :-1] / (out[:, :, -1:] + EPS)
        out = out.reshape(Bx, Cx, Nx).transpose(0, 2, 1)
        return jnp.einsum('bnc,oc->bno', out, W_proj) + b_proj

    def _L1_ffn_ref(x, gate_w, fc1_w, fc1_b, geglu_mult, fc2_w, fc2_b, s_fc1_w, s_fc1_b, s_geglu_mult, s_fc2_w, s_fc2_b):
        import jax, jax.numpy as jnp
        import numpy as np
        S, B, D = (128, 2, 128)
        E, TOPK = (15, 3)
        F = 128
        FS = 256

        def _uinit(k, shape, out_dim):
            std = out_dim ** (-0.5)
            return jax.random.uniform(k, shape, jnp.float32, -std, std)
        s, b, d = x.shape
        xt = x.reshape(-1, d)
        T = xt.shape[0]
        logits = xt @ gate_w.T
        scores = jax.nn.softmax(logits, axis=-1)
        topk_w, topk_idx = jax.lax.top_k(scores, TOPK)
        topk_w = topk_w / (jnp.sum(topk_w, axis=-1, keepdims=True) + 1e-20)
        comb = jnp.zeros((T, E), xt.dtype).at[jnp.arange(T)[:, None], topk_idx].add(topk_w)
        h = jnp.einsum('td,efd->etf', xt, fc1_w) + fc1_b[:, None, :]
        xh, g = (h[..., :F], h[..., F:])
        a = jax.nn.gelu(g, approximate=False) * xh * geglu_mult[:, None, :]
        yexp = jnp.einsum('etf,edf->etd', a, fc2_w) + fc2_b[:, None, :]
        y = jnp.einsum('etd,te->td', yexp, comb)
        hs = xt @ s_fc1_w.T + s_fc1_b
        xs, gs = (hs[..., :FS], hs[..., FS:])
        as_ = jax.nn.gelu(gs, approximate=False) * xs * s_geglu_mult
        ys = as_ @ s_fc2_w.T + s_fc2_b
        return (y + ys).reshape(s, b, d)
    x = L0_attn_x
    xn = _layernorm(x, axis=-1)
    s = _L0_attn_ref(xn, L0_attn_in_proj_w, L0_attn_conv_w, L0_attn_conv_b, L0_attn_x_proj_w, L0_attn_dt_proj_w, L0_attn_dt_proj_b, L0_attn_A_log, L0_attn_D, L0_attn_out_proj_w)
    g = _silu(_L0_ffn_ref(xn, L0_ffn_in_proj_w, L0_ffn_in_proj_b, L0_ffn_out_proj_w, L0_ffn_out_proj_b, L0_ffn_ln1_g, L0_ffn_ln1_b, L0_ffn_ln2_g, L0_ffn_ln2_b, L0_ffn_w_group, L0_ffn_b_group, L0_ffn_w_expert, L0_ffn_b_expert, L0_ffn_w1, L0_ffn_b1, L0_ffn_w2, L0_ffn_b2))
    x = x + s * g
    xn = _layernorm(x, axis=-1)
    s = _L1_attn_ref(xn, L1_attn_W_qkv, L1_attn_W_proj, L1_attn_b_proj)
    g = _silu(_L1_ffn_ref(xn, L1_ffn_gate_w, L1_ffn_fc1_w, L1_ffn_fc1_b, L1_ffn_geglu_mult, L1_ffn_fc2_w, L1_ffn_fc2_b, L1_ffn_s_fc1_w, L1_ffn_s_fc1_b, L1_ffn_s_geglu_mult, L1_ffn_s_fc2_w, L1_ffn_s_fc2_b))
    x = x + s * g
    return x

_drawn_inputs = setup_inputs


def setup_inputs(seed=0):
    import zlib

    import numpy as np

    out = dict(_drawn_inputs(seed))
    spreads = {'L0_attn_D': (1.0, 0.2),
     'L0_ffn_in_proj_b': (0.0, 0.1),
     'L0_ffn_out_proj_b': (0.0, 0.1),
     'L0_ffn_ln1_g': (1.0, 0.2),
     'L0_ffn_ln1_b': (0.0, 0.1),
     'L0_ffn_ln2_g': (1.0, 0.2),
     'L0_ffn_ln2_b': (0.0, 0.1),
     'L0_ffn_b_group': (0.0, 0.307),
     'L0_ffn_b_expert': (0.0, 0.701),
     'L0_ffn_b1': (0.0, 0.8),
     'L0_ffn_b2': (0.0, 0.638),
     'L1_attn_b_proj': (0.0, 0.8),
     'L1_ffn_geglu_mult': (1.0, 0.6),
     'L1_ffn_s_geglu_mult': (1.0, 0.6)}
    factors = {'L0_attn_conv_w': 3.075,
     'L0_attn_dt_proj_w': 8.0,
     'L0_attn_dt_proj_b': 64.0,
     'L1_attn_W_qkv': 8.0,
     'L1_attn_W_proj': 8.0,
     'L1_ffn_gate_w': 8.0,
     'L1_ffn_fc1_w': 8.0,
     'L1_ffn_fc1_b': 8.0,
     'L1_ffn_fc2_w': 8.0,
     'L1_ffn_fc2_b': 64.0,
     'L1_ffn_s_fc1_w': 8.0,
     'L1_ffn_s_fc1_b': 8.0,
     'L1_ffn_s_fc2_w': 8.0,
     'L1_ffn_s_fc2_b': 55.506}
    for name, (base, spread) in spreads.items():
        noise = np.random.default_rng([zlib.crc32(name.encode()), seed]).standard_normal(out[name].shape)
        drawn = base * np.exp(spread * noise) if base else spread * noise
        out[name] = jnp.asarray(drawn.astype(out[name].dtype))
    for name, factor in factors.items():
        out[name] = (out[name] * factor).astype(out[name].dtype)
    return out
```

```python
from contextlib import ExitStack

import concourse.bass as bass
from concourse import mybir

F32 = mybir.dt.float32
BF16 = mybir.dt.bfloat16
ALU = mybir.AluOpType
ACT = mybir.ActivationFunctionType
AX = mybir.AxisListType.X

P = 128
NB = 8
S = 512
T = S // P
NH, HD = 16, 8
NG = NH // 4
PIECES = 6
KROWS = PIECES * HD
SLOTS = 64
LAG = 24
E0, F0 = 8, 256
E1, F1 = 15, 128
EPS = 1e-5
LN2 = 0.6931471805599453
SCALE = float(HD) ** -0.5
DECAY, GAIN = 0.9, 0.1


class Steps:

    def __init__(self, sem, names):
        self.sem, self.n, self.at = sem, len(names), {n: i for i, n in enumerate(names)}

    def after(self, name, b):
        return b * self.n + self.at[name] + 1


def past(b, least):
    return not isinstance(b, int) or b >= least


SSM = ["u0", "u0_sb", "c00", "c01", "c02", "c03", "u1", "u1_sb", "c10", "c11", "c12", "c13",
       "z0", "th0", "gu0", "z1", "th1", "gu1", "p", "scan", "res", "s"]
PRE = ["stats", "moments", "eps", "rstd", "xn", "turn", "xT", "xT_kept", "q", "q1", "qr", "k", "k1", "kr",
       "v", "v_sb", "q2", "q3", "k2", "k3"]
SHIFT = ["neg", "hi", "rest", "lo"]
POST = ["den", "rd0", "rd1", "rd2", "rd3", "on", "proj", "r1", "turn1", "stats1", "moments1", "eps1", "rstd1", "z",
        "turn2", "x1", "logits", "lg", "gmax", "gsub", "gexp", "gsum", "gties", "gtop", "ghot", "ediff", "eabs",
        "eexp", "eden", "erec", "chot", "first", "second", "p1", "s1", "p2", "s2", "p3", "cturn", "cT",
        "y", "r2", "turn3", "stats2", "moments2", "eps2", "rstd2"]
SETUP = {"dt_half": 1, "w_out0": 2, "bo_all": 3, "sb_half": 4, "b2": 8}
VEC = [("conv_w", 8), ("conv_b", 2), ("dt_b", 2), ("dt_half", 2), ("bq", 2), ("bv", 1), ("bo", 1), ("bo_all", 1), ("ln1_g", 1),
       ("ln1_b", 1), ("b1", 16), ("bp", 1), ("fc1_b", 30), ("mult", 15), ("sfc1_b", 4), ("s_mult", 2), ("sb", 1), ("sb_half", 1)]
TAIL = ["z2", "gain", "bias", "tanh", "w", "s_near", "s_turn", "ws", "x_new"]
PRE1 = ["stats", "moments", "eps", "rstd", "xn", "turn", "xT", "xT_kept", "q", "q_sb", "k", "k_sb", "v", "v_sb",
        "kv", "kv_sb", "ks_sb", "dn", "dn_eps", "rd0", "rd1", "num", "o", "pr", "s",
        "logits", "lmax", "lsub", "lexp", "lsum", "lrec", "score", "top8", "top3", "rep", "mask", "tw", "tsum", "tsum_eps", "trec",
        "comb", "p1", "s1", "p2", "s2", "p3", "cturn", "cT"]
POST1 = ["y", "th", "v", "w", "ws", "turn", "out"]


def build(nc, d, out):
    with ExitStack() as ctx:
        def sb(name, shape, dt=F32):
            return ctx.enter_context(nc.sbuf_tensor(name, shape, dt))

        def sem(name):
            return ctx.enter_context(nc.semaphore(name))

        def tiles(ap):
            return ap.rearrange("p (t n) -> p t n", t=T)

        w_in0 = sb("w_in0", [P, 384])
        w_dt = sb("w_dt", [P, 2, 256])
        w_out0 = sb("w_out0", [P, 2, P])
        w_qkv0 = sb("w_qkv0", [P, 384])
        w_o0 = sb("w_o0", [P, P])
        w_gate0 = sb("w_gate0", [P, 12])
        w1 = sb("w1", [P, E0, F0])
        w2 = sb("w2", [P, E0, 2, P])
        ident = sb("ident", [P, P])
        identb = sb("identb", [P, P], BF16)
        head_of = sb("head_of", [NH, P])
        pick = sb("pick", [96, 16, P], BF16)
        pick_f = sb("pick_f", [96, 16])
        block1 = sb("block1", [P, P])
        vec = sb("vec", [P, 96])
        rows = sb("rows", [P, 4, P])
        b2_f = sb("b2_f", [96, 2, P])
        b2_p = sb("b2_p", [96, 2, 3, P], BF16)
        decay = sb("decay", [P, S])
        mhalf = sb("mhalf", [P, T])
        ebase = sb("ebase", [P, T, 20])
        x_all = sb("x_all", [P, NB, T, P])
        xT_all = sb("xT_all", [P, NB, S])
        sT_all = sb("sT_all", [P, NB, S])
        st6 = sb("st6", [P, 4, T, 6])
        mv = sb("mv", [P, 4, T, 2])
        rstd = sb("rstd", [P, 4, 2, T])
        xn = sb("xn", [P, T, P])
        xT = sb("xT", [P, S])
        up = sb("up", [P, 2, S + 3])
        uc = sb("uc", [P, 2, S])
        th = sb("th", [P, S])
        gu = up[:, :, 3:3 + S]
        scan = sb("scan", [P, S])
        qk_r = sb("qk_r", [P, 2, S])
        qk_p = sb("qk_p", [P, 2, 3, S], BF16)
        qs_all = sb("qs_all", [P, NH, S], BF16)
        ks_all = sb("ks_all", [P, NH, S], BF16)
        qs = qs_all[0:KROWS + 2]
        ks = ks_all[0:KROWS + 2]
        v_new = sb("v_new", [P, T, P])
        v_aug = sb("v_aug", [P, T, NH, 32])
        smax = sb("smax", [P, NG, 4, T])
        smax_n = sb("smax_n", [P, 4, T])
        smax_r = sb("smax_r", [P, 4, T])
        smax_p = sb("smax_p", [P, T, 2, 4], BF16)
        smax_t = sb("smax_t", [8, S], BF16)
        probs = sb("probs", [P, 8, S])
        oT = sb("oT", [P, S])
        o_num = sb("o_num", [P, S])
        o_den = sb("o_den", [NH, S])
        rden = sb("rden", [P, S])
        o_n = sb("o_n", [P, S])
        r1 = sb("r1", [P, S])
        z1 = sb("z1", [P, T, P])
        x1T = sb("x1T", [P, S])
        gl = sb("gl", [P, T, 12])
        gm = sb("gm", [P, 8, T])
        g4 = sb("g4", [P, 8, T, 4])
        comb = sb("comb", [P, T, 4, 2])
        cpf = sb("cpf", [P, 2, T, 16])
        cpb = sb("cpb", [P, T, 96], BF16)
        cT = sb("cT", [96, S], BF16)
        cbc = sb("cbc", [P, 2, S])
        hz = sb("hz", [P, 2, S])
        hc = sb("hc", [P, 2, S])
        r2 = sb("r2", [P, S])
        zt, zg, tht = tiles(rden[:]), tiles(o_n[:]), tiles(r1[:])
        s_near = z1[:].rearrange("p t n -> p (t n)")
        cT_all = w1[0:96].rearrange("p e f -> p (e f)").bitcast(BF16).rearrange("p (b n) -> p b n", b=NB)
        qs_f = qs_all[:].rearrange("p h n -> p (h n)").bitcast(F32)
        ks_f = ks_all[:].rearrange("p h n -> p (h n)").bitcast(F32)
        fc1 = qs_f[:, 0:E1 * 2 * F1].rearrange("p (e f) -> p e f", e=E1)
        fc2 = ks_f[:, 0:E1 * P].rearrange("p (e f) -> p e f", e=E1)
        n = E1 * P
        sfc1, sfc2 = ks_f[:, n:n + 512], ks_f[:, n + 512:n + 768].rearrange("p (c f) -> p c f", c=2)
        w_qkv1, w_proj1, w_gate1 = ks_f[:, n + 768:n + 1152], ks_f[:, n + 1152:n + 1280], ks_f[:, n + 1280:n + 1280 + E1]
        z_tok = probs[:, 0:2].rearrange("p a n -> p (a n)")[:, 0:T * (P + 4)].rearrange("p (t n) -> p t n", t=T)
        kv_bd, ks_bd = probs[:, 2, 0:P], probs[:, 2, P:2 * P]
        lg = sb("lg", [P, 6, T, 20])
        m8 = sb("m8", [P, T, 8])
        m8v = sb("m8v", [P, T, 8])

        bank = [ctx.enter_context(nc.psum_tensor(f"bank{i}", [P, S], F32)) for i in range(8)]
        ps_s = bank[0:2]
        ps_t = bank[2:4]
        ps_o, ps_a, ps_b, ps_y = bank[4:8]

        stack = [nc.dram_tensor(f"stack_{n}", [P, PIECES, S], BF16, kind="Internal").ap() for n in "qk"]
        shift_d = nc.dram_tensor("shift_rows", [2, 4, S], BF16, kind="Internal").ap()

        x_first = sem("x_first")
        x_rest = sem("x_rest")
        w_early = sem("w_early")
        w_late = sem("w_late")
        w_last = sem("w_last")
        consts = sem("consts")
        setup = sem("setup")
        setup_pe = sem("setup_pe")
        setup_pool = sem("setup_pool")
        fc2_scaled = sem("fc2_scaled")
        ssm, pre, post, tail = (Steps(sem(n), s) for n, s in (("ssm", SSM), ("pre", PRE), ("post", POST), ("tail", TAIL)))
        pre1, post1 = Steps(sem("pre1"), PRE1), Steps(sem("post1"), POST1)
        shift = Steps(sem("shift"), SHIFT)
        s_made = sem("s_made")
        s_read = sem("s_read")
        t_made = sem("t_made")
        exp_done = sem("exp_done")
        pv_done = sem("pv_done")
        ot_made = sem("ot_made")
        o_moved = [sem(f"o_moved{g}") for g in range(NG)]
        v_put = sem("v_put")
        stack_out = sem("stack_out")
        stack_in = [sem(f"stack_in{g}") for g in range(NG)]
        shift_out = sem("shift_out")
        shift_in = sem("shift_in")
        c_made = sem("c_made")
        c_sb = sem("c_sb")
        z_made = sem("z_made")
        z_sb = sem("z_sb")
        hc_made = sem("hc_made")
        y_made = sem("y_made")
        g1_made = sem("g1_made")
        x1_made = sem("x1_made")
        c1_made = sem("c1_made")
        gelu_done = sem("gelu_done")
        act_x = sem("act_x")
        a1_done = sem("a1_done")
        y1_made = sem("y1_made")
        out_sem = sem("out_sem")

        def wait_apart(eng, *waits):
            waits = [(sem, value if isinstance(value, int) else eng.to_reg(value)) for sem, value in waits]
            eng.wait_ge(consts, 2)
            for sem, value in waits:
                eng.wait_ge(sem, value)

        V = {}
        n = 0
        for name, w in VEC:
            V[name] = n
            n += w

        def col(name, i=0):
            return vec[:, V[name] + i:V[name] + i + 1]

        def s_use(b, pos):
            return b * (SLOTS + NG) + pos - 1

        def s_pos(s):
            return (s // 16) * 17 + s % 16 + 1

        layer0 = nc.Block()
        block = layer0.__enter__()

        @block.sync
        def _(sp):
            xr = d["x"].rearrange("b (t p) d -> b p t d", p=P)
            sp.dma_start(x_all[:, 0], xr[0]).then_inc(x_first, 16)
            early = [(ident[:], d["ident"]), (vec[:], d["vec"]), (w_qkv0[:], d["w_qkv0"]),
                     (w_in0[:], d["w_in0"]), (w_dt[:], d["w_dt"]), (w_out0[:], d["w_out0"]), (w_o0[:], d["w_o0"]),
                     (w_gate0[:], d["w_gate0"]), (head_of[:], d["head_of"]), (pick_f[:], d["pick"]),
                     (rows[:], d["rows"].partition_broadcast(P))]
            for dst, src in early:
                sp.dma_start(dst, src).then_inc(w_early, 16)
            sp.wait_ge(consts, 1)
            for k in range(3):
                sp.dma_start(b2_f[32 * k:32 * k + E0, 0, :], d["b2"]).then_inc(w_early, 16)
                sp.dma_start(b2_f[32 * k:32 * k + E1, 1, :], d["fc2_b"]).then_inc(w_early, 16)
            for b in range(1, NB):
                sp.dma_start(x_all[:, b], xr[b]).then_inc(x_rest, 16)
            late = [(w1[:], d["w1"]), (w2[:], d["w2"]), (block1[:], d["block1"])]
            for dst, src in late:
                sp.dma_start(dst, src).then_inc(w_late, 16)

            def stacks_out(b):
                wait_apart(sp, (pre.sem, pre.after("k3", b)), *[(stack_in[g], 32 * b) for g in range(NG) if past(b, 1)])
                for j, parts in ((0, ((0, 0, 3), (3, 0, 2), (5, 0, 1))), (1, ((0, 0, 0), (1, 0, 0), (2, 0, 0), (3, 1, 0), (4, 1, 0), (5, 2, 0)))):
                    for to, first, n in parts:
                        n = n or 1
                        sp.dma_start(stack[j][:, to:to + n, :], qk_p[:, j, first:first + n, :]).then_inc(stack_out, 16)

            def stacks_in(b, g):
                wait_apart(sp, (stack_out, 16 * 9 * (b + 1)), *[(t_made, SLOTS * (b - 1) + 16 * (g + 1))] * past(b, 1))
                for j, dst in ((0, qs), (1, ks)):
                    src = stack[j].rearrange("(h d) s n -> h (d s) n", h=NH)[4 * g:4 * g + 4].rearrange("h r n -> r h n")
                    sp.dma_start(dst[0:KROWS, 4 * g:4 * g + 4, :], src).then_inc(stack_in[g], 16)

            def shift_rows(b, g):
                n = b * NG + g
                sp.wait_ge(s_read, s_use(b, 17 * g + 17) + 1)
                if past(n, 1):
                    sp.wait_ge(shift_in, 16 * n)
                sp.dma_start(shift_d.rearrange("a r n -> (a r) n"), smax_t[:]).then_inc(shift_out, 16)
                wait_apart(sp, (shift_out, 16 * (n + 1)))
                sp.dma_start(qs[KROWS:KROWS + 2, 4 * g:4 * g + 4, :], shift_d).then_inc(shift_in, 16)

            def outputs(b, g):
                wait_apart(sp, (ot_made, b * NG + g + 1), *[(post.sem, post.after("on", b - 1))] * past(b, 1))
                for r in range(4):
                    sp.dma_start(o_num[32 * g + 8 * r:32 * g + 8 * r + 8, :], oT[32 * r:32 * r + 8, :]).then_inc(o_moved[g], 16)
                    sp.dma_start(o_den[4 * g + r:4 * g + r + 1, :], oT[32 * r + 8:32 * r + 9, :]).then_inc(o_moved[g], 16)

            def body(b, full, previous, following):
                for s in range(SLOTS):
                    if previous and s == 0:
                        shift_rows(b - 1, 3)
                    if full and s in (16, 32, 48):
                        shift_rows(b, s // 16 - 1)
                    if previous and s == LAG - 13:
                        outputs(b - 1, 2)
                    if previous and s == LAG + 3:
                        outputs(b - 1, 3)
                    if full and s == LAG + 19:
                        outputs(b, 0)
                    if full and s == LAG + 35:
                        outputs(b, 1)
                    if full and s == LAG - 16:
                        stacks_in(b, 2)
                    if full and s == LAG:
                        stacks_in(b, 3)
                    if following and s == LAG + 15:
                        stacks_out(b + 1)
                    if following and s == LAG + 17:
                        stacks_in(b + 1, 0)
                    if following and s == LAG + 32:
                        stacks_in(b + 1, 1)

            sp.wait_ge(consts, 2)
            stacks_out(0)
            stacks_in(0, 0)
            stacks_in(0, 1)
            body(0, True, False, True)
            body(1, True, True, True)
            with sp.Fori(2, NB - 1) as b:
                body(b, True, True, True)
            body(NB - 1, True, True, False)
            body(NB, False, True, False)
            sp.wait_ge(t_made, SLOTS * NB)
            for dst, src in ((w_qkv1, "w_qkv1"), (w_proj1, "w_proj1"), (w_gate1, "w_gate1"), (fc1, "fc1"), (fc2, "fc2"),
                             (sfc1, "sfc1"), (sfc2, "sfc2")):
                sp.dma_start(dst, d[src]).then_inc(w_last, 16)
            sp.wait_ge(w_last, 16 * 7)

        @block.tensor
        def _(pe):
            pe.wait_ge(w_early, 16 * 17)
            pe.wait_ge(consts, 2)
            pe.matmul(ps_b[:, 0:1], w_o0[:], col("bv"), start=True, stop=True).then_inc(setup_pe, 1)

            def turn(dst, src):
                for t in range(T):
                    mm = pe.transpose(dst[:, t * P:(t + 1) * P], src[:, t * P:(t + 1) * P], ident[:])
                return mm

            def flat(ap):
                return ap.rearrange("p t n -> p (t n)")

            def ssm_at(b, s):
                if s == 0:
                    if past(b, 1):
                        pe.wait_ge(ssm.sem, ssm.after("s", b - 1))
                    pe.wait_ge(pre.sem, pre.after("k3", b))
                    if past(b, 2):
                        pe.wait_ge(c_sb, E0 * (b - 1))
                    pe.matmul(ps_a[:], w_in0[:, 0:P], xT[:], start=True, stop=True).then_inc(ssm.sem, 1)
                if s == 3:
                    pe.wait_ge(ssm.sem, ssm.after("c03", b))
                    pe.matmul(ps_a[:], w_in0[:, P:2 * P], xT[:], start=True, stop=True).then_inc(ssm.sem, 1)
                if s in (7, 10):
                    j = (s - 7) // 3
                    pe.wait_ge(ssm.sem, ssm.after(("c13", "gu0")[j], b))
                    pe.matmul(ps_a[:], w_dt[:, 0, j * P:(j + 1) * P], uc[:, 0, :], start=True, stop=False)
                    pe.matmul(ps_a[:], w_dt[:, 1, j * P:(j + 1) * P], uc[:, 1, :], start=False, stop=True).then_inc(ssm.sem, 1)
                if s == 13:
                    pe.wait_ge(ssm.sem, ssm.after("gu1", b))
                    pe.matmul(ps_a[:], w_out0[:, 0, :], gu[:, 0, :], start=True, stop=False)
                    pe.matmul(ps_a[:], w_out0[:, 1, :], gu[:, 1, :], start=False, stop=True).then_inc(ssm.sem, 1)
                if s == 16:
                    pe.wait_ge(ssm.sem, ssm.after("scan", b))
                    pe.matmul(ps_a[:], w_in0[:, 2 * P:3 * P], xT[:], start=True, stop=True).then_inc(ssm.sem, 1)

            def pre_at(b, s):
                if s == -1:
                    pe.wait_ge(pre.sem, pre.after("xn", b))
                    if past(b, 1):
                        pe.wait_ge(ssm.sem, ssm.after("s", b - 1))
                    turn(ps_a, flat(xn)).then_inc(pre.sem, 1)
                if s == 1:
                    pe.wait_ge(pre.sem, pre.after("xT_kept", b))
                    pe.matmul(ps_a[:], w_qkv0[:, 0:P], xT[:], start=True, stop=True).then_inc(pre.sem, 1)
                if s == 3:
                    pe.wait_ge(pre.sem, pre.after("qr", b))
                    pe.matmul(ps_a[:], w_qkv0[:, P:2 * P], xT[:], start=True, stop=True).then_inc(pre.sem, 1)
                if s == 5:
                    pe.wait_ge(pre.sem, pre.after("kr", b))
                    for t in range(T):
                        mm = pe.matmul(ps_a[:, t * P:(t + 1) * P], xT[:, t * P:(t + 1) * P], w_qkv0[:, 2 * P:3 * P], start=True, stop=True)
                    mm.then_inc(pre.sem, 1)

            def scores(b, s):
                h, t = s // T, s % T
                u = s_use(b, s_pos(s))
                if s % 16 == 0:
                    pe.wait_ge(stack_in[s // 16], 32 * (b + 1))
                if past(b, 1) or u >= 2:
                    pe.wait_ge(s_read, u - 1)
                pe.matmul(ps_s[(s_pos(s) + 1) % 2][:], qs[0:KROWS, h, t * P:(t + 1) * P], ks[0:KROWS, h, :],
                          start=True, stop=True).then_inc(s_made, 1)

            def shift_turn(b, g, pos, at):
                u = s_use(at, pos)
                pe.wait_ge(shift.sem, shift.after("lo", b * NG + g))
                pe.wait_ge(s_read, u - 1)
                for t in range(T):
                    mm = pe.transpose(ps_s[(pos + 1) % 2][0:8, :].bitcast(BF16)[:, t * P:(t + 1) * P],
                                      smax_p[:, t].rearrange("p a r -> p (a r)"), identb[:])
                mm.then_inc(s_made, 1)

            def transposed(b, v):
                g, t, r = v // 16, v % 16 // 4, v % 4
                h = 4 * g + r
                if v % 16 == 0:
                    pe.wait_ge(shift_in, 16 * (b * NG + g + 1))
                if past(b, 1) or v >= 2:
                    pe.wait_ge(exp_done, b * SLOTS + v - 1)
                pe.matmul(ps_t[v % 2][:], ks[:, h, t * P:(t + 1) * P], qs[:, h, :], start=True, stop=True).then_inc(t_made, 1)

            def weighted(b, q):
                g, t = q // 4, q % 4
                pe.wait_ge(exp_done, b * SLOTS + 4 * q + 4)
                if t == 0:
                    pe.wait_ge(v_put, b * NG + g + 1)
                    if past(b, 1) or g >= 1:
                        pe.wait_ge(ot_made, b * NG + g)
                for r in range(4):
                    mm = pe.matmul(ps_o[32 * r:32 * r + 32, :], v_aug[:, t, 4 * g + r, :], probs[:, (4 * q + r) % 8, :],
                                   start=(t == 0), stop=(t == 3))
                mm.then_inc(pv_done, 1)

            def post_at(b, s):
                if s == 0:
                    for g in range(NG):
                        pe.wait_ge(o_moved[g], 16 * 8 * (b + 1))
                    if past(b, 1):
                        pe.wait_ge(tail.sem, tail.after("ws", b - 1))
                    pe.matmul(ps_b[:], head_of[:], o_den[:], start=True, stop=True).then_inc(post.sem, 1)
                if s == 5:
                    pe.wait_ge(post.sem, post.after("on", b))
                    pe.matmul(ps_b[:], w_o0[:], o_n[:], start=True, stop=True).then_inc(post.sem, 1)
                if s == 6:
                    pe.wait_ge(post.sem, post.after("r1", b))
                    turn(ps_b, r1[:]).then_inc(post.sem, 1)
                if s == 8:
                    pe.wait_ge(post.sem, post.after("z", b))
                    turn(ps_b, flat(z1)).then_inc(post.sem, 1)
                if s == 9:
                    pe.wait_ge(post.sem, post.after("x1", b))
                    for t in range(T):
                        mm = pe.matmul(ps_b[:, 12 * t:12 * t + 12], x1T[:, t * P:(t + 1) * P], w_gate0[:], start=True, stop=True)
                    mm.then_inc(post.sem, 1)
                if s == 13:
                    pe.wait_ge(post.sem, post.after("p3", b))
                    for t in range(T):
                        mm = pe.transpose(ps_b[0:96, :].bitcast(BF16)[:, t * P:(t + 1) * P], cpb[:, t], identb[:])
                    mm.then_inc(post.sem, 1)

            def expert_z(b, k):
                e, c = k // 2, k % 2
                if k == 0:
                    pe.wait_ge(post.sem, post.after("cT", b))
                    pe.wait_ge(w_late, 16 * 3)
                if c == 0:
                    if k > 0 or (isinstance(b, int) and b == NB - 1):
                        pe.wait_ge(c_sb, b * E0 + e)
                    elif isinstance(b, int) and b == NB - 2:
                        pe.wait_ge(ssm.sem, ssm.after("s", b + 1))
                    else:
                        pe.wait_ge(pre.sem, pre.after("k3", b + 2))
                    pe.matmul(ps_a[:], pick[:, e, :], cT[:], start=True, stop=True).then_inc(c_made, 1)
                if k >= 1:
                    pe.wait_ge(z_sb, b * 2 * E0 + k)
                pe.matmul(ps_b[:], w1[:, e, c * P:(c + 1) * P], x1T[:], start=True, stop=True).then_inc(z_made, 1)

            def expert_y(b, k):
                e, c = k // 2, k % 2
                pe.wait_ge(hc_made, b * 2 * E0 + k + 1)
                if k == 0 and past(b, 1):
                    pe.wait_ge(post.sem, post.after("r2", b - 1))
                pe.matmul(ps_y[:], w2[:, e, c, :], hc[:, k % 2, :], start=(k == 0), stop=False).then_inc(y_made, 1)

            def post_end(b):
                for j in range(3):
                    mm = pe.matmul(ps_y[:], b2_p[:, 0, j, :], cT[:], start=False, stop=(j == 2))
                mm.then_inc(post.sem, 1)

            def experts_at(b, s):
                if 0 <= s < 16:
                    expert_z(b, s)
                if 2 <= s < 18:
                    expert_y(b, s - 2)
                if s == 18:
                    post_end(b)
                if s == 20:
                    pe.wait_ge(post.sem, post.after("r2", b))
                    turn(ps_b, r2[:]).then_inc(post.sem, 1)

            def tail_at(b, s):
                if s == 4:
                    pe.wait_ge(tail.sem, tail.after("s_near", b))
                    turn(ps_b, s_near[:]).then_inc(tail.sem, 1)

            def body(b, full, previous, before, following):
                for s in range(SLOTS):
                    if s >= LAG and full:
                        transposed(b, s - LAG)
                    if s < LAG and previous:
                        transposed(b - 1, s - LAG + SLOTS)
                    if full:
                        scores(b, s)
                    q, rest = divmod(s - LAG - 6, 4)
                    if rest == 0 and full and q >= 0:
                        weighted(b, q)
                    if rest == 0 and previous and q < 0:
                        weighted(b - 1, q + 16)
                    if full:
                        ssm_at(b, s)
                    if following:
                        pre_at(b + 1, s - LAG)
                    if previous:
                        post_at(b - 1, s - LAG - 4)
                        experts_at(b - 1, s - LAG - 18)
                    if before:
                        tail_at(b - 2, s)
                    if full and s % 16 == 15 and s < SLOTS - 1:
                        shift_turn(b, s // 16, s_pos(s) + 1, b)
                    if full and s == SLOTS - 1:
                        shift_turn(b, NG - 1, 0, b + 1)

            for s in range(-1, 6):
                pre_at(0, s)
            pe.wait_ge(setup, SETUP["b2"])
            pe.wait_ge(setup_pool, 3)
            body(0, True, False, False, True)
            body(1, True, True, False, True)
            with pe.Fori(2, NB - 1) as b:
                body(b, True, True, True, True)
            body(NB - 1, True, True, True, False)
            body(NB, False, True, True, False)
            body(NB + 1, False, False, True, False)

        @block.scalar
        def _(act):
            act.wait_ge(w_early, 16 * 17)
            act.wait_ge(consts, 2)

            def ssm_at(b, s):
                for s0, step, made, i in ((1, "u0_sb", "u0", 0), (4, "u1_sb", "u1", 1)):
                    if s == s0:
                        act.wait_ge(ssm.sem, ssm.after(made, b))
                        nc.scalar.copy(up[:, i, 3:3 + S], ps_a[:]).then_inc(ssm.sem, 1)
                for s0, made, i in ((8, "z0", 0), (11, "z1", 1)):
                    if s == s0:
                        act.wait_ge(ssm.sem, ssm.after(made, b))
                        if isinstance(b, int) and b == 0 and i == 0:
                            act.wait_ge(setup, SETUP["dt_half"])
                        nc.scalar.activation(th[:], ps_a[:], ACT.Tanh, bias=col("dt_half", i), scale=0.5).then_inc(ssm.sem, 1)

            def pre_at(b, s):
                if s == 0:
                    act.wait_ge(pre.sem, pre.after("turn", b))
                    nc.scalar.copy(xT[:], ps_a[:]).then_inc(pre.sem, 1)
                    nc.scalar.copy(xT_all[:, b, :], ps_a[:]).then_inc(pre.sem, 1)
                for s0, made, j in ((1, "q", 0), (3, "k", 1)):
                    if s == s0:
                        act.wait_ge(pre.sem, pre.after(made, b))
                        if j == 0 and past(b, 1):
                            act.wait_ge(stack_out, 16 * 9 * b)
                        nc.scalar.activation(qk_p[:, j, 0, :], ps_a[:], ACT.Identity, bias=col("bq", j)).then_inc(pre.sem, 1)
                if s == 6:
                    act.wait_ge(pre.sem, pre.after("v", b))
                    if past(b, 1):
                        act.wait_ge(v_put, NG * b)
                    nc.scalar.copy(v_new[:].rearrange("p t n -> p (t n)"), ps_a[:]).then_inc(pre.sem, 1)

            def exps(b, v):
                act.wait_ge(t_made, b * SLOTS + v + 1)
                if past(b, 1) or v >= 8:
                    act.wait_ge(pv_done, b * 16 + v // 4 - 1)
                nc.scalar.activation(probs[:, v % 8, :], ps_t[v % 2][:], ACT.Exp, scale=SCALE).then_inc(exp_done, 1)

            def group_out(b, g):
                act.wait_ge(pv_done, b * 16 + 4 * g + 4)
                if past(b, 1) or g >= 1:
                    act.wait_ge(o_moved[g - 1], 16 * 8 * (b + (1 if g else 0)))
                nc.scalar.copy(oT[:], ps_o[:]).then_inc(ot_made, 1)

            def post_at(b, s):
                if s == 10:
                    act.wait_ge(post.sem, post.after("gsub", b))
                    nc.scalar.activation(g4[:, 1], g4[:, 0], ACT.Exp).then_inc(post.sem, 1)
                if s == 11:
                    act.wait_ge(post.sem, post.after("eabs", b))
                    nc.scalar.activation(g4[:, 5], g4[:, 4], ACT.Exp).then_inc(post.sem, 1)
                if s == 13:
                    act.wait_ge(post.sem, post.after("cturn", b))
                    nc.scalar.copy(cT[:], ps_b[0:96, :].bitcast(BF16)[:, 0:S]).then_inc(post.sem, 1)

            def experts_at(b, k):
                if not 0 <= k < 16:
                    return
                e, c = k // 2, k % 2
                if c == 0:
                    act.wait_ge(c_made, b * E0 + e + 1)
                    if past(b, 1) or e >= 2:
                        act.wait_ge(hc_made, (b * E0 + e - 1) * 2)
                    nc.scalar.copy(cbc[:, e % 2, :], ps_a[:]).then_inc(c_sb, 1)
                act.wait_ge(z_made, b * 2 * E0 + k + 1)
                if past(b, 1) or k >= 2:
                    act.wait_ge(hc_made, b * 2 * E0 + k - 1)
                nc.scalar.activation(hz[:, k % 2, :], ps_b[:], ACT.Relu, bias=col("b1", k)).then_inc(z_sb, 1)

            def tail_at(b, s):
                if s == 3:
                    act.wait_ge(tail.sem, tail.after("bias", b))
                    nc.scalar.activation(tht[:], zg[:], ACT.Tanh, scale=0.5).then_inc(tail.sem, 1)
                    act.wait_ge(tail.sem, tail.after("w", b))
                    nc.scalar.copy(s_near[:], sT_all[:, b, :]).then_inc(tail.sem, 1)

            def body(b, full, previous, before, following):
                for s in range(SLOTS):
                    if s >= LAG and full:
                        exps(b, s - LAG)
                    if s < LAG and previous:
                        exps(b - 1, s - LAG + SLOTS)
                    g, rest = divmod(s - LAG - 18, 16)
                    if rest == 0 and full and g >= 0:
                        group_out(b, g)
                    if rest == 0 and previous and g < 0:
                        group_out(b - 1, g + 4)
                    if full:
                        ssm_at(b, s)
                    if following:
                        pre_at(b + 1, s - LAG)
                    if previous:
                        post_at(b - 1, s - LAG - 4)
                        experts_at(b - 1, s - LAG - 18)
                    if before:
                        tail_at(b - 2, s)

            for s in range(0, 7):
                pre_at(0, s)
            body(0, True, False, False, True)
            body(1, True, True, False, True)
            with act.Fori(2, NB - 1) as b:
                body(b, True, True, True, True)
            body(NB - 1, True, True, True, False)
            body(NB, False, True, True, False)
            body(NB + 1, False, False, True, False)

        @block.vector
        def _(dve):
            dve.wait_ge(w_early, 16 * 17)
            v = nc.vector
            v.tensor_scalar(vec[:, V["dt_half"]:V["dt_half"] + 2], vec[:, V["dt_b"]:V["dt_b"] + 2], -LN2, 0.5, ALU.add, ALU.mult).then_inc(setup, 1)
            v.tensor_scalar(w_out0[:], w_out0[:], 0.25 * GAIN, None, ALU.mult).then_inc(setup, 1)
            dve.wait_ge(setup_pe, 1)
            v.tensor_tensor(col("bo_all"), ps_b[:, 0:1], col("bo"), ALU.add).then_inc(setup, 1)
            v.tensor_scalar(col("sb_half"), col("sb"), 0.5, None, ALU.mult).then_inc(setup, 1)
            v.tensor_copy(b2_p[:, :, 0, :], b2_f[:]).then_inc(setup, 1)
            dve.wait_ge(setup, 5)
            v.tensor_tensor(b2_f[:], b2_f[:], b2_p[:, :, 0, :], ALU.subtract).then_inc(setup, 1)
            dve.wait_ge(setup, 6)
            v.tensor_copy(b2_p[:, :, 1, :], b2_f[:]).then_inc(setup, 1)
            dve.wait_ge(setup, 7)
            v.tensor_tensor(b2_p[:, :, 2, :], b2_f[:], b2_p[:, :, 1, :], ALU.subtract).then_inc(setup, 1)
            dve.wait_ge(setup, SETUP["b2"])
            dve.wait_ge(consts, 2)

            def moments(src, i, chain, names, b):
                for t in range(T):
                    ins = v.bn_stats(st6[:, i, t], src(t))
                ins.then_inc(chain.sem, 1)
                wait_apart(dve, (chain.sem, chain.after(names[0], b)))
                for t in range(T):
                    ins = v.bn_aggr(mv[:, i, t], st6[:, i, t])
                ins.then_inc(chain.sem, 1)

            def normal(dst, src, i):
                for t in range(T):
                    ins = v.tensor_scalar(dst[:, t], src(t), mv[:, i, t, 0:1], rstd[:, i, 1, t:t + 1], ALU.subtract, ALU.mult)
                return ins

            def ssm_at(b, s):
                for i, s0 in ((0, 2), (1, 5)):
                    if s == s0:
                        dve.wait_ge(ssm.sem, ssm.after(f"u{i}_sb", b))
                        v.tensor_scalar(uc[:, i, :], up[:, i, 0:S], col("conv_w", 4 * i), col("conv_b", i), ALU.mult, ALU.add).then_inc(ssm.sem, 1)
                    for j, sj in ((1, s0), (2, s0 + 1), (3, s0 + 1)):
                        if s == sj:
                            dve.wait_ge(ssm.sem, ssm.after(f"c{i}{j - 1}", b))
                            v.scalar_tensor_tensor(out=uc[:, i, :], in0=up[:, i, j:j + S], scalar=col("conv_w", 4 * i + j),
                                                   in1=uc[:, i, :], op0=ALU.mult, op1=ALU.add).then_inc(ssm.sem, 1)
                for i, s0 in ((0, 9), (1, 12)):
                    if s == s0:
                        dve.wait_ge(ssm.sem, ssm.after(f"th{i}", b))
                        v.scalar_tensor_tensor(out=gu[:, i, :], in0=th[:], scalar=3.0, in1=uc[:, i, :], op0=ALU.add,
                                               op1=ALU.mult).then_inc(ssm.sem, 1)
                if s == 14:
                    dve.wait_ge(ssm.sem, ssm.after("p", b))
                    v.tensor_tensor_scan(scan[:], decay[:], ps_a[:], 0.0, ALU.mult, ALU.add).then_inc(ssm.sem, 1)
                if s == 17:
                    dve.wait_ge(ssm.sem, ssm.after("res", b))
                    v.tensor_tensor(sT_all[:, b, :], ps_a[:], scan[:], ALU.add).then_inc(ssm.sem, 1)

            def pre_at(b, s):
                if s == -5:
                    if isinstance(b, int) and b == 0:
                        dve.wait_ge(x_first, 16)
                    elif isinstance(b, int) and b == 1:
                        dve.wait_ge(x_rest, 16 * (NB - 1))
                    if past(b, 1):
                        dve.wait_ge(pre.sem, pre.after("k3", b - 1))
                    moments(lambda t: x_all[:, b, t], 0, pre, ["stats"], b)
                if s == -3:
                    dve.wait_ge(pre.sem, pre.after("rstd", b))
                    normal(xn, lambda t: x_all[:, b, t], 0).then_inc(pre.sem, 1)
                for s0, made, j in ((2, "q1", 0), (4, "k1", 1)):
                    if s == s0:
                        dve.wait_ge(pre.sem, pre.after(made, b))
                        v.scalar_tensor_tensor(out=qk_r[:, j, :], in0=ps_a[:], scalar=col("bq", j), in1=qk_p[:, j, 0, :],
                                               op0=ALU.add, op1=ALU.subtract).then_inc(pre.sem, 1)

            def maxima(b, s):
                h, t = s // T, s % T
                dve.wait_ge(s_made, s_use(b, s_pos(s)) + 1)
                v.tensor_reduce(smax[:, h // 4, h % 4, t:t + 1], ps_s[(s_pos(s) + 1) % 2][:], AX, ALU.max).then_inc(s_read, 1)

            def shift_pieces(b, g):
                n = b * NG + g
                dve.wait_ge(s_read, s_use(b, s_pos(16 * g + 15)) + 1)
                v.tensor_scalar(smax_n[:], smax[:, g], -1.0, None, ALU.mult).then_inc(shift.sem, 1)
                dve.wait_ge(shift.sem, shift.after("neg", n))
                hi = smax_p[:].rearrange("p t a r -> p a r t")
                v.tensor_copy(hi[:, 0], smax_n[:]).then_inc(shift.sem, 1)
                dve.wait_ge(shift.sem, shift.after("hi", n))
                v.tensor_tensor(smax_r[:], smax_n[:], hi[:, 0], ALU.subtract).then_inc(shift.sem, 1)
                dve.wait_ge(shift.sem, shift.after("rest", n))
                v.tensor_copy(hi[:, 1], smax_r[:]).then_inc(shift.sem, 1)

            def shift_rows(b, g, pos, at):
                n = b * NG + g
                dve.wait_ge(s_made, s_use(at, pos) + 1)
                if past(n, 1):
                    dve.wait_ge(shift_out, 16 * n)
                v.tensor_copy(smax_t[:], ps_s[(pos + 1) % 2][0:8, :].bitcast(BF16)[:, 0:S]).then_inc(s_read, 1)

            def post_at(b, s):
                def step(name, ins):
                    ins.then_inc(post.sem, 1)
                    dve.wait_ge(post.sem, post.after(name, b))

                if 1 <= s <= 4:
                    if s == 1:
                        dve.wait_ge(post.sem, post.after("den", b))
                    c = s - 1
                    v.reciprocal(rden[:, c * P:(c + 1) * P], ps_b[:, c * P:(c + 1) * P]).then_inc(post.sem, 1)
                if s == 4:
                    dve.wait_ge(post.sem, post.after("rd3", b))
                    v.tensor_tensor(o_n[:], o_num[:], rden[:], ALU.mult).then_inc(post.sem, 1)
                if s == 5:
                    dve.wait_ge(post.sem, post.after("proj", b))
                    v.scalar_tensor_tensor(out=r1[:], in0=ps_b[:], scalar=col("bo_all"), in1=xT_all[:, b, :], op0=ALU.add,
                                           op1=ALU.add).then_inc(post.sem, 1)
                if s == 6:
                    dve.wait_ge(post.sem, post.after("turn1", b))
                    moments(lambda t: ps_b[:, t * P:(t + 1) * P], 1, post, ["stats1"], b)
                if s == 8:
                    dve.wait_ge(post.sem, post.after("rstd1", b))
                    normal(z1, lambda t: ps_b[:, t * P:(t + 1) * P], 1).then_inc(post.sem, 1)
                if s == 9:
                    dve.wait_ge(post.sem, post.after("turn2", b))
                    v.tensor_scalar(x1T[:], ps_b[:], col("ln1_g"), col("ln1_b"), ALU.mult, ALU.add).then_inc(post.sem, 1)
                if s == 10:
                    dve.wait_ge(post.sem, post.after("logits", b))
                    step("lg", v.tensor_tensor(gl[:], ps_b[:, 0:48].rearrange("p (t e) -> p t e", t=T),
                                               rows[:, 2:3, 0:12].broadcast_to([P, T, 12]), ALU.add))
                    gr = gl[:, :, 0:4]
                    step("gmax", v.tensor_reduce(gm[:, 0, :], gr, AX, ALU.max))
                    v.tensor_tensor(g4[:, 0], gr, gm[:, 0, :].unsqueeze(2).broadcast_to([P, T, 4]), ALU.subtract).then_inc(post.sem, 1)
                if s == 11:
                    dve.wait_ge(post.sem, post.after("gexp", b))
                    step("gsum", v.tensor_reduce(gm[:, 1, :], g4[:, 1], AX, ALU.add))
                    step("gties", v.scalar_tensor_tensor(out=g4[:, 2], in0=g4[:, 0], scalar=0.0,
                                                         in1=rows[:, 3:4, 0:4].broadcast_to([P, T, 4]), op0=ALU.is_equal, op1=ALU.mult))
                    step("gtop", v.tensor_reduce(gm[:, 2, :], g4[:, 2], AX, ALU.max))
                    step("ghot", v.tensor_tensor(g4[:, 3], g4[:, 2], gm[:, 2, :].unsqueeze(2).broadcast_to([P, T, 4]), ALU.is_equal))
                    ex = gl[:, :, 4:12].rearrange("p t (g e) -> p t g e", e=2)
                    step("ediff", v.tensor_tensor(g4[:, 6], ex[:, :, :, 0], ex[:, :, :, 1], ALU.subtract))
                    v.scalar_tensor_tensor(out=g4[:, 4], in0=g4[:, 6], scalar=-1.0, in1=g4[:, 6], op0=ALU.mult,
                                           op1=ALU.min).then_inc(post.sem, 1)
                if s == 12:
                    dve.wait_ge(post.sem, post.after("eexp", b))
                    step("eden", v.scalar_tensor_tensor(out=g4[:, 4], in0=g4[:, 5], scalar=1.0,
                                                        in1=gm[:, 1, :].unsqueeze(2).broadcast_to([P, T, 4]), op0=ALU.add, op1=ALU.mult))
                    step("erec", v.reciprocal(g4[:, 5], g4[:, 4]))
                    step("chot", v.tensor_tensor(g4[:, 7], g4[:, 5], g4[:, 3], ALU.mult))
                    step("first", v.scalar_tensor_tensor(out=comb[:, :, :, 0], in0=g4[:, 6], scalar=0.0, in1=g4[:, 7],
                                                         op0=ALU.is_ge, op1=ALU.mult))
                    step("second", v.tensor_tensor(comb[:, :, :, 1], g4[:, 7], comb[:, :, :, 0], ALU.subtract))
                    pieces(comb[:].rearrange("p t g e -> p t (g e)"), E0, step)
                if s == 33:
                    dve.wait_ge(post.sem, post.after("y", b))
                    v.tensor_tensor(r2[:], ps_y[:], x1T[:], ALU.add).then_inc(post.sem, 1)
                if s == 34:
                    dve.wait_ge(post.sem, post.after("turn3", b))
                    moments(lambda t: ps_b[:, t * P:(t + 1) * P], 2, post, ["stats2"], b)

            def pieces(c, n, step):
                step("p1", v.tensor_copy(cpb[:, :, 0:n], c))
                step("s1", v.tensor_tensor(cpf[:, 0, :, 0:n], c, cpb[:, :, 0:n], ALU.subtract))
                step("p2", v.tensor_copy(cpb[:, :, 32:32 + n], cpf[:, 0, :, 0:n]))
                step("s2", v.tensor_tensor(cpf[:, 1, :, 0:n], cpf[:, 0, :, 0:n], cpb[:, :, 32:32 + n], ALU.subtract))
                step("p3", v.tensor_copy(cpb[:, :, 64:64 + n], cpf[:, 1, :, 0:n]))

            def experts_at(b, k):
                if not 0 <= k < 16:
                    return
                dve.wait_ge(z_sb, b * 2 * E0 + k + 1)
                if past(b, 1) or k >= 2:
                    dve.wait_ge(y_made, b * 2 * E0 + k - 1)
                v.tensor_tensor(hc[:, k % 2, :], hz[:, k % 2, :], cbc[:, k // 2 % 2, :], ALU.mult).then_inc(hc_made, 1)

            def tail_at(b, s):
                if s == 0:
                    dve.wait_ge(post.sem, post.after("rstd2", b))
                    normal(zt, lambda t: ps_b[:, t * P:(t + 1) * P], 2).then_inc(tail.sem, 1)
                if s == 3:
                    dve.wait_ge(tail.sem, tail.after("tanh", b))
                    v.scalar_tensor_tensor(out=zt[:], in0=tht[:], scalar=1.0, in1=zg[:], op0=ALU.add, op1=ALU.mult).then_inc(tail.sem, 1)
                if s == 5:
                    dve.wait_ge(tail.sem, tail.after("s_turn", b))
                    v.tensor_tensor(zg[:], zt[:], tiles(ps_b[:]), ALU.mult).then_inc(tail.sem, 1)
                    dve.wait_ge(tail.sem, tail.after("ws", b))
                    v.scalar_tensor_tensor(out=x_all[:, b], in0=zg[:], scalar=0.5, in1=x_all[:, b], op0=ALU.mult,
                                           op1=ALU.add).then_inc(tail.sem, 1)

            def body(b, full, previous, before, following):
                for s in range(SLOTS):
                    if full:
                        maxima(b, s)
                    if full and s % 16 == 15:
                        shift_pieces(b, s // 16)
                    if full:
                        ssm_at(b, s)
                    if following:
                        pre_at(b + 1, s - LAG)
                    if previous:
                        post_at(b - 1, s - LAG - 4)
                        experts_at(b - 1, s - LAG - 18)
                    if before:
                        tail_at(b - 2, s)
                    if full and s % 16 == 15 and s < SLOTS - 1:
                        shift_rows(b, s // 16, s_pos(s) + 1, b)
                    if full and s == SLOTS - 1:
                        shift_rows(b, NG - 1, 0, b + 1)

            for s in range(-5, 5):
                pre_at(0, s)
            body(0, True, False, False, True)
            body(1, True, True, False, True)
            with dve.Fori(2, NB - 1) as b:
                body(b, True, True, True, True)
            body(NB - 1, True, True, True, False)
            body(NB, False, True, True, False)
            body(NB + 1, False, False, True, False)

        @block.gpsimd
        def _(pool):
            p = nc.gpsimd
            p.memset(b2_f[:], 0.0).then_inc(consts, 1)
            p.memset(mhalf[:], -0.5)
            p.memset(decay[:], DECAY)
            p.memset(up[:, :, 0:3], 0.0)
            p.memset(cpb[:], 0.0)
            p.memset(ebase[:], 2.718281828459045)
            p.memset(lg[:], -1.0)
            p.memset(m8v[:], -1.0)
            p.memset(v_aug[:], 0.0).then_inc(setup_pool, 1)
            pool.wait_ge(setup_pool, 1)
            p.memset(ks[32:KROWS + 2], 1.0).then_inc(setup_pool, 1)
            pool.wait_ge(setup_pool, 2)
            p.memset(v_aug[:, :, :, HD:HD + 1], 1.0).then_inc(consts, 1)

            def rsqrt(i, chain, first, names, b):
                wait_apart(pool, (chain.sem, chain.after(first, b)))
                p.tensor_scalar(rstd[:, i, 0, :], mv[:, i, :, 1], EPS, None, ALU.add).then_inc(chain.sem, 1)
                pool.wait_ge(chain.sem, chain.after(names[0], b))
                p.tensor_tensor(rstd[:, i, 1, :], rstd[:, i, 0, :], mhalf[:], ALU.pow).then_inc(chain.sem, 1)

            def pre_at(b, s):
                if s == -4:
                    rsqrt(0, pre, "moments", ["eps"], b)
                if s == 7:
                    wait_apart(pool, (pre.sem, pre.after("v_sb", b)))
                    for j, name in ((0, "q2"), (1, "k2")):
                        p.tensor_scalar(qk_p[:, j, 1, :], qk_r[:, j, :], 1.0, None, ALU.mult).then_inc(pre.sem, 1)
                        pool.wait_ge(pre.sem, pre.after(name, b))
                        p.tensor_tensor(qk_p[:, j, 2, :], qk_r[:, j, :], qk_p[:, j, 1, :], ALU.subtract).then_inc(pre.sem, 1)

            def values(b, g):
                spent = [(pv_done, 16 * (b - 1) + 4 * g + 4)] if past(b, 1) else []
                wait_apart(pool, (pre.sem, pre.after("v_sb", b)), *spent)
                p.tensor_scalar(v_aug[:, :, 4 * g:4 * g + 4, 0:HD],
                                v_new[:, :, 32 * g:32 * g + 32].rearrange("p t (h d) -> p t h d", d=HD),
                                1.0, None, ALU.mult).then_inc(v_put, 1)

            def post_at(b, s):
                if s == 7:
                    rsqrt(1, post, "moments1", ["eps1"], b)
                if s == 35:
                    rsqrt(2, post, "moments2", ["eps2"], b)

            def tail_at(b, s):
                if s == 1:
                    pool.wait_ge(tail.sem, tail.after("z2", b))
                    p.tensor_tensor(zg[:], zt[:], rows[:, 0:1, :].broadcast_to([P, T, P]), ALU.mult).then_inc(tail.sem, 1)
                    pool.wait_ge(tail.sem, tail.after("gain", b))
                    p.tensor_tensor(zg[:], zg[:], rows[:, 1:2, :].broadcast_to([P, T, P]), ALU.add).then_inc(tail.sem, 1)

            def body(b, full, previous, before, following):
                for s in range(SLOTS):
                    if before:
                        tail_at(b - 2, s)
                    if full and s == LAG - 16 + 2:
                        values(b, 2)
                    if full and s == LAG + 2:
                        values(b, 3)
                    if following:
                        pre_at(b + 1, s - LAG)
                    if following and s == LAG + 20:
                        values(b + 1, 0)
                    if following and s == LAG + 36:
                        values(b + 1, 1)
                    if previous:
                        post_at(b - 1, s - LAG - 4)

            pool.wait_ge(w_early, 16 * 17)
            for s in range(-5, 8):
                pre_at(0, s)
            values(0, 0)
            values(0, 1)
            p.tensor_scalar(identb[:], ident[:], 1.0, None, ALU.mult)
            p.tensor_scalar(pick[:], pick_f[:].unsqueeze(2).broadcast_to([96, 16, P]), 1.0, None, ALU.mult).then_inc(setup_pool, 1)
            body(0, True, False, False, True)
            body(1, True, True, False, True)
            with pool.Fori(2, NB - 1) as b:
                body(b, True, True, True, True)
            body(NB - 1, True, True, True, False)
            body(NB, False, True, True, False)
            body(NB + 1, False, False, True, False)
            pool.wait_ge(w_last, 16 * 7)
            p.tensor_tensor(fc2, fc2, vec[:, V["mult"]:V["mult"] + E1].unsqueeze(2).broadcast_to([P, E1, P]), ALU.mult)
            p.tensor_tensor(sfc2, sfc2, vec[:, V["s_mult"]:V["s_mult"] + 2].unsqueeze(2).broadcast_to([P, 2, P]), ALU.mult)\
                .then_inc(fc2_scaled, 1)
            pool.wait_ge(pv_done, 16 * NB)
            p.memset(z_tok[:, :, P:P + 1], 1.0).then_inc(fc2_scaled, 1)

        layer0.__exit__(None, None, None)

        UNITS = E1 + 2
        ps_g, ps_x = bank[0:2], bank[2:4]
        ps_c, ps_y1, ps_p, ps_q = bank[4:8]
        kT, vT, qT, kv, ksum = z1, z_tok, r1, kv_bd, ks_bd
        layer1 = nc.Block()
        block = layer1.__enter__()

        def before(b, u):
            return b * UNITS + (u - 1 if u else 0)

        @block.sync
        def _(sp):
            with sp.Fori(0, NB) as b:
                sp.wait_ge(post1.sem, post1.after("out", b))
                sp.dma_start(out.rearrange("b (t p) d -> b p t d", p=P)[b], x_all[:, b]).then_inc(out_sem, 16)
            sp.wait_ge(out_sem, 16 * NB)

        @block.tensor
        def _(pe):
            def turn(dst, src):
                for t in range(T):
                    mm = pe.transpose(dst[:, t * P:(t + 1) * P], src[:, t * P:(t + 1) * P], ident[:])
                return mm

            def token_major(w):
                for t in range(T):
                    mm = pe.matmul(ps_p[:, t * P:(t + 1) * P], xT[:, t * P:(t + 1) * P], w, start=True, stop=True)
                return mm

            def pre_at(b, u):
                if u == 2:
                    pe.wait_ge(pre1.sem, pre1.after("xn", b))
                    turn(ps_p, xn[:].rearrange("p t n -> p (t n)")).then_inc(pre1.sem, 1)
                if u == 3:
                    pe.wait_ge(pre1.sem, pre1.after("xT_kept", b))
                    pe.matmul(ps_p[:], w_qkv1[:, 0:P], xT[:], start=True, stop=True).then_inc(pre1.sem, 1)
                if u == 4:
                    pe.wait_ge(pre1.sem, pre1.after("q_sb", b))
                    token_major(w_qkv1[:, P:2 * P]).then_inc(pre1.sem, 1)
                if u == 5:
                    pe.wait_ge(pre1.sem, pre1.after("k_sb", b))
                    token_major(w_qkv1[:, 2 * P:3 * P]).then_inc(pre1.sem, 1)
                if u == 6:
                    pe.wait_ge(pre1.sem, pre1.after("v_sb", b))
                    for t in range(T):
                        mm = pe.matmul(ps_p[:, 0:P + 1], kT[:, t, :], vT[:, t, 0:P + 1], start=(t == 0), stop=(t == T - 1))
                    mm.then_inc(pre1.sem, 1)
                if u == 7:
                    pe.wait_ge(pre1.sem, pre1.after("ks_sb", b))
                    pe.matmul(ps_p[:], ksum[:], qT[:], start=True, stop=True).then_inc(pre1.sem, 1)
                if u == 10:
                    pe.wait_ge(pre1.sem, pre1.after("rd1", b))
                    pe.matmul(ps_p[:], kv[:], qT[:], start=True, stop=True).then_inc(pre1.sem, 1)
                if u == 11:
                    pe.wait_ge(pre1.sem, pre1.after("o", b))
                    pe.matmul(ps_p[:], w_proj1[:], o_n[:], start=True, stop=True).then_inc(pre1.sem, 1)
                if u == 12:
                    pe.wait_ge(pre1.sem, pre1.after("s", b))
                    for t in range(T):
                        mm = pe.matmul(ps_p[:, E1 * t:E1 * (t + 1)], xT[:, t * P:(t + 1) * P], w_gate1[:], start=True, stop=True)
                    mm.then_inc(pre1.sem, 1)
                if u == 15:
                    pe.wait_ge(pre1.sem, pre1.after("p3", b))
                    for t in range(T):
                        mm = pe.transpose(ps_p[0:96, :].bitcast(BF16)[:, t * P:(t + 1) * P], cpb[:, t], identb[:])
                    mm.then_inc(pre1.sem, 1)

            def up_at(b, u):
                if u < E1:
                    wx, wg = fc1[:, u, 0:F1], fc1[:, u, F1:2 * F1]
                else:
                    wx, wg = sfc1[:, (u - E1) * P:(u - E1 + 1) * P], sfc1[:, (u - E1 + 2) * P:(u - E1 + 3) * P]
                if u == 0:
                    pe.wait_ge(pre1.sem, pre1.after("cT", b))
                if past(b, 1) or u >= 2:
                    pe.wait_ge(gelu_done, before(b, u))
                pe.matmul(ps_g[u % 2][:], wg, xT_all[:, b, :], start=True, stop=True).then_inc(g1_made, 1)
                if past(b, 1) or u >= 2:
                    pe.wait_ge(act_x, before(b, u))
                pe.matmul(ps_x[u % 2][:], wx, xT_all[:, b, :], start=True, stop=True).then_inc(x1_made, 1)
                if u < E1:
                    if past(b, 1) or u >= 1:
                        pe.wait_ge(a1_done, b * E1 + u)
                    pe.matmul(ps_c[:], pick[:, u, :], cT_all[:, b, :], start=True, stop=True).then_inc(c1_made, 1)

            def down_at(b, u):
                if u < E1:
                    pe.wait_ge(a1_done, b * E1 + u + 1)
                else:
                    pe.wait_ge(act_x, b * UNITS + u + 1)
                if u == 0:
                    if past(b, 1):
                        pe.wait_ge(post1.sem, post1.after("v", b - 1))
                w = fc2[:, u, :] if u < E1 else sfc2[:, u - E1, :]
                pe.matmul(ps_y1[:], w, hc[:, u % 2, :], start=(u == 0), stop=False).then_inc(y1_made, 1)

            def biases(b):
                for j in range(3):
                    mm = pe.matmul(ps_y1[:], b2_p[:, 1, j, :], cT_all[:, b, :], start=False, stop=(j == 2))
                mm.then_inc(post1.sem, 1)

            def end_at(b, u):
                if u == 2:
                    pe.wait_ge(post1.sem, post1.after("ws", b))
                    turn(ps_q, rden[:]).then_inc(post1.sem, 1)

            def body(b, full, previous, following):
                for u in range(UNITS):
                    if full:
                        up_at(b, u)
                    if full and u >= 1:
                        down_at(b, u - 1)
                    if previous and u == 0:
                        down_at(b - 1, UNITS - 1)
                        biases(b - 1)
                    if following:
                        pre_at(b + 1, u)
                    if previous:
                        end_at(b - 1, u)

            pe.wait_ge(fc2_scaled, 2)
            for u in range(UNITS):
                pre_at(0, u)
            body(0, True, False, True)
            with pe.Fori(1, NB - 1) as b:
                body(b, True, True, True)
            body(NB - 1, True, True, False)
            body(NB, False, True, False)

        @block.scalar
        def _(act):
            def pre_at(b, u):
                if u == 2:
                    act.wait_ge(pre1.sem, pre1.after("turn", b))
                    nc.scalar.copy(xT[:], ps_p[:]).then_inc(pre1.sem, 1)
                    nc.scalar.copy(xT_all[:, b, :], ps_p[:]).then_inc(pre1.sem, 1)
                if u == 5:
                    act.wait_ge(pre1.sem, pre1.after("v", b))
                    nc.scalar.copy(vT[:, :, 0:P], tiles(ps_p[:])).then_inc(pre1.sem, 1)
                if u == 15:
                    act.wait_ge(pre1.sem, pre1.after("cturn", b))
                    nc.scalar.copy(cT_all[:, b, :], ps_p[0:96, :].bitcast(BF16)[:, 0:S]).then_inc(pre1.sem, 1)

            def gelu_at(b, u):
                n = b * UNITS + u
                act.wait_ge(g1_made, n + 1)
                if past(b, 1) or u >= 2:
                    act.wait_ge(act_x, before(b, u))
                bias = col("fc1_b", 2 * u + 1) if u < E1 else col("sfc1_b", u - E1 + 2)
                nc.scalar.activation(hz[:, u % 2, :], ps_g[u % 2][:], ACT.Gelu, bias=bias).then_inc(gelu_done, 1)

            def end_at(b, u):
                if u == 0:
                    act.wait_ge(post1.sem, post1.after("y", b))
                    nc.scalar.activation(th[:], ps_y1[:], ACT.Tanh, bias=col("sb_half"), scale=0.5).then_inc(post1.sem, 1)

            def body(b, full, previous, following):
                for u in range(UNITS):
                    if full:
                        gelu_at(b, u)
                    if previous:
                        end_at(b - 1, u)
                    if following:
                        pre_at(b + 1, u)

            for u in range(UNITS):
                pre_at(0, u)
            body(0, True, False, True)
            with act.Fori(1, NB - 1) as b:
                body(b, True, True, True)
            body(NB - 1, True, True, False)
            body(NB, False, True, False)

        @block.vector
        def _(dve):
            v = nc.vector

            def pre_at(b, u):
                def step(name, ins, own=False):
                    ins.then_inc(pre1.sem, 1)
                    if own:
                        wait_apart(dve, (pre1.sem, pre1.after(name, b)))
                    else:
                        dve.wait_ge(pre1.sem, pre1.after(name, b))

                if u == 0:
                    if past(b, 1):
                        dve.wait_ge(pre1.sem, pre1.after("cT", b - 1))
                    for t in range(T):
                        ins = v.bn_stats(st6[:, 3, t], x_all[:, b, t])
                    step("stats", ins, own=True)
                    for t in range(T):
                        ins = v.bn_aggr(mv[:, 3, t], st6[:, 3, t])
                    ins.then_inc(pre1.sem, 1)
                if u == 1:
                    dve.wait_ge(pre1.sem, pre1.after("rstd", b))
                    for t in range(T):
                        ins = v.tensor_scalar(xn[:, t], x_all[:, b, t], mv[:, 3, t, 0:1], rstd[:, 3, 1, t:t + 1], ALU.subtract, ALU.mult)
                    ins.then_inc(pre1.sem, 1)
                if u == 3:
                    dve.wait_ge(pre1.sem, pre1.after("q", b))
                    v.tensor_scalar(qT[:], ps_p[:], 0.0, None, ALU.max).then_inc(pre1.sem, 1)
                if u == 4:
                    dve.wait_ge(pre1.sem, pre1.after("k", b))
                    v.tensor_scalar(kT[:], tiles(ps_p[:]), 0.0, None, ALU.max).then_inc(pre1.sem, 1)
                if u == 6:
                    dve.wait_ge(pre1.sem, pre1.after("kv", b))
                    v.tensor_tensor(kv[:], ps_p[:, 0:P], block1[:], ALU.mult).then_inc(pre1.sem, 1)
                    v.tensor_scalar(ksum[:], block1[:], ps_p[:, P:P + 1], None, ALU.mult).then_inc(pre1.sem, 1)
                if u == 7:
                    dve.wait_ge(pre1.sem, pre1.after("dn", b))
                    v.tensor_scalar(o_num[:], ps_p[:], 1e-15, None, ALU.add).then_inc(pre1.sem, 1)
                if u in (8, 9):
                    c = (u - 8) * 256
                    if u == 8:
                        dve.wait_ge(pre1.sem, pre1.after("dn_eps", b))
                    v.reciprocal(r2[:, c:c + 256], o_num[:, c:c + 256]).then_inc(pre1.sem, 1)
                if u == 10:
                    dve.wait_ge(pre1.sem, pre1.after("num", b))
                    v.tensor_tensor(o_n[:], ps_p[:], r2[:], ALU.mult).then_inc(pre1.sem, 1)
                if u == 11:
                    dve.wait_ge(pre1.sem, pre1.after("pr", b))
                    v.tensor_scalar(sT_all[:, b, :], ps_p[:], col("bp"), None, ALU.add).then_inc(pre1.sem, 1)
                if u == 12:
                    dve.wait_ge(pre1.sem, pre1.after("logits", b))
                    lp = ps_p[:, 0:T * E1].rearrange("p (t e) -> p t e", t=T)
                    step("lmax", v.tensor_reduce(gm[:, 0, :], lp, AX, ALU.max))
                    v.tensor_tensor(lg[:, 0, :, 0:E1], lp, spread(gm[:, 0, :]), ALU.subtract).then_inc(pre1.sem, 1)
                if u == 13:
                    dve.wait_ge(pre1.sem, pre1.after("lexp", b))
                    step("lsum", v.tensor_reduce(gm[:, 1, :], lg[:, 1, :, 0:E1], AX, ALU.add))
                    step("lrec", v.reciprocal(gm[:, 2, :], gm[:, 1, :]))
                    step("score", v.tensor_tensor(lg[:, 2, :, 0:E1], lg[:, 1, :, 0:E1], spread(gm[:, 2, :]), ALU.mult), own=True)
                    for t in range(T):
                        ins = v.max(m8[:, t], lg[:, 2, t])
                    step("top8", ins)
                    step("top3", v.tensor_copy(m8v[:, :, 0:3], m8[:, :, 0:3]), own=True)
                    for t in range(T):
                        ins = v.match_replace(lg[:, 3, t], m8v[:, t], lg[:, 2, t], -2.0)
                    ins.then_inc(pre1.sem, 1)
                if u == 14:
                    dve.wait_ge(pre1.sem, pre1.after("rep", b))
                    step("mask", v.tensor_tensor(lg[:, 4, :, 0:E1], lg[:, 3, :, 0:E1], lg[:, 2, :, 0:E1], ALU.not_equal))
                    step("tw", v.tensor_tensor(lg[:, 5, :, 0:E1], lg[:, 4, :, 0:E1], lg[:, 2, :, 0:E1], ALU.mult))
                    step("tsum", v.tensor_reduce(gm[:, 3, :], lg[:, 5, :, 0:E1], AX, ALU.add))
                    step("tsum_eps", v.tensor_scalar(gm[:, 4, :], gm[:, 3, :], 1e-20, None, ALU.add))
                    step("trec", v.reciprocal(gm[:, 5, :], gm[:, 4, :]))
                    step("comb", v.tensor_tensor(lg[:, 4, :, 0:E1], lg[:, 5, :, 0:E1], spread(gm[:, 5, :]), ALU.mult))
                    c = lg[:, 4, :, 0:E1]
                    step("p1", v.tensor_copy(cpb[:, :, 0:E1], c))
                    step("s1", v.tensor_tensor(cpf[:, 0, :, 0:E1], c, cpb[:, :, 0:E1], ALU.subtract))
                    step("p2", v.tensor_copy(cpb[:, :, 32:32 + E1], cpf[:, 0, :, 0:E1]))
                    step("s2", v.tensor_tensor(cpf[:, 1, :, 0:E1], cpf[:, 0, :, 0:E1], cpb[:, :, 32:32 + E1], ALU.subtract))
                    v.tensor_copy(cpb[:, :, 64:64 + E1], cpf[:, 1, :, 0:E1]).then_inc(pre1.sem, 1)

            def spread(x):
                return x.unsqueeze(2).broadcast_to([P, T, E1])

            def unit_at(b, u):
                n = b * UNITS + u
                dve.wait_ge(gelu_done, n + 1)
                dve.wait_ge(x1_made, n + 1)
                if past(b, 1) or u >= 2:
                    dve.wait_ge(y1_made, before(b, u))
                bias = col("fc1_b", 2 * u) if u < E1 else col("sfc1_b", u - E1)
                mid = cbc if u < E1 else hc
                ins = v.scalar_tensor_tensor(out=mid[:, u % 2, :], in0=ps_x[u % 2][:], scalar=bias,
                                             in1=hz[:, u % 2, :], op0=ALU.add, op1=ALU.mult)
                ins.then_inc(act_x, 1)
                if u < E1:
                    dve.wait_ge(act_x, n + 1)
                    dve.wait_ge(c1_made, b * E1 + u + 1)
                    v.tensor_tensor(hc[:, u % 2, :], cbc[:, u % 2, :], ps_c[:], ALU.mult).then_inc(a1_done, 1)

            def end_at(b, u):
                if u == 0:
                    dve.wait_ge(post1.sem, post1.after("th", b))
                    v.tensor_scalar(scan[:], ps_y1[:], col("sb"), None, ALU.add).then_inc(post1.sem, 1)
                    dve.wait_ge(post1.sem, post1.after("v", b))
                    v.scalar_tensor_tensor(out=s_near[:], in0=th[:], scalar=1.0, in1=scan[:], op0=ALU.add, op1=ALU.mult).then_inc(post1.sem, 1)
                    dve.wait_ge(post1.sem, post1.after("w", b))
                    v.tensor_tensor(rden[:], s_near[:], sT_all[:, b, :], ALU.mult).then_inc(post1.sem, 1)
                if u == 2:
                    dve.wait_ge(post1.sem, post1.after("turn", b))
                    v.scalar_tensor_tensor(out=x_all[:, b], in0=tiles(ps_q[:]), scalar=0.5, in1=x_all[:, b], op0=ALU.mult,
                                           op1=ALU.add).then_inc(post1.sem, 1)

            def body(b, full, previous, following):
                for u in range(UNITS):
                    if full:
                        unit_at(b, u)
                    if previous:
                        end_at(b - 1, u)
                    if following:
                        pre_at(b + 1, u)

            for u in range(UNITS):
                pre_at(0, u)
            body(0, True, False, True)
            with dve.Fori(1, NB - 1) as b:
                body(b, True, True, True)
            body(NB - 1, True, True, False)
            body(NB, False, True, False)

        @block.gpsimd
        def _(pool):
            p = nc.gpsimd

            def pre_at(b, u):
                if u == 0:
                    wait_apart(pool, (pre1.sem, pre1.after("moments", b)))
                    p.tensor_scalar(rstd[:, 3, 0, :], mv[:, 3, :, 1], EPS, None, ALU.add).then_inc(pre1.sem, 1)
                    pool.wait_ge(pre1.sem, pre1.after("eps", b))
                    p.tensor_tensor(rstd[:, 3, 1, :], rstd[:, 3, 0, :], mhalf[:], ALU.pow).then_inc(pre1.sem, 1)
                if u == 12:
                    pool.wait_ge(pre1.sem, pre1.after("lsub", b))
                    p.tensor_tensor(lg[:, 1, :, 0:E1], ebase[:, :, 0:E1], lg[:, 0, :, 0:E1], ALU.pow).then_inc(pre1.sem, 1)

            def body(b, following):
                for u in range(UNITS):
                    if following:
                        pre_at(b + 1, u)

            for u in range(UNITS):
                pre_at(0, u)
            body(0, True)
            with pool.Fori(1, NB - 1) as b:
                body(b, True)

        layer1.__exit__(None, None, None)


def lay_out(i):
    import numpy as np

    def c(a):
        return np.ascontiguousarray(a)

    def chunks(a, n):
        return a.reshape(n, P, -1).transpose(1, 0, 2)

    a = {k: np.asarray(v) for k, v in i.items()}
    f = np.float32
    vec = np.zeros((P, 96), f)
    given = {
        "conv_w": chunks(a["L0_attn_conv_w"].reshape(256, 4), 2).reshape(P, 8),
        "conv_b": chunks(a["L0_attn_conv_b"][:, None], 2).reshape(P, 2),
        "dt_b": chunks(a["L0_attn_dt_proj_b"][:, None], 2).reshape(P, 2),
        "bq": a["L0_ffn_in_proj_b"].reshape(3, P).T[:, 0:2],
        "bv": a["L0_ffn_in_proj_b"].reshape(3, P).T[:, 2:3],
        "bo": a["L0_ffn_out_proj_b"][:, None],
        "ln1_g": a["L0_ffn_ln1_g"][:, None],
        "ln1_b": a["L0_ffn_ln1_b"][:, None],
        "b1": a["L0_ffn_b1"].reshape(16, P).T,
        "bp": a["L1_attn_b_proj"][:, None],
        "fc1_b": a["L1_ffn_fc1_b"].reshape(30, P).T,
        "mult": a["L1_ffn_geglu_mult"].T,
        "sfc1_b": a["L1_ffn_s_fc1_b"].reshape(4, P).T,
        "s_mult": a["L1_ffn_s_geglu_mult"].reshape(2, P).T,
        "sb": a["L1_ffn_s_fc2_b"][:, None],
    }
    n = 0
    for name, w in VEC:
        if name in given:
            vec[:, n:n + w] = given[name]
        n += w
    rows = np.zeros((1, 4, P), f)
    rows[0, 0], rows[0, 1] = a["L0_ffn_ln2_g"], a["L0_ffn_ln2_b"]
    rows[0, 2, 0:12] = np.concatenate([a["L0_ffn_b_group"], a["L0_ffn_b_expert"].reshape(8)])
    rows[0, 3, 0:4] = (4, 3, 2, 1)
    eye = np.eye(P, dtype=f)
    return {
        "x": c(a["L0_attn_x"]),
        "ident": eye,
        "vec": vec,
        "rows": rows.reshape(1, 4 * P).reshape(4 * P),
        "head_of": c(np.repeat(np.eye(NH, dtype=f), HD, axis=1)),
        "pick": c(np.tile(np.eye(32, 16, dtype=f), (3, 1))),
        "block1": c(np.kron(np.eye(4, dtype=f), np.ones((32, 32), f))),
        "w_in0": c(a["L0_attn_in_proj_w"].T),
        "w_dt": c(chunks(a["L0_attn_dt_proj_w"].T, 2)),
        "w_out0": c(chunks(a["L0_attn_out_proj_w"].T, 2)),
        "w_qkv0": c(a["L0_ffn_in_proj_w"].T),
        "w_o0": c(a["L0_ffn_out_proj_w"].T),
        "w_gate0": c(np.concatenate([a["L0_ffn_w_group"], a["L0_ffn_w_expert"].transpose(1, 0, 2).reshape(P, 8)], axis=1)),
        "w1": c(a["L0_ffn_w1"].transpose(1, 0, 2)),
        "w2": c(a["L0_ffn_w2"].reshape(E0, 2, P, P).transpose(2, 0, 1, 3)),
        "b2": c(a["L0_ffn_b2"]),
        "w_qkv1": c(a["L1_attn_W_qkv"].T),
        "w_proj1": c(a["L1_attn_W_proj"].T),
        "w_gate1": c(a["L1_ffn_gate_w"].T),
        "fc1": c(a["L1_ffn_fc1_w"].transpose(2, 0, 1)),
        "fc2": c(a["L1_ffn_fc2_w"].transpose(2, 0, 1)),
        "fc2_b": c(a["L1_ffn_fc2_b"]),
        "sfc1": c(a["L1_ffn_s_fc1_w"].T),
        "sfc2": c(chunks(a["L1_ffn_s_fc2_w"].T, 2)),
    }


def kernel(**inputs):
    import concourse.bacc as bacc
    from concourse.bass_utils import run_bass_kernel_spmd

    nc = bacc.Bacc("TRN2", target_bir_lowering=False, num_devices=1)
    arrays = lay_out(inputs)
    d = {n: nc.dram_tensor("in_" + n, a.shape, mybir.dt.from_np(a.dtype), kind="ExternalInput").ap() for n, a in arrays.items()}
    out = nc.dram_tensor("out", [NB, S, P], F32, kind="ExternalOutput").ap()
    build(nc, d, out)
    return run_bass_kernel_spmd(nc, [{"in_" + n: a for n, a in arrays.items()}], core_ids=[0]).results[0]["out"]
```

```python
from contextlib import ExitStack

import concourse.bass as bass
from concourse import mybir

F32 = mybir.dt.float32
BF16 = mybir.dt.bfloat16
ALU = mybir.AluOpType
ACT = mybir.ActivationFunctionType
AX = mybir.AxisListType.X

P = 128
NB = 8
S = 512
T = S // P
NH, HD = 16, 8
NG = NH // 4
PIECES = 6
KROWS = PIECES * HD
SLOTS = 64
LAG = 24
E0, F0 = 8, 256
E1, F1 = 15, 128
EPS = 1e-5
LN2 = 0.6931471805599453
SCALE = float(HD) ** -0.5
DECAY, GAIN = 0.9, 0.1


class Steps:

    def __init__(self, sem, names):
        self.sem, self.n, self.at = sem, len(names), {n: i for i, n in enumerate(names)}

    def after(self, name, b):
        return b * self.n + self.at[name] + 1


def past(b, least):
    return not isinstance(b, int) or b >= least


SSM = ["u0", "u0_sb", "u1", "u1_sb", "c00", "c01", "c02", "c03", "c10", "c11", "c12", "c13",
       "z0", "th0", "gu0", "z1", "th1", "gu1", "p", "scan", "res", "s"]
PRE = ["stats", "moments", "eps", "rstd", "xn", "turn", "xT", "xT_kept", "q", "q1", "qr", "k", "k1", "kr",
       "v", "v_sb", "q2", "q3", "k2", "k3"]
SHIFT = ["neg", "hi", "rest", "lo"]
POST = ["den", "rd0", "rd1", "rd2", "rd3", "on", "proj", "r1", "turn1", "stats1", "moments1", "eps1", "rstd1", "z",
        "turn2", "x1", "logits", "lg", "gmax", "gsub", "gexp", "gsum", "gties", "gtop", "ghot", "ediff", "eabs",
        "eexp", "eden", "erec", "chot", "first", "second", "p1", "s1", "p2", "s2", "p3", "cturn", "cT",
        "y", "r2", "turn3", "stats2", "moments2", "eps2", "rstd2"]
AT = {"u0": -27, "u0_sb": -26, "u1": -25, "u1_sb": -24, "c0": -23, "c1": -19, "z0": -15, "th0": -14, "gu0": -13,
      "z1": -11, "th1": -10, "gu1": -9, "p": -7, "scan": -6, "res": -4, "s": -3,
      "stats": -52, "rstd": -50, "xn": -46, "turn": -40, "xT": -39, "q": -37, "q1": -36, "qr": -35, "k": -33, "k1": -32,
      "kr": -31, "v": -29, "v_sb": -28, "q2": -27, "stacks_out": -22, "stacks_in0": -16, "stacks_in1": -7,
      "stacks_in2": 8, "stacks_in3": 24, "values0": -20, "values1": -4, "values2": 10, "values3": 26,
      "out0": 43, "out1": 59, "out2": 75, "out3": 91,
      "den": 95, "rd": 96, "proj": 101, "r1": 102, "turn1": 103, "stats1": 104, "rstd1": 105, "z": 107, "turn2": 109,
      "x1": 110, "logits": 111, "group": 112, "gexp": 113, "expert": 114, "eexp": 115, "comb": 116, "cturn": 119,
      "cT": 120, "experts": 121, "s_near": 132, "s_turn": 134, "s_tok": 135, "y": 148, "r2": 149, "turn3": 150,
      "stats2": 151, "rstd2": 152, "z2": 154, "gain": 155, "tanh": 158, "w": 159, "ws": 160,
      "load1": 92, "ones1": 92, "scale1": 106}
C_AT = [AT["experts"] + 13 * e // 4 for e in range(E0)]
Z_AT = [C_AT[k // 2] + 1 + k % 2 for k in range(2 * E0)]
Y_AT = [z + 2 for z in Z_AT]
UNITS = E1 + 2
PRE1_AT = [94 + u for u in range(UNITS)]
UNIT1_AT = [114 + 2 * u for u in range(UNITS)]
SETUP = {"dt_half": 1, "w_out0": 2, "bo_all": 3, "sb_half": 4, "b2": 8}
VEC = [("conv_w", 8), ("conv_b", 2), ("dt_b", 2), ("dt_half", 2), ("bq", 2), ("bv", 1), ("bo", 1), ("bo_all", 1), ("ln1_g", 1),
       ("ln1_b", 1), ("b1", 16), ("bp", 1), ("fc1_b", 30), ("mult", 15), ("sfc1_b", 4), ("s_mult", 2), ("sb", 1), ("sb_half", 1)]
TAIL = ["s_near", "s_turn", "s_tok", "z2", "gain", "bias", "tanh", "w", "ws", "x_new"]
PRE1 = ["stats", "moments", "eps", "rstd", "xn", "turn", "xT", "xT_kept", "q", "q_sb", "k", "k_sb", "v", "v_sb",
        "kv", "kv_sb", "ks_sb", "dn", "dn_eps", "rd0", "rd1", "num", "o", "pr", "s"]
GATE1 = ["logits", "lmax", "lsub", "lexp", "lsum", "lrec", "score", "top8", "top3", "rep", "mask", "tw", "tsum", "tsum_eps",
         "trec", "comb", "p1", "s1", "p2", "s2", "p3", "cturn", "cT"]
POST1 = ["y", "th", "v", "w", "ws", "turn", "out"]


def build(nc, d, out):
    with ExitStack() as ctx:
        def sb(name, shape, dt=F32):
            return ctx.enter_context(nc.sbuf_tensor(name, shape, dt))

        def sem(name):
            return ctx.enter_context(nc.semaphore(name))

        def tiles(ap):
            return ap.rearrange("p (t n) -> p t n", t=T)

        w_in0 = sb("w_in0", [P, 384])
        w_dt = sb("w_dt", [P, 2, 256])
        w_out0 = sb("w_out0", [P, 2, P])
        w_qkv0 = sb("w_qkv0", [P, 384])
        w_o0 = sb("w_o0", [P, P])
        w_gate0 = sb("w_gate0", [P, 12])
        w1 = sb("w1", [P, E0, F0])
        w2 = sb("w2", [P, E0, 2, P])
        ident = sb("ident", [P, P])
        identb = sb("identb", [P, P], BF16)
        head_of = sb("head_of", [NH, P])
        pick = sb("pick", [96, 16, P], BF16)
        pick_f = sb("pick_f", [96, 16])
        block1 = sb("block1", [P, P])
        vec = sb("vec", [P, 96])
        rows = sb("rows", [P, 4, P])
        b2_f = sb("b2_f", [96, 2, P])
        b2_p = sb("b2_p", [96, 2, 3, P], BF16)
        decay = sb("decay", [P, S])
        mhalf = sb("mhalf", [P, T])
        ebase = sb("ebase", [P, T, 20])
        x_all = sb("x_all", [P, NB, T, P])
        xT_all = sb("xT_all", [P, NB, S])
        sT_all = sb("sT_all", [P, NB, S])
        st6 = sb("st6", [P, 4, T, 6])
        mv = sb("mv", [P, 4, T, 2])
        rstd = sb("rstd", [P, 4, 2, T])
        xn = sb("xn", [P, T, P])
        xT = sb("xT", [P, S])
        up = sb("up", [P, 2, S + 3])
        uc = sb("uc", [P, 2, S])
        th = sb("th", [P, S])
        gu = up[:, :, 3:3 + S]
        scan = sb("scan", [P, S])
        s_tok_f = sb("s_tok", [P, S])
        qk_r = sb("qk_r", [P, 2, S])
        qk_p = sb("qk_p", [P, 2, 3, S], BF16)
        qs_all = sb("qs_all", [P, NH, S], BF16)
        ks_all = sb("ks_all", [P, NH, S], BF16)
        qs = qs_all[0:KROWS + 2]
        ks = ks_all[0:KROWS + 2]
        v_new = sb("v_new", [P, T, P])
        v_aug = sb("v_aug", [P, T, NH, 32])
        smax = sb("smax", [P, NG, 4, T])
        smax_n = sb("smax_n", [P, 4, T])
        smax_r = sb("smax_r", [P, 4, T])
        smax_p = sb("smax_p", [P, T, 2, 4], BF16)
        smax_t = sb("smax_t", [8, S], BF16)
        probs = sb("probs", [P, 8, S])
        oT = sb("oT", [P, S])
        o_num = sb("o_num", [P, S])
        o_den = sb("o_den", [NH, S])
        rden = sb("rden", [P, S])
        o_n = sb("o_n", [P, S])
        r1 = sb("r1", [P, S])
        z1 = sb("z1", [P, T, P])
        x1T = sb("x1T", [P, S])
        gl = sb("gl", [P, T, 12])
        gm = sb("gm", [P, 8, T])
        g4 = sb("g4", [P, 8, T, 4])
        comb = sb("comb", [P, T, 4, 2])
        cpf = sb("cpf", [P, 2, T, 16])
        cpb = sb("cpb", [P, T, 96], BF16)
        cT = sb("cT", [96, S], BF16)
        cbc = sb("cbc", [P, 2, S])
        hz = sb("hz", [P, 2, S])
        hc = sb("hc", [P, 2, S])
        r2 = sb("r2", [P, S])
        zt, zg, tht = tiles(rden[:]), tiles(o_n[:]), tiles(r1[:])
        s_tok = tiles(s_tok_f[:])
        s_near = z1[:].rearrange("p t n -> p (t n)")
        cT_all = probs[0:96, 4:8].rearrange("p e f -> p (e f)").bitcast(BF16).rearrange("p (b n) -> p b n", b=NB)
        qs_f = qs_all[:].rearrange("p h n -> p (h n)").bitcast(F32)
        ks_f = ks_all[:].rearrange("p h n -> p (h n)").bitcast(F32)
        fc1 = qs_f[:, 0:E1 * 2 * F1].rearrange("p (e f) -> p e f", e=E1)
        fc2 = ks_f[:, 0:E1 * P].rearrange("p (e f) -> p e f", e=E1)
        n = E1 * P
        sfc1, sfc2 = ks_f[:, n:n + 512], ks_f[:, n + 512:n + 768].rearrange("p (c f) -> p c f", c=2)
        w_qkv1, w_proj1, w_gate1 = ks_f[:, n + 768:n + 1152], ks_f[:, n + 1152:n + 1280], ks_f[:, n + 1280:n + 1280 + E1]
        z_tok = probs[:, 0:2].rearrange("p a n -> p (a n)")[:, 0:T * (P + 4)].rearrange("p (t n) -> p t n", t=T)
        kv_bd, ks_bd = probs[:, 2, 0:P], probs[:, 2, P:2 * P]
        lg = sb("lg", [P, 6, T, 20])
        gm1 = sb("gm1", [P, 8, T])
        cpf1 = sb("cpf1", [P, 2, T, 16])
        cpb1 = ks_f[:, 26 * P:27 * P + 64].bitcast(BF16).rearrange("p (t n) -> p t n", t=T)
        kT, vT, qT, kv, ksum = tiles(qk_r[:, 1]), z_tok, qk_r[:, 0], kv_bd, ks_bd
        o_num1, r21, o_n1, cbc1 = uc[:, 0], uc[:, 1], oT, gu
        v_flat = v_aug[:].rearrange("p t h d -> p (t h d)")
        hz1, hc1 = (v_flat[:, k * 2 * S:(k + 1) * 2 * S].rearrange("p (a n) -> p a n", a=2) for k in range(2))
        m8 = sb("m8", [P, T, 8])
        m8v = sb("m8v", [P, T, 8])

        bank = [ctx.enter_context(nc.psum_tensor(f"bank{i}", [P, S], F32)) for i in range(8)]
        ps_s = bank[0:2]
        ps_t = bank[2:4]
        ps_o, ps_a, ps_b, ps_y = bank[4:8]
        ps_g, ps_x = bank[0:2], [bank[2], bank[7]]
        ps_c, ps_y1, ps_p, ps_q = bank[4], bank[3], bank[5], bank[6]

        stack = [nc.dram_tensor(f"stack_{n}", [P, PIECES, S], BF16, kind="Internal").ap() for n in "qk"]
        shift_d = nc.dram_tensor("shift_rows", [2, 4, S], BF16, kind="Internal").ap()

        x_first = sem("x_first")
        x_rest = sem("x_rest")
        w_early = sem("w_early")
        w_late = sem("w_late")
        w_attn1 = sem("w_attn1")
        w_last = sem("w_last")
        consts = sem("consts")
        setup = sem("setup")
        setup_pe = sem("setup_pe")
        setup_pool = sem("setup_pool")
        ready1 = sem("ready1")
        ssm, pre, post, tail = (Steps(sem(n), s) for n, s in (("ssm", SSM), ("pre", PRE), ("post", POST), ("tail", TAIL)))
        pre1, gate1, post1 = Steps(sem("pre1"), PRE1), Steps(sem("gate1"), GATE1), Steps(sem("post1"), POST1)
        shift = Steps(sem("shift"), SHIFT)
        s_made = sem("s_made")
        s_read = sem("s_read")
        t_made = sem("t_made")
        exp_done = sem("exp_done")
        pv_done = sem("pv_done")
        ot_made = sem("ot_made")
        o_moved = [sem(f"o_moved{g}") for g in range(NG)]
        v_put = sem("v_put")
        stack_out = sem("stack_out")
        stack_in = [sem(f"stack_in{g}") for g in range(NG)]
        shift_out = sem("shift_out")
        shift_in = sem("shift_in")
        c_made = sem("c_made")
        c_sb = sem("c_sb")
        z_made = sem("z_made")
        z_sb = sem("z_sb")
        hc_made = sem("hc_made")
        y_made = sem("y_made")
        g1_made = sem("g1_made")
        x1_made = sem("x1_made")
        c1_made = sem("c1_made")
        gelu_done = sem("gelu_done")
        act_x = sem("act_x")
        a1_done = sem("a1_done")
        y1_made = sem("y1_made")
        out_sem = sem("out_sem")

        def wait_apart(eng, *waits):
            waits = [(sem, value if isinstance(value, int) else eng.to_reg(value)) for sem, value in waits]
            eng.wait_ge(consts, 2)
            for sem, value in waits:
                eng.wait_ge(sem, value)

        V = {}
        n = 0
        for name, w in VEC:
            V[name] = n
            n += w

        def col(name, i=0):
            return vec[:, V[name] + i:V[name] + i + 1]

        def before(b, u):
            return b * UNITS + (u - 1 if u else 0)

        def s_bank_of(b):
            return bank[1] if isinstance(b, int) and b == NB - 1 else ps_a

        def half(b, u):
            return u % 2 if past(b, 1) else 0

        def bank_before(b, u):
            return before(b, u) if past(b, 1) else u

        def s_use(b, pos):
            if isinstance(b, int) and b == 0:
                return pos if pos < 2 else pos - 1
            if isinstance(b, int) and b == NB:
                return b * (SLOTS + NG) - 1
            return b * (SLOTS + NG) + pos - 1

        def s_pos(s):
            return (s // 16) * 17 + s % 16 + (1 if s % 16 >= 2 else 0)

        def turn_use(b, g):
            return (b, 17 * g + 19) if g < NG - 1 else (b + 1, 2)

        def s_bank(b, pos):
            return ps_s[s_use(b, pos) % 2] if isinstance(b, int) else ps_s[(pos + 1) % 2]

        program = nc.Block()
        block = program.__enter__()

        @block.sync
        def _(sp):
            xr = d["x"].rearrange("b (t p) d -> b p t d", p=P)
            sp.dma_start(x_all[:, 0], xr[0]).then_inc(x_first, 16)
            early = [(ident[:], d["ident"]), (vec[:], d["vec"]), (w_qkv0[:], d["w_qkv0"]),
                     (w_in0[:], d["w_in0"]), (w_dt[:], d["w_dt"]), (w_out0[:], d["w_out0"]), (w_o0[:], d["w_o0"]),
                     (w_gate0[:], d["w_gate0"]), (head_of[:], d["head_of"]), (pick_f[:], d["pick"]),
                     (rows[:], d["rows"].partition_broadcast(P))]
            for dst, src in early:
                sp.dma_start(dst, src).then_inc(w_early, 16)
            sp.wait_ge(consts, 1)
            for k in range(3):
                sp.dma_start(b2_f[32 * k:32 * k + E0, 0, :], d["b2"]).then_inc(w_early, 16)
                sp.dma_start(b2_f[32 * k:32 * k + E1, 1, :], d["fc2_b"]).then_inc(w_early, 16)
            for b in range(1, NB):
                sp.dma_start(x_all[:, b], xr[b]).then_inc(x_rest, 16)
            late = [(w1[:], d["w1"]), (w2[:], d["w2"]), (block1[:], d["block1"])]
            for dst, src in late:
                sp.dma_start(dst, src).then_inc(w_late, 16)

            def stacks_out(b):
                wait_apart(sp, (pre.sem, pre.after("k3", b)), *[(stack_in[g], 32 * b) for g in range(NG) if past(b, 1)])
                for j, parts in ((0, ((0, 0, 3), (3, 0, 2), (5, 0, 1))), (1, ((0, 0, 0), (1, 0, 0), (2, 0, 0), (3, 1, 0), (4, 1, 0), (5, 2, 0)))):
                    for to, first, n in parts:
                        n = n or 1
                        sp.dma_start(stack[j][:, to:to + n, :], qk_p[:, j, first:first + n, :]).then_inc(stack_out, 16)

            def stacks_in(b, g):
                wait_apart(sp, (stack_out, 16 * 9 * (b + 1)), *[(t_made, SLOTS * (b - 1) + 16 * (g + 1))] * past(b, 1))
                for j, dst in ((0, qs), (1, ks)):
                    src = stack[j].rearrange("(h d) s n -> h (d s) n", h=NH)[4 * g:4 * g + 4].rearrange("h r n -> r h n")
                    sp.dma_start(dst[0:KROWS, 4 * g:4 * g + 4, :], src).then_inc(stack_in[g], 16)

            def shift_rows(b, g):
                n = b * NG + g
                sp.wait_ge(s_read, s_use(*turn_use(b, g)) + 1)
                if past(n, 1):
                    sp.wait_ge(shift_in, 16 * n)
                sp.dma_start(shift_d.rearrange("a r n -> (a r) n"), smax_t[:]).then_inc(shift_out, 16)
                wait_apart(sp, (shift_out, 16 * (n + 1)))
                sp.dma_start(qs[KROWS:KROWS + 2, 4 * g:4 * g + 4, :], shift_d).then_inc(shift_in, 16)

            def outputs(b, g):
                wait_apart(sp, (ot_made, b * NG + g + 1), *[(post.sem, post.after("on", b - 1))] * past(b, 1))
                for r in range(4):
                    sp.dma_start(o_num[32 * g + 8 * r:32 * g + 8 * r + 8, :], oT[32 * r:32 * r + 8, :]).then_inc(o_moved[g], 16)
                    sp.dma_start(o_den[4 * g + r:4 * g + r + 1, :], oT[32 * r + 8:32 * r + 9, :]).then_inc(o_moved[g], 16)

            def body(b, full, previous, following):
                for s in range(SLOTS):
                    if previous and s == 2:
                        shift_rows(b - 1, NG - 1)
                    if full and s in (18, 34, 50):
                        shift_rows(b, s // 16 - 1)
                    for g in range(NG):
                        for alive, n, pos in ((previous, b - 1, s + SLOTS), (full, b, s)):
                            if alive and pos == AT[f"out{g}"]:
                                outputs(n, g)
                        for alive, n, pos in ((full, b, s), (following, b + 1, s - SLOTS)):
                            if alive and pos == AT[f"stacks_in{g}"]:
                                stacks_in(n, g)
                    if isinstance(b, int) and b == NB and s + SLOTS == AT["load1"]:
                        sp.wait_ge(t_made, SLOTS * NB)
                        for dst, src in ((w_qkv1, "w_qkv1"), (w_proj1, "w_proj1"), (w_gate1, "w_gate1")):
                            sp.dma_start(dst, d[src]).then_inc(w_attn1, 16)
                        for dst, src in ((fc1, "fc1"), (fc2, "fc2"), (sfc1, "sfc1"), (sfc2, "sfc2")):
                            sp.dma_start(dst, d[src]).then_inc(w_last, 16)
                    if following and s - SLOTS == AT["stacks_out"]:
                        stacks_out(b + 1)

            sp.wait_ge(consts, 2)
            stacks_out(0)
            stacks_in(0, 0)
            stacks_in(0, 1)
            body(0, True, False, True)
            body(1, True, True, True)
            with sp.Fori(2, NB - 1) as b:
                body(b, True, True, True)
            body(NB - 1, True, True, False)
            body(NB, False, True, False)
            with sp.Fori(0, NB) as b:
                sp.wait_ge(post1.sem, post1.after("out", b))
                sp.dma_start(out.rearrange("b (t p) d -> b p t d", p=P)[b], x_all[:, b]).then_inc(out_sem, 16)
            sp.wait_ge(out_sem, 16 * NB)

        @block.tensor
        def _(pe):
            pe.wait_ge(w_early, 16 * 17)
            pe.wait_ge(consts, 2)
            pe.matmul(ps_b[:, 0:1], w_o0[:], col("bv"), start=True, stop=True).then_inc(setup_pe, 1)

            def turn(dst, src):
                for t in range(T):
                    mm = pe.transpose(dst[:, t * P:(t + 1) * P], src[:, t * P:(t + 1) * P], ident[:])
                return mm

            def flat(ap):
                return ap.rearrange("p t n -> p (t n)")

            def ssm_at(b, s):
                if s == AT["u0"]:
                    if past(b, 1):
                        pe.wait_ge(ssm.sem, ssm.after("s", b - 1))
                    pe.wait_ge(pre.sem, pre.after("v_sb", b))
                    pe.matmul(ps_a[:], w_in0[:, 0:P], xT[:], start=True, stop=True).then_inc(ssm.sem, 1)
                if s == AT["u1"]:
                    pe.wait_ge(ssm.sem, ssm.after("u0_sb", b))
                    pe.matmul(ps_a[:], w_in0[:, P:2 * P], xT[:], start=True, stop=True).then_inc(ssm.sem, 1)
                if s in (AT["z0"], AT["z1"]):
                    j = 0 if s == AT["z0"] else 1
                    pe.wait_ge(ssm.sem, ssm.after(("c13", "gu0")[j], b))
                    pe.matmul(ps_a[:], w_dt[:, 0, j * P:(j + 1) * P], uc[:, 0, :], start=True, stop=False)
                    pe.matmul(ps_a[:], w_dt[:, 1, j * P:(j + 1) * P], uc[:, 1, :], start=False, stop=True).then_inc(ssm.sem, 1)
                if s == AT["p"]:
                    pe.wait_ge(ssm.sem, ssm.after("gu1", b))
                    pe.matmul(ps_a[:], w_out0[:, 0, :], gu[:, 0, :], start=True, stop=False)
                    pe.matmul(ps_a[:], w_out0[:, 1, :], gu[:, 1, :], start=False, stop=True).then_inc(ssm.sem, 1)
                if s == AT["res"]:
                    pe.wait_ge(ssm.sem, ssm.after("scan", b))
                    pe.matmul(ps_a[:], w_in0[:, 2 * P:3 * P], xT[:], start=True, stop=True).then_inc(ssm.sem, 1)

            def pre_at(b, s):
                if s == AT["turn"]:
                    pe.wait_ge(pre.sem, pre.after("xn", b))
                    if past(b, 1):
                        pe.wait_ge(ssm.sem, ssm.after("s", b - 1))
                    if past(b, 3):
                        pe.wait_ge(tail.sem, tail.after("s_tok", b - 3))
                    turn(ps_a, flat(xn)).then_inc(pre.sem, 1)
                if s == AT["q"]:
                    pe.wait_ge(pre.sem, pre.after("xT_kept", b))
                    pe.matmul(ps_a[:], w_qkv0[:, 0:P], xT[:], start=True, stop=True).then_inc(pre.sem, 1)
                if s == AT["k"]:
                    pe.wait_ge(pre.sem, pre.after("qr", b))
                    pe.matmul(ps_a[:], w_qkv0[:, P:2 * P], xT[:], start=True, stop=True).then_inc(pre.sem, 1)
                if s == AT["v"]:
                    pe.wait_ge(pre.sem, pre.after("kr", b))
                    for t in range(T):
                        mm = pe.matmul(ps_a[:, t * P:(t + 1) * P], xT[:, t * P:(t + 1) * P], w_qkv0[:, 2 * P:3 * P], start=True, stop=True)
                    mm.then_inc(pre.sem, 1)

            def scores(b, s):
                h, t = s // T, s % T
                u = s_use(b, s_pos(s))
                if s % 16 == 0:
                    pe.wait_ge(stack_in[s // 16], 32 * (b + 1))
                if past(b, 1) or u >= 2:
                    pe.wait_ge(s_read, u - 1)
                pe.matmul(s_bank(b, s_pos(s))[:], qs[0:KROWS, h, t * P:(t + 1) * P], ks[0:KROWS, h, :],
                          start=True, stop=True).then_inc(s_made, 1)

            def shift_turn(b, g):
                at, pos = turn_use(b, g)
                u = s_use(at, pos)
                pe.wait_ge(shift.sem, shift.after("lo", b * NG + g))
                pe.wait_ge(s_read, u - 1)
                for t in range(T):
                    mm = pe.transpose(s_bank(at, pos)[0:8, :].bitcast(BF16)[:, t * P:(t + 1) * P],
                                      smax_p[:, t].rearrange("p a r -> p (a r)"), identb[:])
                mm.then_inc(s_made, 1)

            def transposed(b, v):
                g, t, r = v // 16, v % 16 // 4, v % 4
                h = 4 * g + r
                if v % 16 == 0:
                    pe.wait_ge(shift_in, 16 * (b * NG + g + 1))
                if past(b, 1) or v >= 2:
                    pe.wait_ge(exp_done, b * SLOTS + v - 1)
                pe.matmul(ps_t[v % 2][:], ks[:, h, t * P:(t + 1) * P], qs[:, h, :], start=True, stop=True).then_inc(t_made, 1)

            def weighted(b, q):
                g, t = q // 4, q % 4
                pe.wait_ge(exp_done, b * SLOTS + 4 * q + 4)
                if t == 0:
                    pe.wait_ge(v_put, b * NG + g + 1)
                    if past(b, 1) or g >= 1:
                        pe.wait_ge(ot_made, b * NG + g)
                for r in range(4):
                    mm = pe.matmul(ps_o[32 * r:32 * r + 32, :], v_aug[:, t, 4 * g + r, :], probs[:, (4 * q + r) % 8, :],
                                   start=(t == 0), stop=(t == 3))
                mm.then_inc(pv_done, 1)

            def post_at(b, s):
                if s == AT["den"]:
                    for g in range(NG):
                        pe.wait_ge(o_moved[g], 16 * 8 * (b + 1))
                    if past(b, 1):
                        pe.wait_ge(tail.sem, tail.after("z2", b - 1))
                    pe.matmul(ps_b[:], head_of[:], o_den[:], start=True, stop=True).then_inc(post.sem, 1)
                if s == AT["proj"]:
                    pe.wait_ge(post.sem, post.after("on", b))
                    pe.matmul(ps_b[:], w_o0[:], o_n[:], start=True, stop=True).then_inc(post.sem, 1)
                if s == AT["turn1"]:
                    pe.wait_ge(post.sem, post.after("r1", b))
                    turn(ps_b, r1[:]).then_inc(post.sem, 1)
                if s == AT["turn2"]:
                    pe.wait_ge(post.sem, post.after("z", b))
                    turn(ps_b, flat(z1)).then_inc(post.sem, 1)
                if s == AT["logits"]:
                    pe.wait_ge(post.sem, post.after("x1", b))
                    for t in range(T):
                        mm = pe.matmul(ps_b[:, 12 * t:12 * t + 12], x1T[:, t * P:(t + 1) * P], w_gate0[:], start=True, stop=True)
                    mm.then_inc(post.sem, 1)
                if s == AT["cturn"]:
                    pe.wait_ge(post.sem, post.after("p3", b))
                    for t in range(T):
                        mm = pe.transpose(ps_b[0:96, :].bitcast(BF16)[:, t * P:(t + 1) * P], cpb[:, t], identb[:])
                    mm.then_inc(post.sem, 1)

            def expert_c(b, e):
                if e == 0:
                    pe.wait_ge(post.sem, post.after("cT", b))
                    pe.wait_ge(w_late, 16 * 3)
                else:
                    pe.wait_ge(z_sb, (b * E0 + e) * 2)
                pe.matmul(ps_b[:], pick[:, e, :], cT[:], start=True, stop=True).then_inc(c_made, 1)

            def expert_z(b, k):
                e, c = k // 2, k % 2
                if c == 0:
                    pe.wait_ge(c_sb, b * E0 + e + 1)
                else:
                    pe.wait_ge(z_sb, b * 2 * E0 + k)
                pe.matmul(ps_b[:], w1[:, e, c * P:(c + 1) * P], x1T[:], start=True, stop=True).then_inc(z_made, 1)

            def expert_y(b, k):
                e, c = k // 2, k % 2
                pe.wait_ge(hc_made, b * 2 * E0 + k + 1)
                if k == 0 and past(b, 1):
                    pe.wait_ge(post.sem, post.after("r2", b - 1))
                pe.matmul(ps_y[:], w2[:, e, c, :], hc[:, k % 2, :], start=(k == 0), stop=False).then_inc(y_made, 1)

            def post_end(b):
                for j in range(3):
                    mm = pe.matmul(ps_y[:], b2_p[:, 0, j, :], cT[:], start=False, stop=(j == 2))
                mm.then_inc(post.sem, 1)

            def experts_at(b, s):
                for k in range(2 * E0):
                    if s == Y_AT[k]:
                        expert_y(b, k)
                for e in range(E0):
                    if s == C_AT[e]:
                        expert_c(b, e)
                for k in range(2 * E0):
                    if s == Z_AT[k]:
                        expert_z(b, k)
                if s == AT["y"]:
                    post_end(b)
                if s == AT["turn3"]:
                    pe.wait_ge(post.sem, post.after("r2", b))
                    turn(ps_b, r2[:]).then_inc(post.sem, 1)

            def tail_at(b, s):
                if s == AT["s_turn"]:
                    pe.wait_ge(tail.sem, tail.after("s_near", b))
                    if not isinstance(b, int) or b < NB - 2:
                        pe.wait_ge(ssm.sem, ssm.after("s", b + 2))
                    turn(s_bank_of(b), s_near[:]).then_inc(tail.sem, 1)

            def token_major(w):
                for t in range(T):
                    mm = pe.matmul(ps_p[:, t * P:(t + 1) * P], xT[:, t * P:(t + 1) * P], w, start=True, stop=True)
                return mm

            def pre1_at(b, u):
                if u == 2:
                    pe.wait_ge(pre1.sem, pre1.after("xn", b))
                    turn(ps_p, xn[:].rearrange("p t n -> p (t n)")).then_inc(pre1.sem, 1)
                if u == 3:
                    pe.wait_ge(pre1.sem, pre1.after("xT_kept", b))
                    if isinstance(b, int) and b == 0:
                        pe.wait_ge(w_attn1, 16 * 3)
                    for t in range(T):
                        mm = pe.matmul(ps_p[:, E1 * t:E1 * (t + 1)], xT[:, t * P:(t + 1) * P], w_gate1[:], start=True, stop=True)
                    mm.then_inc(gate1.sem, 1)
                if u == 4:
                    pe.wait_ge(gate1.sem, gate1.after("lsub", b))
                    pe.matmul(ps_p[:], w_qkv1[:, 0:P], xT[:], start=True, stop=True).then_inc(pre1.sem, 1)
                if u == 5:
                    pe.wait_ge(pre1.sem, pre1.after("q_sb", b))
                    token_major(w_qkv1[:, P:2 * P]).then_inc(pre1.sem, 1)
                if u == 6:
                    pe.wait_ge(pre1.sem, pre1.after("k_sb", b))
                    token_major(w_qkv1[:, 2 * P:3 * P]).then_inc(pre1.sem, 1)
                if u == 7:
                    pe.wait_ge(pre1.sem, pre1.after("v_sb", b))
                    if isinstance(b, int) and b == 0:
                        pe.wait_ge(ready1, 1)
                    for t in range(T):
                        mm = pe.matmul(ps_p[:, 0:P + 1], kT[:, t, :], vT[:, t, 0:P + 1], start=(t == 0), stop=(t == T - 1))
                    mm.then_inc(pre1.sem, 1)
                if u == 9:
                    pe.wait_ge(pre1.sem, pre1.after("ks_sb", b))
                    pe.matmul(ps_p[:], ksum[:], qT[:], start=True, stop=True).then_inc(pre1.sem, 1)
                if u == 12:
                    pe.wait_ge(pre1.sem, pre1.after("rd1", b))
                    pe.matmul(ps_p[:], kv[:], qT[:], start=True, stop=True).then_inc(pre1.sem, 1)
                if u == 13:
                    pe.wait_ge(pre1.sem, pre1.after("o", b))
                    pe.matmul(ps_p[:], w_proj1[:], o_n1[:], start=True, stop=True).then_inc(pre1.sem, 1)
                if u == 15:
                    pe.wait_ge(pre1.sem, pre1.after("s", b))
                    pe.wait_ge(gate1.sem, gate1.after("p3", b))
                    for t in range(T):
                        mm = pe.transpose(ps_p[0:96, :].bitcast(BF16)[:, t * P:(t + 1) * P], cpb1[:, t], identb[:])
                    mm.then_inc(gate1.sem, 1)

            def up_at(b, u):
                if u < E1:
                    wx, wg = fc1[:, u, 0:F1], fc1[:, u, F1:2 * F1]
                else:
                    wx, wg = sfc1[:, (u - E1) * P:(u - E1 + 1) * P], sfc1[:, (u - E1 + 2) * P:(u - E1 + 3) * P]
                if u == 0:
                    pe.wait_ge(gate1.sem, gate1.after("cT", b))
                if u == 0 and not past(b, 1):
                    pe.wait_ge(ready1, 2)
                if past(b, 1) or u >= 1:
                    pe.wait_ge(gelu_done, bank_before(b, u))
                pe.matmul(ps_g[half(b, u)][:], wg, xT_all[:, b, :], start=True, stop=True).then_inc(g1_made, 1)
                if past(b, 1) or u >= 1:
                    pe.wait_ge(act_x, bank_before(b, u))
                pe.matmul(ps_x[half(b, u)][:], wx, xT_all[:, b, :], start=True, stop=True).then_inc(x1_made, 1)
                if u < E1:
                    if past(b, 1) or u >= 1:
                        pe.wait_ge(a1_done, b * E1 + u)
                    pe.matmul(ps_c[:], pick[:, u, :], cT_all[:, b, :], start=True, stop=True).then_inc(c1_made, 1)

            def down_at(b, u):
                if u < E1:
                    pe.wait_ge(a1_done, b * E1 + u + 1)
                else:
                    pe.wait_ge(act_x, b * UNITS + u + 1)
                if u == 0:
                    if past(b, 1):
                        pe.wait_ge(post1.sem, post1.after("v", b - 1))
                w = fc2[:, u, :] if u < E1 else sfc2[:, u - E1, :]
                pe.matmul(ps_y1[:], w, hc1[:, u % 2, :], start=(u == 0), stop=False).then_inc(y1_made, 1)

            def biases(b):
                for j in range(3):
                    mm = pe.matmul(ps_y1[:], b2_p[:, 1, j, :], cT_all[:, b, :], start=False, stop=(j == 2))
                mm.then_inc(post1.sem, 1)

            def end1_at(b, u):
                if u == 2:
                    pe.wait_ge(post1.sem, post1.after("ws", b))
                    turn(ps_q, rden[:]).then_inc(post1.sem, 1)

            def unit1(b, u, full, previous, following):
                if full:
                    up_at(b, u)
                if full and u >= 1:
                    down_at(b, u - 1)
                if previous and u == 0:
                    down_at(b - 1, UNITS - 1)
                    biases(b - 1)
                if following:
                    pre1_at(b + 1, u)
                if previous:
                    end1_at(b - 1, u)

            def body1(b, full, previous, following):
                for u in range(UNITS):
                    unit1(b, u, full, previous, following)

            def layer1_at(pos):
                for u in range(UNITS):
                    if pos == PRE1_AT[u]:
                        pre1_at(0, u)
                    if pos == UNIT1_AT[u]:
                        unit1(0, u, True, False, True)

            def body(b, full, previous, before, following):
                alive = [(n, b - n) for n in range(3) if (full, previous, before)[n]]
                for s in range(SLOTS):
                    for n, batch in alive:
                        if LAG <= s + SLOTS * n < LAG + SLOTS:
                            transposed(batch, s + SLOTS * n - LAG)
                    if full:
                        scores(b, s)
                    for n, batch in alive:
                        q, rest = divmod(s + SLOTS * n - LAG - 6, 4)
                        if rest == 0 and 0 <= q < 16:
                            weighted(batch, q)
                    if following:
                        ssm_at(b + 1, s - SLOTS)
                    if following:
                        pre_at(b + 1, s - SLOTS)
                    for n, batch in alive[::-1]:
                        tail_at(batch, s + SLOTS * n)
                        post_at(batch, s + SLOTS * n)
                        experts_at(batch, s + SLOTS * n)
                    if isinstance(b, int) and b >= NB:
                        layer1_at(s + SLOTS * (b - NB + 1))
                    if full and s in (17, 33, 49):
                        shift_turn(b, s // 16 - 1)
                    if previous and s == 1:
                        shift_turn(b - 1, NG - 1)

            for s in range(-SLOTS, 0):
                pre_at(0, s)
                ssm_at(0, s)
            pe.wait_ge(setup, SETUP["b2"])
            pe.wait_ge(setup_pool, 3)
            body(0, True, False, False, True)
            body(1, True, True, False, True)
            with pe.Fori(2, NB - 1) as b:
                body(b, True, True, True, True)
            body(NB - 1, True, True, True, False)
            body(NB, False, True, True, False)
            body(NB + 1, False, False, True, False)
            with pe.Fori(1, NB - 1) as b:
                body1(b, True, True, True)
            body1(NB - 1, True, True, False)
            body1(NB, False, True, False)

        @block.scalar
        def _(act):
            act.wait_ge(w_early, 16 * 17)
            act.wait_ge(consts, 2)

            def ssm_at(b, s):
                for s0, step, made, i in ((AT["u0_sb"], "u0_sb", "u0", 0), (AT["u1_sb"], "u1_sb", "u1", 1)):
                    if s == s0:
                        act.wait_ge(ssm.sem, ssm.after(made, b))
                        nc.scalar.copy(up[:, i, 3:3 + S], ps_a[:]).then_inc(ssm.sem, 1)
                for s0, made, i in ((AT["th0"], "z0", 0), (AT["th1"], "z1", 1)):
                    if s == s0:
                        act.wait_ge(ssm.sem, ssm.after(made, b))
                        if isinstance(b, int) and b == 0 and i == 0:
                            act.wait_ge(setup, SETUP["dt_half"])
                        nc.scalar.activation(th[:], ps_a[:], ACT.Tanh, bias=col("dt_half", i), scale=0.5).then_inc(ssm.sem, 1)

            def pre_at(b, s):
                if s == AT["xT"]:
                    act.wait_ge(pre.sem, pre.after("turn", b))
                    nc.scalar.copy(xT[:], ps_a[:]).then_inc(pre.sem, 1)
                    nc.scalar.copy(xT_all[:, b, :], ps_a[:]).then_inc(pre.sem, 1)
                for s0, made, j in ((AT["q1"], "q", 0), (AT["k1"], "k", 1)):
                    if s == s0:
                        act.wait_ge(pre.sem, pre.after(made, b))
                        if j == 0 and past(b, 1):
                            act.wait_ge(stack_out, 16 * 9 * b)
                        nc.scalar.activation(qk_p[:, j, 0, :], ps_a[:], ACT.Identity, bias=col("bq", j)).then_inc(pre.sem, 1)
                if s == AT["v_sb"]:
                    act.wait_ge(pre.sem, pre.after("v", b))
                    if past(b, 1):
                        act.wait_ge(v_put, NG * b)
                    nc.scalar.copy(v_new[:].rearrange("p t n -> p (t n)"), ps_a[:]).then_inc(pre.sem, 1)

            def exps(b, v):
                act.wait_ge(t_made, b * SLOTS + v + 1)
                if past(b, 1) or v >= 8:
                    act.wait_ge(pv_done, b * 16 + v // 4 - 1)
                nc.scalar.activation(probs[:, v % 8, :], ps_t[v % 2][:], ACT.Exp, scale=SCALE).then_inc(exp_done, 1)

            def group_out(b, g):
                act.wait_ge(pv_done, b * 16 + 4 * g + 4)
                if past(b, 1) or g >= 1:
                    act.wait_ge(o_moved[g - 1], 16 * 8 * (b + (1 if g else 0)))
                nc.scalar.copy(oT[:], ps_o[:]).then_inc(ot_made, 1)

            def post_at(b, s):
                if s == AT["gexp"]:
                    act.wait_ge(post.sem, post.after("gsub", b))
                    nc.scalar.activation(g4[:, 1], g4[:, 0], ACT.Exp).then_inc(post.sem, 1)
                if s == AT["eexp"]:
                    act.wait_ge(post.sem, post.after("eabs", b))
                    nc.scalar.activation(g4[:, 5], g4[:, 4], ACT.Exp).then_inc(post.sem, 1)
                if s == AT["cT"]:
                    act.wait_ge(post.sem, post.after("cturn", b))
                    nc.scalar.copy(cT[:], ps_b[0:96, :].bitcast(BF16)[:, 0:S]).then_inc(post.sem, 1)

            def experts_at(b, s):
                for e in range(E0):
                    if s == C_AT[e]:
                        act.wait_ge(c_made, b * E0 + e + 1)
                        if e >= 2 or past(b, 1):
                            act.wait_ge(hc_made, (b * E0 + e - 1) * 2)
                        nc.scalar.copy(cbc[:, e % 2, :], ps_b[:]).then_inc(c_sb, 1)
                for k in range(2 * E0):
                    if s == Z_AT[k]:
                        act.wait_ge(z_made, b * 2 * E0 + k + 1)
                        if k >= 2 or past(b, 1):
                            act.wait_ge(hc_made, b * 2 * E0 + k - 1)
                        nc.scalar.activation(hz[:, k % 2, :], ps_b[:], ACT.Relu, bias=col("b1", k)).then_inc(z_sb, 1)

            def tail_at(b, s):
                if s == AT["tanh"]:
                    act.wait_ge(tail.sem, tail.after("bias", b))
                    nc.scalar.activation(tht[:], zg[:], ACT.Tanh, scale=0.5).then_inc(tail.sem, 1)
                if s == AT["s_near"]:
                    nc.scalar.copy(s_near[:], sT_all[:, b, :]).then_inc(tail.sem, 1)
                if s == AT["s_tok"]:
                    act.wait_ge(tail.sem, tail.after("s_turn", b))
                    nc.scalar.copy(s_tok[:], tiles(s_bank_of(b)[:])).then_inc(tail.sem, 1)

            def pre1_at(b, u):
                if u == 2:
                    act.wait_ge(pre1.sem, pre1.after("turn", b))
                    nc.scalar.copy(xT[:], ps_p[:]).then_inc(pre1.sem, 1)
                    nc.scalar.copy(xT_all[:, b, :], ps_p[:]).then_inc(pre1.sem, 1)
                if u == 6:
                    act.wait_ge(pre1.sem, pre1.after("v", b))
                    nc.scalar.copy(vT[:, :, 0:P], tiles(ps_p[:])).then_inc(pre1.sem, 1)
                if u == 15:
                    act.wait_ge(gate1.sem, gate1.after("cturn", b))
                    nc.scalar.copy(cT_all[:, b, :], ps_p[0:96, :].bitcast(BF16)[:, 0:S]).then_inc(gate1.sem, 1)

            def gelu_at(b, u):
                n = b * UNITS + u
                act.wait_ge(g1_made, n + 1)
                if past(b, 1) or u >= 2:
                    act.wait_ge(act_x, before(b, u))
                bias = col("fc1_b", 2 * u + 1) if u < E1 else col("sfc1_b", u - E1 + 2)
                nc.scalar.activation(hz1[:, u % 2, :], ps_g[half(b, u)][:], ACT.Gelu, bias=bias).then_inc(gelu_done, 1)

            def end1_at(b, u):
                if u == 0:
                    act.wait_ge(post1.sem, post1.after("y", b))
                    nc.scalar.activation(th[:], ps_y1[:], ACT.Tanh, bias=col("sb_half"), scale=0.5).then_inc(post1.sem, 1)

            def unit1(b, u, full, previous, following):
                if full:
                    gelu_at(b, u)
                if previous:
                    end1_at(b - 1, u)
                if following:
                    pre1_at(b + 1, u)

            def body1(b, full, previous, following):
                for u in range(UNITS):
                    unit1(b, u, full, previous, following)

            def layer1_at(pos):
                for u in range(UNITS):
                    if pos == PRE1_AT[u]:
                        pre1_at(0, u)
                    if pos == UNIT1_AT[u]:
                        unit1(0, u, True, False, True)

            def body(b, full, previous, before, following):
                alive = [(n, b - n) for n in range(3) if (full, previous, before)[n]]
                for s in range(SLOTS):
                    for n, batch in alive:
                        if LAG <= s + SLOTS * n < LAG + SLOTS:
                            exps(batch, s + SLOTS * n - LAG)
                    for n, batch in alive:
                        g, rest = divmod(s + SLOTS * n - LAG - 18, 16)
                        if rest == 0 and 0 <= g < NG:
                            group_out(batch, g)
                    if following:
                        ssm_at(b + 1, s - SLOTS)
                    if following:
                        pre_at(b + 1, s - SLOTS)
                    for n, batch in alive[::-1]:
                        tail_at(batch, s + SLOTS * n)
                        post_at(batch, s + SLOTS * n)
                        experts_at(batch, s + SLOTS * n)
                    if isinstance(b, int) and b >= NB:
                        layer1_at(s + SLOTS * (b - NB + 1))

            for s in range(-SLOTS, 0):
                pre_at(0, s)
                ssm_at(0, s)
            body(0, True, False, False, True)
            body(1, True, True, False, True)
            with act.Fori(2, NB - 1) as b:
                body(b, True, True, True, True)
            body(NB - 1, True, True, True, False)
            body(NB, False, True, True, False)
            body(NB + 1, False, False, True, False)
            with act.Fori(1, NB - 1) as b:
                body1(b, True, True, True)
            body1(NB - 1, True, True, False)
            body1(NB, False, True, False)

        @block.vector
        def _(dve):
            dve.wait_ge(w_early, 16 * 17)
            v = nc.vector
            v.tensor_scalar(vec[:, V["dt_half"]:V["dt_half"] + 2], vec[:, V["dt_b"]:V["dt_b"] + 2], -LN2, 0.5, ALU.add, ALU.mult).then_inc(setup, 1)
            v.tensor_scalar(w_out0[:], w_out0[:], 0.25 * GAIN, None, ALU.mult).then_inc(setup, 1)
            dve.wait_ge(setup_pe, 1)
            v.tensor_tensor(col("bo_all"), ps_b[:, 0:1], col("bo"), ALU.add).then_inc(setup, 1)
            v.tensor_scalar(col("sb_half"), col("sb"), 0.5, None, ALU.mult).then_inc(setup, 1)
            v.tensor_copy(b2_p[:, :, 0, :], b2_f[:]).then_inc(setup, 1)
            dve.wait_ge(setup, 5)
            v.tensor_tensor(b2_f[:], b2_f[:], b2_p[:, :, 0, :], ALU.subtract).then_inc(setup, 1)
            dve.wait_ge(setup, 6)
            v.tensor_copy(b2_p[:, :, 1, :], b2_f[:]).then_inc(setup, 1)
            dve.wait_ge(setup, 7)
            v.tensor_tensor(b2_p[:, :, 2, :], b2_f[:], b2_p[:, :, 1, :], ALU.subtract).then_inc(setup, 1)
            dve.wait_ge(setup, SETUP["b2"])
            dve.wait_ge(consts, 2)

            def moments(src, i, chain, names, b):
                for t in range(T):
                    ins = v.bn_stats(st6[:, i, t], src(t))
                ins.then_inc(chain.sem, 1)
                wait_apart(dve, (chain.sem, chain.after(names[0], b)))
                for t in range(T):
                    ins = v.bn_aggr(mv[:, i, t], st6[:, i, t])
                ins.then_inc(chain.sem, 1)

            def normal(dst, src, i):
                for t in range(T):
                    ins = v.tensor_scalar(dst[:, t], src(t), mv[:, i, t, 0:1], rstd[:, i, 1, t:t + 1], ALU.subtract, ALU.mult)
                return ins

            def ssm_at(b, s):
                for i, s0 in ((0, AT["c0"]), (1, AT["c1"])):
                    if s == s0:
                        dve.wait_ge(ssm.sem, ssm.after(("u1_sb", "c03")[i], b))
                        v.tensor_scalar(uc[:, i, :], up[:, i, 0:S], col("conv_w", 4 * i), col("conv_b", i), ALU.mult, ALU.add).then_inc(ssm.sem, 1)
                    for j in (1, 2, 3):
                        if s == s0 + j:
                            dve.wait_ge(ssm.sem, ssm.after(f"c{i}{j - 1}", b))
                            v.scalar_tensor_tensor(out=uc[:, i, :], in0=up[:, i, j:j + S], scalar=col("conv_w", 4 * i + j),
                                                   in1=uc[:, i, :], op0=ALU.mult, op1=ALU.add).then_inc(ssm.sem, 1)
                for i, s0 in ((0, AT["gu0"]), (1, AT["gu1"])):
                    if s == s0:
                        dve.wait_ge(ssm.sem, ssm.after(f"th{i}", b))
                        v.scalar_tensor_tensor(out=gu[:, i, :], in0=th[:], scalar=3.0, in1=uc[:, i, :], op0=ALU.add,
                                               op1=ALU.mult).then_inc(ssm.sem, 1)
                if s == AT["scan"]:
                    dve.wait_ge(ssm.sem, ssm.after("p", b))
                    v.tensor_tensor_scan(scan[:], decay[:], ps_a[:], 0.0, ALU.mult, ALU.add).then_inc(ssm.sem, 1)
                if s == AT["s"]:
                    dve.wait_ge(ssm.sem, ssm.after("res", b))
                    v.tensor_tensor(sT_all[:, b, :], ps_a[:], scan[:], ALU.add).then_inc(ssm.sem, 1)

            def pre_at(b, s):
                if s == AT["stats"]:
                    if isinstance(b, int) and b == 0:
                        dve.wait_ge(x_first, 16)
                    elif isinstance(b, int) and b == 1:
                        dve.wait_ge(x_rest, 16 * (NB - 1))
                    if past(b, 1):
                        dve.wait_ge(pre.sem, pre.after("k3", b - 1))
                    moments(lambda t: x_all[:, b, t], 0, pre, ["stats"], b)
                if s == AT["xn"]:
                    dve.wait_ge(pre.sem, pre.after("rstd", b))
                    normal(xn, lambda t: x_all[:, b, t], 0).then_inc(pre.sem, 1)
                for s0, made, j in ((AT["qr"], "q1", 0), (AT["kr"], "k1", 1)):
                    if s == s0:
                        dve.wait_ge(pre.sem, pre.after(made, b))
                        v.scalar_tensor_tensor(out=qk_r[:, j, :], in0=ps_a[:], scalar=col("bq", j), in1=qk_p[:, j, 0, :],
                                               op0=ALU.add, op1=ALU.subtract).then_inc(pre.sem, 1)

            def maxima(b, s):
                h, t = s // T, s % T
                dve.wait_ge(s_made, s_use(b, s_pos(s)) + 1)
                v.tensor_reduce(smax[:, h // 4, h % 4, t:t + 1], s_bank(b, s_pos(s))[:], AX, ALU.max).then_inc(s_read, 1)

            def shift_pieces(b, g):
                n = b * NG + g
                dve.wait_ge(s_read, s_use(b, s_pos(16 * g + 15)) + 1)
                v.tensor_scalar(smax_n[:], smax[:, g], -1.0, None, ALU.mult).then_inc(shift.sem, 1)
                dve.wait_ge(shift.sem, shift.after("neg", n))
                hi = smax_p[:].rearrange("p t a r -> p a r t")
                v.tensor_copy(hi[:, 0], smax_n[:]).then_inc(shift.sem, 1)
                dve.wait_ge(shift.sem, shift.after("hi", n))
                v.tensor_tensor(smax_r[:], smax_n[:], hi[:, 0], ALU.subtract).then_inc(shift.sem, 1)
                dve.wait_ge(shift.sem, shift.after("rest", n))
                v.tensor_copy(hi[:, 1], smax_r[:]).then_inc(shift.sem, 1)

            def shift_rows(b, g):
                at, pos = turn_use(b, g)
                n = b * NG + g
                dve.wait_ge(s_made, s_use(at, pos) + 1)
                if past(n, 1):
                    dve.wait_ge(shift_out, 16 * n)
                v.tensor_copy(smax_t[:], s_bank(at, pos)[0:8, :].bitcast(BF16)[:, 0:S]).then_inc(s_read, 1)

            def post_at(b, s):
                def step(name, ins):
                    ins.then_inc(post.sem, 1)
                    dve.wait_ge(post.sem, post.after(name, b))

                if AT["rd"] <= s < AT["rd"] + T:
                    if s == AT["rd"]:
                        dve.wait_ge(post.sem, post.after("den", b))
                    c = s - AT["rd"]
                    v.reciprocal(rden[:, c * P:(c + 1) * P], ps_b[:, c * P:(c + 1) * P]).then_inc(post.sem, 1)
                if s == AT["rd"] + T - 1:
                    dve.wait_ge(post.sem, post.after("rd3", b))
                    v.tensor_tensor(o_n[:], o_num[:], rden[:], ALU.mult).then_inc(post.sem, 1)
                if s == AT["r1"]:
                    dve.wait_ge(post.sem, post.after("proj", b))
                    v.scalar_tensor_tensor(out=r1[:], in0=ps_b[:], scalar=col("bo_all"), in1=xT_all[:, b, :], op0=ALU.add,
                                           op1=ALU.add).then_inc(post.sem, 1)
                if s == AT["stats1"]:
                    dve.wait_ge(post.sem, post.after("turn1", b))
                    moments(lambda t: ps_b[:, t * P:(t + 1) * P], 1, post, ["stats1"], b)
                if s == AT["z"]:
                    dve.wait_ge(post.sem, post.after("rstd1", b))
                    normal(z1, lambda t: ps_b[:, t * P:(t + 1) * P], 1).then_inc(post.sem, 1)
                if s == AT["x1"]:
                    dve.wait_ge(post.sem, post.after("turn2", b))
                    v.tensor_scalar(x1T[:], ps_b[:], col("ln1_g"), col("ln1_b"), ALU.mult, ALU.add).then_inc(post.sem, 1)
                if s == AT["group"]:
                    dve.wait_ge(post.sem, post.after("logits", b))
                    step("lg", v.tensor_tensor(gl[:], ps_b[:, 0:48].rearrange("p (t e) -> p t e", t=T),
                                               rows[:, 2:3, 0:12].broadcast_to([P, T, 12]), ALU.add))
                    gr = gl[:, :, 0:4]
                    step("gmax", v.tensor_reduce(gm[:, 0, :], gr, AX, ALU.max))
                    v.tensor_tensor(g4[:, 0], gr, gm[:, 0, :].unsqueeze(2).broadcast_to([P, T, 4]), ALU.subtract).then_inc(post.sem, 1)
                if s == AT["expert"]:
                    dve.wait_ge(post.sem, post.after("gexp", b))
                    step("gsum", v.tensor_reduce(gm[:, 1, :], g4[:, 1], AX, ALU.add))
                    step("gties", v.scalar_tensor_tensor(out=g4[:, 2], in0=g4[:, 0], scalar=0.0,
                                                         in1=rows[:, 3:4, 0:4].broadcast_to([P, T, 4]), op0=ALU.is_equal, op1=ALU.mult))
                    step("gtop", v.tensor_reduce(gm[:, 2, :], g4[:, 2], AX, ALU.max))
                    step("ghot", v.tensor_tensor(g4[:, 3], g4[:, 2], gm[:, 2, :].unsqueeze(2).broadcast_to([P, T, 4]), ALU.is_equal))
                    ex = gl[:, :, 4:12].rearrange("p t (g e) -> p t g e", e=2)
                    step("ediff", v.tensor_tensor(g4[:, 6], ex[:, :, :, 0], ex[:, :, :, 1], ALU.subtract))
                    v.scalar_tensor_tensor(out=g4[:, 4], in0=g4[:, 6], scalar=-1.0, in1=g4[:, 6], op0=ALU.mult,
                                           op1=ALU.min).then_inc(post.sem, 1)
                if s == AT["comb"]:
                    dve.wait_ge(post.sem, post.after("eexp", b))
                    step("eden", v.scalar_tensor_tensor(out=g4[:, 4], in0=g4[:, 5], scalar=1.0,
                                                        in1=gm[:, 1, :].unsqueeze(2).broadcast_to([P, T, 4]), op0=ALU.add, op1=ALU.mult))
                    step("erec", v.reciprocal(g4[:, 5], g4[:, 4]))
                    step("chot", v.tensor_tensor(g4[:, 7], g4[:, 5], g4[:, 3], ALU.mult))
                    step("first", v.scalar_tensor_tensor(out=comb[:, :, :, 0], in0=g4[:, 6], scalar=0.0, in1=g4[:, 7],
                                                         op0=ALU.is_ge, op1=ALU.mult))
                    step("second", v.tensor_tensor(comb[:, :, :, 1], g4[:, 7], comb[:, :, :, 0], ALU.subtract))
                    pieces(comb[:].rearrange("p t g e -> p t (g e)"), E0, step)
                if s == AT["r2"]:
                    dve.wait_ge(post.sem, post.after("y", b))
                    v.tensor_tensor(r2[:], ps_y[:], x1T[:], ALU.add).then_inc(post.sem, 1)
                if s == AT["stats2"]:
                    dve.wait_ge(post.sem, post.after("turn3", b))
                    moments(lambda t: ps_b[:, t * P:(t + 1) * P], 2, post, ["stats2"], b)

            def pieces(c, n, step):
                step("p1", v.tensor_copy(cpb[:, :, 0:n], c))
                step("s1", v.tensor_tensor(cpf[:, 0, :, 0:n], c, cpb[:, :, 0:n], ALU.subtract))
                step("p2", v.tensor_copy(cpb[:, :, 32:32 + n], cpf[:, 0, :, 0:n]))
                step("s2", v.tensor_tensor(cpf[:, 1, :, 0:n], cpf[:, 0, :, 0:n], cpb[:, :, 32:32 + n], ALU.subtract))
                step("p3", v.tensor_copy(cpb[:, :, 64:64 + n], cpf[:, 1, :, 0:n]))

            def tail_at(b, s):
                if s == AT["z2"]:
                    dve.wait_ge(post.sem, post.after("rstd2", b))
                    normal(zt, lambda t: ps_b[:, t * P:(t + 1) * P], 2).then_inc(tail.sem, 1)
                if s == AT["w"]:
                    dve.wait_ge(tail.sem, tail.after("tanh", b))
                    v.scalar_tensor_tensor(out=zt[:], in0=tht[:], scalar=1.0, in1=zg[:], op0=ALU.add, op1=ALU.mult).then_inc(tail.sem, 1)
                if s == AT["ws"]:
                    dve.wait_ge(tail.sem, tail.after("w", b))
                    v.tensor_tensor(zg[:], zt[:], s_tok[:], ALU.mult).then_inc(tail.sem, 1)
                    dve.wait_ge(tail.sem, tail.after("ws", b))
                    v.scalar_tensor_tensor(out=x_all[:, b], in0=zg[:], scalar=0.5, in1=x_all[:, b], op0=ALU.mult,
                                           op1=ALU.add).then_inc(tail.sem, 1)

            def pre1_at(b, u):
                def step(name, ins, chain=gate1, own=False):
                    ins.then_inc(chain.sem, 1)
                    if own:
                        wait_apart(dve, (chain.sem, chain.after(name, b)))
                    else:
                        dve.wait_ge(chain.sem, chain.after(name, b))

                if u == 0:
                    if past(b, 1):
                        dve.wait_ge(gate1.sem, gate1.after("cT", b - 1))
                    for t in range(T):
                        ins = v.bn_stats(st6[:, 3, t], x_all[:, b, t])
                    step("stats", ins, pre1, own=True)
                    for t in range(T):
                        ins = v.bn_aggr(mv[:, 3, t], st6[:, 3, t])
                    ins.then_inc(pre1.sem, 1)
                if u == 1:
                    dve.wait_ge(pre1.sem, pre1.after("rstd", b))
                    for t in range(T):
                        ins = v.tensor_scalar(xn[:, t], x_all[:, b, t], mv[:, 3, t, 0:1], rstd[:, 3, 1, t:t + 1], ALU.subtract, ALU.mult)
                    ins.then_inc(pre1.sem, 1)
                if u == 3:
                    dve.wait_ge(gate1.sem, gate1.after("logits", b))
                    lp = ps_p[:, 0:T * E1].rearrange("p (t e) -> p t e", t=T)
                    step("lmax", v.tensor_reduce(gm1[:, 0, :], lp, AX, ALU.max))
                    v.tensor_tensor(lg[:, 0, :, 0:E1], lp, spread(gm1[:, 0, :]), ALU.subtract).then_inc(gate1.sem, 1)
                if u == 4:
                    dve.wait_ge(pre1.sem, pre1.after("q", b))
                    v.tensor_scalar(qT[:], ps_p[:], 0.0, None, ALU.max).then_inc(pre1.sem, 1)
                if u == 5:
                    dve.wait_ge(pre1.sem, pre1.after("k", b))
                    v.tensor_scalar(kT[:], tiles(ps_p[:]), 0.0, None, ALU.max).then_inc(pre1.sem, 1)
                if u == 7:
                    dve.wait_ge(pre1.sem, pre1.after("kv", b))
                    v.tensor_tensor(kv[:], ps_p[:, 0:P], block1[:], ALU.mult).then_inc(pre1.sem, 1)
                    v.tensor_scalar(ksum[:], block1[:], ps_p[:, P:P + 1], None, ALU.mult).then_inc(pre1.sem, 1)
                if u == 8:
                    dve.wait_ge(gate1.sem, gate1.after("lexp", b))
                    step("lsum", v.tensor_reduce(gm1[:, 1, :], lg[:, 1, :, 0:E1], AX, ALU.add))
                    step("lrec", v.reciprocal(gm1[:, 2, :], gm1[:, 1, :]))
                    step("score", v.tensor_tensor(lg[:, 2, :, 0:E1], lg[:, 1, :, 0:E1], spread(gm1[:, 2, :]), ALU.mult), own=True)
                    for t in range(T):
                        ins = v.max(m8[:, t], lg[:, 2, t])
                    ins.then_inc(gate1.sem, 1)
                if u == 9:
                    dve.wait_ge(pre1.sem, pre1.after("dn", b))
                    v.tensor_scalar(o_num1[:], ps_p[:], 1e-15, None, ALU.add).then_inc(pre1.sem, 1)
                    dve.wait_ge(gate1.sem, gate1.after("top8", b))
                    step("top3", v.tensor_copy(m8v[:, :, 0:3], m8[:, :, 0:3]), own=True)
                    for t in range(T):
                        ins = v.match_replace(lg[:, 3, t], m8v[:, t], lg[:, 2, t], -2.0)
                    ins.then_inc(gate1.sem, 1)
                if u in (10, 11):
                    c = (u - 10) * 256
                    if u == 10:
                        dve.wait_ge(pre1.sem, pre1.after("dn_eps", b))
                    v.reciprocal(r21[:, c:c + 256], o_num1[:, c:c + 256]).then_inc(pre1.sem, 1)
                if u == 12:
                    dve.wait_ge(pre1.sem, pre1.after("num", b))
                    v.tensor_tensor(o_n1[:], ps_p[:], r21[:], ALU.mult).then_inc(pre1.sem, 1)
                    dve.wait_ge(gate1.sem, gate1.after("rep", b))
                    step("mask", v.tensor_tensor(lg[:, 4, :, 0:E1], lg[:, 3, :, 0:E1], lg[:, 2, :, 0:E1], ALU.not_equal))
                    step("tw", v.tensor_tensor(lg[:, 5, :, 0:E1], lg[:, 4, :, 0:E1], lg[:, 2, :, 0:E1], ALU.mult))
                    step("tsum", v.tensor_reduce(gm1[:, 3, :], lg[:, 5, :, 0:E1], AX, ALU.add))
                    v.tensor_scalar(gm1[:, 4, :], gm1[:, 3, :], 1e-20, None, ALU.add).then_inc(gate1.sem, 1)
                if u == 13:
                    dve.wait_ge(pre1.sem, pre1.after("pr", b))
                    v.tensor_scalar(sT_all[:, b, :], ps_p[:], col("bp"), None, ALU.add).then_inc(pre1.sem, 1)
                    dve.wait_ge(gate1.sem, gate1.after("tsum_eps", b))
                    step("trec", v.reciprocal(gm1[:, 5, :], gm1[:, 4, :]))
                    if not past(b, 1):
                        dve.wait_ge(ready1, 1)
                    step("comb", v.tensor_tensor(lg[:, 4, :, 0:E1], lg[:, 5, :, 0:E1], spread(gm1[:, 5, :]), ALU.mult))
                    v.tensor_copy(cpb1[:, :, 0:E1], lg[:, 4, :, 0:E1]).then_inc(gate1.sem, 1)
                if u == 14:
                    dve.wait_ge(gate1.sem, gate1.after("p1", b))
                    step("s1", v.tensor_tensor(cpf1[:, 0, :, 0:E1], lg[:, 4, :, 0:E1], cpb1[:, :, 0:E1], ALU.subtract))
                    step("p2", v.tensor_copy(cpb1[:, :, 32:32 + E1], cpf1[:, 0, :, 0:E1]))
                    step("s2", v.tensor_tensor(cpf1[:, 1, :, 0:E1], cpf1[:, 0, :, 0:E1], cpb1[:, :, 32:32 + E1], ALU.subtract))
                    v.tensor_copy(cpb1[:, :, 64:64 + E1], cpf1[:, 1, :, 0:E1]).then_inc(gate1.sem, 1)

            def spread(x):
                return x.unsqueeze(2).broadcast_to([P, T, E1])

            def unit_at(b, u):
                n = b * UNITS + u
                dve.wait_ge(gelu_done, n + 1)
                dve.wait_ge(x1_made, n + 1)
                if past(b, 1) or u >= 2:
                    dve.wait_ge(y1_made, before(b, u))
                bias = col("fc1_b", 2 * u) if u < E1 else col("sfc1_b", u - E1)
                mid = cbc1 if u < E1 else hc1
                ins = v.scalar_tensor_tensor(out=mid[:, u % 2, :], in0=ps_x[half(b, u)][:], scalar=bias,
                                             in1=hz1[:, u % 2, :], op0=ALU.add, op1=ALU.mult)
                ins.then_inc(act_x, 1)
                if u < E1:
                    dve.wait_ge(act_x, n + 1)
                    dve.wait_ge(c1_made, b * E1 + u + 1)
                    v.tensor_tensor(hc1[:, u % 2, :], cbc1[:, u % 2, :], ps_c[:], ALU.mult).then_inc(a1_done, 1)

            def end1_at(b, u):
                if u == 0:
                    dve.wait_ge(post1.sem, post1.after("th", b))
                    v.tensor_scalar(scan[:], ps_y1[:], col("sb"), None, ALU.add).then_inc(post1.sem, 1)
                    dve.wait_ge(post1.sem, post1.after("v", b))
                    v.scalar_tensor_tensor(out=s_near[:], in0=th[:], scalar=1.0, in1=scan[:], op0=ALU.add, op1=ALU.mult).then_inc(post1.sem, 1)
                    dve.wait_ge(post1.sem, post1.after("w", b))
                    v.tensor_tensor(rden[:], s_near[:], sT_all[:, b, :], ALU.mult).then_inc(post1.sem, 1)
                if u == 2:
                    dve.wait_ge(post1.sem, post1.after("turn", b))
                    v.scalar_tensor_tensor(out=x_all[:, b], in0=tiles(ps_q[:]), scalar=0.5, in1=x_all[:, b], op0=ALU.mult,
                                           op1=ALU.add).then_inc(post1.sem, 1)

            def unit1(b, u, full, previous, following):
                if full:
                    unit_at(b, u)
                if previous:
                    end1_at(b - 1, u)
                if following:
                    pre1_at(b + 1, u)

            def body1(b, full, previous, following):
                for u in range(UNITS):
                    unit1(b, u, full, previous, following)

            def layer1_at(pos):
                for u in range(UNITS):
                    if pos == PRE1_AT[u]:
                        pre1_at(0, u)
                    if pos == UNIT1_AT[u]:
                        unit1(0, u, True, False, True)

            def body(b, full, previous, before, following):
                alive = [(n, b - n) for n in range(3) if (full, previous, before)[n]]
                for s in range(SLOTS):
                    if full:
                        maxima(b, s)
                    if full and s % 16 == 15:
                        shift_pieces(b, s // 16)
                    if full and s in (17, 33, 49):
                        shift_rows(b, s // 16 - 1)
                    if previous and s == 1:
                        shift_rows(b - 1, NG - 1)
                    if following:
                        ssm_at(b + 1, s - SLOTS)
                    if following:
                        pre_at(b + 1, s - SLOTS)
                    for n, batch in alive[::-1]:
                        tail_at(batch, s + SLOTS * n)
                        post_at(batch, s + SLOTS * n)
                    if isinstance(b, int) and b >= NB:
                        layer1_at(s + SLOTS * (b - NB + 1))

            for s in range(-SLOTS, 0):
                pre_at(0, s)
                ssm_at(0, s)
            body(0, True, False, False, True)
            body(1, True, True, False, True)
            with dve.Fori(2, NB - 1) as b:
                body(b, True, True, True, True)
            body(NB - 1, True, True, True, False)
            body(NB, False, True, True, False)
            body(NB + 1, False, False, True, False)
            with dve.Fori(1, NB - 1) as b:
                body1(b, True, True, True)
            body1(NB - 1, True, True, False)
            body1(NB, False, True, False)

        @block.gpsimd
        def _(pool):
            p = nc.gpsimd
            p.memset(b2_f[:], 0.0).then_inc(consts, 1)
            p.memset(mhalf[:], -0.5)
            p.memset(decay[:], DECAY)
            p.memset(up[:, :, 0:3], 0.0)
            p.memset(cpb[:], 0.0)
            p.memset(ebase[:], 2.718281828459045)
            p.memset(lg[:], -1.0)
            p.memset(m8v[:], -1.0)
            p.memset(v_aug[:], 0.0).then_inc(setup_pool, 1)
            pool.wait_ge(setup_pool, 1)
            p.memset(ks[32:KROWS + 2], 1.0).then_inc(setup_pool, 1)
            pool.wait_ge(setup_pool, 2)
            p.memset(v_aug[:, :, :, HD:HD + 1], 1.0).then_inc(consts, 1)

            def rsqrt(i, chain, first, names, b):
                wait_apart(pool, (chain.sem, chain.after(first, b)))
                p.tensor_scalar(rstd[:, i, 0, :], mv[:, i, :, 1], EPS, None, ALU.add).then_inc(chain.sem, 1)
                pool.wait_ge(chain.sem, chain.after(names[0], b))
                p.tensor_tensor(rstd[:, i, 1, :], rstd[:, i, 0, :], mhalf[:], ALU.pow).then_inc(chain.sem, 1)

            def pre_at(b, s):
                if s == AT["rstd"]:
                    rsqrt(0, pre, "moments", ["eps"], b)
                if s == AT["q2"]:
                    wait_apart(pool, (pre.sem, pre.after("v_sb", b)))
                    for j, name in ((0, "q2"), (1, "k2")):
                        p.tensor_scalar(qk_p[:, j, 1, :], qk_r[:, j, :], 1.0, None, ALU.mult).then_inc(pre.sem, 1)
                        pool.wait_ge(pre.sem, pre.after(name, b))
                        p.tensor_tensor(qk_p[:, j, 2, :], qk_r[:, j, :], qk_p[:, j, 1, :], ALU.subtract).then_inc(pre.sem, 1)

            def values(b, g):
                spent = [(pv_done, 16 * (b - 1) + 4 * g + 4)] if past(b, 1) else []
                wait_apart(pool, (pre.sem, pre.after("v_sb", b)), *spent)
                p.tensor_scalar(v_aug[:, :, 4 * g:4 * g + 4, 0:HD],
                                v_new[:, :, 32 * g:32 * g + 32].rearrange("p t (h d) -> p t h d", d=HD),
                                1.0, None, ALU.mult).then_inc(v_put, 1)

            def post_at(b, s):
                if s == AT["rstd1"]:
                    rsqrt(1, post, "moments1", ["eps1"], b)
                if s == AT["rstd2"]:
                    rsqrt(2, post, "moments2", ["eps2"], b)

            def tail_at(b, s):
                if s == AT["gain"]:
                    pool.wait_ge(tail.sem, tail.after("z2", b))
                    p.tensor_tensor(zg[:], zt[:], rows[:, 0:1, :].broadcast_to([P, T, P]), ALU.mult).then_inc(tail.sem, 1)
                    pool.wait_ge(tail.sem, tail.after("gain", b))
                    p.tensor_tensor(zg[:], zg[:], rows[:, 1:2, :].broadcast_to([P, T, P]), ALU.add).then_inc(tail.sem, 1)

            def experts_at(b, s):
                for k in range(2 * E0):
                    if s == Z_AT[k]:
                        pool.wait_ge(z_sb, b * 2 * E0 + k + 1)
                        if past(b, 1) or k >= 2:
                            pool.wait_ge(y_made, b * 2 * E0 + k - 1)
                        p.tensor_tensor(hc[:, k % 2, :], hz[:, k % 2, :], cbc[:, k // 2 % 2, :], ALU.mult).then_inc(hc_made, 1)

            def pre1_at(b, u):
                if u == 0:
                    wait_apart(pool, (pre1.sem, pre1.after("moments", b)))
                    p.tensor_scalar(rstd[:, 3, 0, :], mv[:, 3, :, 1], EPS, None, ALU.add).then_inc(pre1.sem, 1)
                    pool.wait_ge(pre1.sem, pre1.after("eps", b))
                    p.tensor_tensor(rstd[:, 3, 1, :], rstd[:, 3, 0, :], mhalf[:], ALU.pow).then_inc(pre1.sem, 1)
                if u == 3:
                    pool.wait_ge(gate1.sem, gate1.after("lsub", b))
                    p.tensor_tensor(lg[:, 1, :, 0:E1], ebase[:, :, 0:E1], lg[:, 0, :, 0:E1], ALU.pow).then_inc(gate1.sem, 1)

            def unit1(b, u, following):
                if following:
                    pre1_at(b + 1, u)

            def body1(b, following):
                for u in range(UNITS):
                    unit1(b, u, following)

            def layer1_at(pos):
                if pos == AT["ones1"]:
                    pool.wait_ge(pv_done, 16 * NB)
                    p.memset(cpb1[:], 0.0)
                    p.memset(z_tok[:, :, P:P + 1], 1.0).then_inc(ready1, 1)
                if pos == AT["scale1"]:
                    pool.wait_ge(w_last, 16 * 4)
                    p.tensor_tensor(fc2, fc2, vec[:, V["mult"]:V["mult"] + E1].unsqueeze(2).broadcast_to([P, E1, P]), ALU.mult)
                    p.tensor_tensor(sfc2, sfc2, vec[:, V["s_mult"]:V["s_mult"] + 2].unsqueeze(2).broadcast_to([P, 2, P]), ALU.mult)\
                        .then_inc(ready1, 1)
                for u in range(UNITS):
                    if pos == PRE1_AT[u]:
                        pre1_at(0, u)
                    if pos == UNIT1_AT[u]:
                        unit1(0, u, True)

            def body(b, full, previous, before, following):
                alive = [(n, b - n) for n in range(3) if (full, previous, before)[n]]
                for s in range(SLOTS):
                    for n, batch in alive[::-1]:
                        tail_at(batch, s + SLOTS * n)
                        post_at(batch, s + SLOTS * n)
                        experts_at(batch, s + SLOTS * n)
                    if isinstance(b, int) and b >= NB:
                        layer1_at(s + SLOTS * (b - NB + 1))
                    for g in range(NG):
                        if full and s == AT[f"values{g}"]:
                            values(b, g)
                        if following and s - SLOTS == AT[f"values{g}"]:
                            values(b + 1, g)
                    if following:
                        pre_at(b + 1, s - SLOTS)

            pool.wait_ge(w_early, 16 * 17)
            for s in range(-SLOTS, 0):
                pre_at(0, s)
            values(0, 0)
            values(0, 1)
            p.tensor_scalar(identb[:], ident[:], 1.0, None, ALU.mult)
            p.tensor_scalar(pick[:], pick_f[:].unsqueeze(2).broadcast_to([96, 16, P]), 1.0, None, ALU.mult).then_inc(setup_pool, 1)
            body(0, True, False, False, True)
            body(1, True, True, False, True)
            with pool.Fori(2, NB - 1) as b:
                body(b, True, True, True, True)
            body(NB - 1, True, True, True, False)
            body(NB, False, True, True, False)
            body(NB + 1, False, False, True, False)
            with pool.Fori(1, NB - 1) as b:
                body1(b, True)
        program.__exit__(None, None, None)


def lay_out(i):
    import numpy as np

    def c(a):
        return np.ascontiguousarray(a)

    def chunks(a, n):
        return a.reshape(n, P, -1).transpose(1, 0, 2)

    a = {k: np.asarray(v) for k, v in i.items()}
    f = np.float32
    vec = np.zeros((P, 96), f)
    given = {
        "conv_w": chunks(a["L0_attn_conv_w"].reshape(256, 4), 2).reshape(P, 8),
        "conv_b": chunks(a["L0_attn_conv_b"][:, None], 2).reshape(P, 2),
        "dt_b": chunks(a["L0_attn_dt_proj_b"][:, None], 2).reshape(P, 2),
        "bq": a["L0_ffn_in_proj_b"].reshape(3, P).T[:, 0:2],
        "bv": a["L0_ffn_in_proj_b"].reshape(3, P).T[:, 2:3],
        "bo": a["L0_ffn_out_proj_b"][:, None],
        "ln1_g": a["L0_ffn_ln1_g"][:, None],
        "ln1_b": a["L0_ffn_ln1_b"][:, None],
        "b1": a["L0_ffn_b1"].reshape(16, P).T,
        "bp": a["L1_attn_b_proj"][:, None],
        "fc1_b": a["L1_ffn_fc1_b"].reshape(30, P).T,
        "mult": a["L1_ffn_geglu_mult"].T,
        "sfc1_b": a["L1_ffn_s_fc1_b"].reshape(4, P).T,
        "s_mult": a["L1_ffn_s_geglu_mult"].reshape(2, P).T,
        "sb": a["L1_ffn_s_fc2_b"][:, None],
    }
    n = 0
    for name, w in VEC:
        if name in given:
            vec[:, n:n + w] = given[name]
        n += w
    rows = np.zeros((1, 4, P), f)
    rows[0, 0], rows[0, 1] = a["L0_ffn_ln2_g"], a["L0_ffn_ln2_b"]
    rows[0, 2, 0:12] = np.concatenate([a["L0_ffn_b_group"], a["L0_ffn_b_expert"].reshape(8)])
    rows[0, 3, 0:4] = (4, 3, 2, 1)
    eye = np.eye(P, dtype=f)
    return {
        "x": c(a["L0_attn_x"]),
        "ident": eye,
        "vec": vec,
        "rows": rows.reshape(1, 4 * P).reshape(4 * P),
        "head_of": c(np.repeat(np.eye(NH, dtype=f), HD, axis=1)),
        "pick": c(np.tile(np.eye(32, 16, dtype=f), (3, 1))),
        "block1": c(np.kron(np.eye(4, dtype=f), np.ones((32, 32), f))),
        "w_in0": c(a["L0_attn_in_proj_w"].T),
        "w_dt": c(chunks(a["L0_attn_dt_proj_w"].T, 2)),
        "w_out0": c(chunks(a["L0_attn_out_proj_w"].T, 2)),
        "w_qkv0": c(a["L0_ffn_in_proj_w"].T),
        "w_o0": c(a["L0_ffn_out_proj_w"].T),
        "w_gate0": c(np.concatenate([a["L0_ffn_w_group"], a["L0_ffn_w_expert"].transpose(1, 0, 2).reshape(P, 8)], axis=1)),
        "w1": c(a["L0_ffn_w1"].transpose(1, 0, 2)),
        "w2": c(a["L0_ffn_w2"].reshape(E0, 2, P, P).transpose(2, 0, 1, 3)),
        "b2": c(a["L0_ffn_b2"]),
        "w_qkv1": c(a["L1_attn_W_qkv"].T),
        "w_proj1": c(a["L1_attn_W_proj"].T),
        "w_gate1": c(a["L1_ffn_gate_w"].T),
        "fc1": c(a["L1_ffn_fc1_w"].transpose(2, 0, 1)),
        "fc2": c(a["L1_ffn_fc2_w"].transpose(2, 0, 1)),
        "fc2_b": c(a["L1_ffn_fc2_b"]),
        "sfc1": c(a["L1_ffn_s_fc1_w"].T),
        "sfc2": c(chunks(a["L1_ffn_s_fc2_w"].T, 2)),
    }


def kernel(**inputs):
    import concourse.bacc as bacc
    from concourse.bass_utils import run_bass_kernel_spmd

    nc = bacc.Bacc("TRN2", target_bir_lowering=False, num_devices=1)
    arrays = lay_out(inputs)
    d = {n: nc.dram_tensor("in_" + n, a.shape, mybir.dt.from_np(a.dtype), kind="ExternalInput").ap() for n, a in arrays.items()}
    out = nc.dram_tensor("out", [NB, S, P], F32, kind="ExternalOutput").ap()
    build(nc, d, out)
    return run_bass_kernel_spmd(nc, [{"in_" + n: a for n, a in arrays.items()}], core_ids=[0]).results[0]["out"]
```

```python
from contextlib import ExitStack

import concourse.bass as bass
from concourse import mybir

F32 = mybir.dt.float32
BF16 = mybir.dt.bfloat16
ALU = mybir.AluOpType
ACT = mybir.ActivationFunctionType
AX = mybir.AxisListType.X

P = 128
NB = 8
S = 512
T = S // P
NH, HD = 16, 8
NG = NH // 4
PIECES = 6
KROWS = PIECES * HD
SLOTS = 64
LAG = 24
E0, F0 = 8, 256
E1, F1 = 15, 128
EPS = 1e-5
LN2 = 0.6931471805599453
SCALE = float(HD) ** -0.5
DECAY, GAIN = 0.9, 0.1


class Steps:

    def __init__(self, sem, names):
        self.sem, self.n, self.at = sem, len(names), {n: i for i, n in enumerate(names)}

    def after(self, name, b):
        return b * self.n + self.at[name] + 1


def past(b, least):
    return not isinstance(b, int) or b >= least


SSM = ["u0", "u0_sb", "u1", "u1_sb", "c00", "c01", "c02", "c03", "c10", "c11", "c12", "c13",
       "z0", "th0", "gu0", "z1", "th1", "gu1", "p", "scan", "res", "s"]
PRE = ["stats", "moments", "eps", "rstd", "xn", "turn", "xT", "xT_kept", "q", "q1", "qr", "k", "k1", "kr",
       "v", "v_sb", "q2", "q3", "k2", "k3"]
SHIFT = ["neg", "hi", "rest", "lo"]
POST = ["rd", "den", "on", "proj", "r1", "turn1", "stats1", "moments1", "eps1", "rstd1", "z",
        "turn2", "x1", "logits", "lg", "gmax", "gsub", "gexp", "gsum", "gties", "gtop", "ghot", "ediff", "eabs",
        "eexp", "eden", "erec", "chot", "first", "second", "p1", "s1", "p2", "s2", "p3", "cturn", "cT",
        "y", "r2", "turn3", "stats2", "moments2", "eps2", "rstd2"]
AT = {"u0": -28, "u0_sb": -27, "u1": -26, "u1_sb": -26, "c0": -25, "c1": -20, "z0": -15, "th0": -15, "gu0": -14,
      "z1": -12, "th1": -11, "gu1": -9, "p": -7, "scan": -6, "res": -4, "s": -3, "stats": -52, "rstd": -50, "xn": -46,
      "turn": -40, "xT": -39, "q": -37, "q1": -34, "qr": -35, "k": -33, "k1": -33, "kr": -33, "v": -31, "v_sb": -29,
      "q2": -28, "stacks_out": -24, "stacks_in0": -18, "stacks_in1": -8, "stacks_in2": 8, "stacks_in3": 24,
      "values0": -19, "values1": -4, "values2": 9, "values3": 25, "out0": 44, "out1": 59, "out2": 78, "out3": 90,
      "rd": 96, "den": 99, "on": 100, "proj": 101, "r1": 102, "turn1": 102, "stats1": 104, "rstd1": 106, "z": 107,
      "turn2": 110, "x1": 111, "logits": 112, "group": 114, "gexp": 116, "expert": 116, "eexp": 117, "comb": 119,
      "cturn": 121, "cT": 122, "experts": 124, "s_near": 132, "s_turn": 134, "s_tok": 135, "y": 150, "r2": 152,
      "turn3": 153, "stats2": 154, "rstd2": 155, "z2": 156, "gain": 159, "tanh": 162, "w": 163, "ws": 163,
      "load1": 76, "load1_end": 92, "ones1": 8, "scale1": 92}
LATE0 = AT["turn"] + SLOTS - AT["s"]
C_AT = [AT["experts"] + 3 * e for e in range(E0)]
Z_AT = [C_AT[k // 2] + 1 + k % 2 for k in range(2 * E0)]
Y_AT = [z + 3 for z in Z_AT]
UNITS = E1 + 2
PRE1_AT = [12 + 3 * u for u in range(UNITS)]
UNIT1_AT = [94 + 2 * n for n in range(2 * UNITS)]
SETUP = {"dt_half": 1, "w_out0": 2, "bo_all": 3, "sb_half": 4, "b2": 8}
VEC = [("conv_w", 8), ("conv_b", 2), ("dt_b", 2), ("dt_half", 2), ("bq", 2), ("bv", 1), ("bo", 1), ("bo_all", 1), ("ln1_g", 1),
       ("ln1_b", 1), ("b1", 16), ("bp", 1), ("fc1_b", 30), ("mult", 15), ("sfc1_b", 4), ("s_mult", 2), ("sb", 1), ("sb_half", 1)]
TAIL = ["s_near", "s_turn", "s_tok", "z2", "gain", "bias", "tanh", "half", "w", "ws", "x_new"]
PRE1 = ["stats", "moments", "eps", "rstd", "xn", "turn", "xT", "xT_kept", "q", "q_sb", "k", "k_sb", "v", "v_sb",
        "kv", "kv_sb", "ks_sb", "dn", "dn_eps", "rd0", "rd1", "num", "o", "pr", "s"]
GATE1 = ["logits", "lmax", "lsub", "lexp", "lsum", "lrec", "score", "top8", "top3", "rep", "mask", "tw", "tsum", "tsum_eps",
         "trec", "comb", "p1", "s1", "p2", "s2", "p3", "cturn", "cT"]
POST1 = ["th", "v", "w", "ws", "turn", "out"]


def build(nc, d, out):
    with ExitStack() as ctx:
        def sb(name, shape, dt=F32):
            return ctx.enter_context(nc.sbuf_tensor(name, shape, dt))

        def sem(name):
            return ctx.enter_context(nc.semaphore(name))

        def tiles(ap):
            return ap.rearrange("p (t n) -> p t n", t=T)

        w_in0 = sb("w_in0", [P, 384])
        w_dt = sb("w_dt", [P, 2, 256])
        w_out0 = sb("w_out0", [P, 2, P])
        w_qkv0 = sb("w_qkv0", [P, 384])
        w_o0 = sb("w_o0", [P, P])
        w_gate0 = sb("w_gate0", [P, 12])
        w1 = sb("w1", [P, E0, F0])
        w2 = sb("w2", [P, E0, 2, P])
        ident = sb("ident", [P, P])
        identb = sb("identb", [P, P], BF16)
        head_of = sb("head_of", [NH, P])
        pick = sb("pick", [96, 16, P], BF16)
        pick_f = sb("pick_f", [96, 16])
        block1 = sb("block1", [P, P])
        vec = sb("vec", [P, 96])
        rows = sb("rows", [P, 3, P])
        b2_f = sb("b2_f", [96, 2, P])
        b2_p = sb("b2_p", [96, 2, 3, P], BF16)
        decay = sb("decay", [P, S])
        mhalf = sb("mhalf", [P, T])
        ebase = sb("ebase", [P, T, 20])
        x_all = sb("x_all", [P, NB, T, P])
        xT_all = sb("xT_all", [P, NB, S])
        sT_all = sb("sT_all", [P, NB, S])
        st6 = sb("st6", [P, 4, T, 6])
        mv = sb("mv", [P, 4, T, 2])
        rstd = sb("rstd", [P, 4, 2, T])
        xn = sb("xn", [P, T, P])
        xT = sb("xT", [P, S])
        up = sb("up", [P, 2, S + 3])
        uc = sb("uc", [P, 2, S])
        th = sb("th", [P, S])
        gu = up[:, :, 3:3 + S]
        scan = sb("scan", [P, S])
        s_tok_f = sb("s_tok", [P, S])
        qk_r = sb("qk_r", [P, 2, S])
        qk_p = sb("qk_p", [P, 2, 3, S], BF16)
        qs_all = sb("qs_all", [P, NH, S], BF16)
        ks_all = sb("ks_all", [P, NH, S], BF16)
        qs = qs_all[0:KROWS + 2]
        ks = ks_all[0:KROWS + 2]
        v_new = sb("v_new", [P, T, P])
        v_aug = sb("v_aug", [P, T, NH, 32])
        smax = sb("smax", [P, NG, 4, T])
        smax_n = sb("smax_n", [P, 4, T])
        smax_r = sb("smax_r", [P, 4, T])
        smax_p = sb("smax_p", [P, T, 2, 4], BF16)
        smax_t = sb("smax_t", [8, S], BF16)
        probs = sb("probs", [P, 8, S])
        oT = sb("oT", [P, S])
        o_num = sb("o_num", [P, S])
        o_den = sb("o_den", [NH, S])
        o_den_c = sb("o_den_c", [P, S // 8])
        rden = sb("rden", [P, S])
        o_n = sb("o_n", [P, S])
        r1 = sb("r1", [P, S])
        z1 = sb("z1", [P, T, P])
        x1T = sb("x1T", [P, S])
        gl = sb("gl", [P, T, 12])
        gm = sb("gm", [P, 8, T])
        g4 = sb("g4", [P, 8, T, 4])
        comb = sb("comb", [P, T, 4, 2])
        cpf = sb("cpf", [P, 2, T, 16])
        cpb = sb("cpb", [P, T, 96], BF16)
        cT = sb("cT", [96, S], BF16)
        cbc = sb("cbc", [P, 2, S])
        hz = sb("hz", [P, 2, S])
        hc = sb("hc", [P, 2, S])
        r2 = sb("r2", [P, S])
        zt, zg, tht = tiles(rden[:]), z1, tiles(r2[:])
        s_tok = tiles(s_tok_f[:])
        s_near = z1[:].rearrange("p t n -> p (t n)")
        cT1 = qk_p[0:96, 0, 0, :]
        qs_f = qs_all[:].rearrange("p h n -> p (h n)").bitcast(F32)
        ks_f = ks_all[:].rearrange("p h n -> p (h n)").bitcast(F32)
        fc1 = qs_f[:, 0:E1 * 2 * F1].rearrange("p (e f) -> p e f", e=E1)
        fc2 = ks_f[:, 0:E1 * P].rearrange("p (e f) -> p e f", e=E1)
        n = E1 * P
        sfc1, sfc2 = ks_f[:, n:n + 512], ks_f[:, n + 512:n + 768].rearrange("p (c f) -> p c f", c=2)
        w_dt_f = w_dt[:].rearrange("p c n -> p (c n)")
        w_qkv1, w_proj1, w_gate1 = w_dt_f[:, 0:3 * P], w_dt_f[:, 3 * P:4 * P], w_in0[:, 0:E1]
        z_tok = up[:].rearrange("p a n -> p (a n)")[:, 0:T * (P + 4)].rearrange("p (t n) -> p t n", t=T)
        kv_bd, ks_bd = th[:, 0:P], th[:, P:2 * P]
        lg = sb("lg", [P, 6, T, 20])
        gm1 = sb("gm1", [P, 8, T])
        cpf1 = sb("cpf1", [P, 2, T, 16])
        cpb1 = w_in0[:, P:2 * P + 64].bitcast(BF16).rearrange("p (t n) -> p t n", t=T)
        kT, vT, qT, kv, ksum = tiles(qk_r[:, 1]), z_tok, qk_r[:, 0], kv_bd, ks_bd
        o_num1, r21, o_n1, cbc1 = uc[:, 0], uc[:, 1], scan, probs[:, 0:2]
        s_gated, ws1 = probs[:, 2], probs[:, 3]
        v_flat = v_aug[:].rearrange("p t h d -> p (t h d)")
        hz1, hc1 = (v_flat[:, k * 2 * S:(k + 1) * 2 * S].rearrange("p (a n) -> p a n", a=2) for k in range(2))
        m8 = sb("m8", [P, T, 8])
        m8v = sb("m8v", [P, T, 8])

        bank = [ctx.enter_context(nc.psum_tensor(f"bank{i}", [P, S], F32)) for i in range(8)]
        ps_s = bank[0:2]
        ps_t = bank[2:4]
        ps_o, ps_a, ps_b, ps_y = bank[4:8]
        ps_g, ps_x = bank[0:2], [bank[2], bank[7]]
        ps_c, ps_y1, ps_p, ps_q = bank[4], bank[3], bank[5], bank[6]

        stack = [nc.dram_tensor(f"stack_{n}", [P, PIECES, S], BF16, kind="Internal").ap() for n in "qk"]
        shift_d = nc.dram_tensor("shift_rows", [2, 4, S], BF16, kind="Internal").ap()

        x_first = sem("x_first")
        x_rest = sem("x_rest")
        w_first = sem("w_first")
        w_early = sem("w_early")
        w_late = sem("w_late")
        w_attn1 = sem("w_attn1")
        w_up1 = sem("w_up1")
        w_up1_end = sem("w_up1_end")
        w_down1 = sem("w_down1")
        consts = sem("consts")
        setup = sem("setup")
        setup_pe = sem("setup_pe")
        setup_pool = sem("setup_pool")
        ready1 = sem("ready1")
        ssm, pre, post, tail = (Steps(sem(n), s) for n, s in (("ssm", SSM), ("pre", PRE), ("post", POST), ("tail", TAIL)))
        pre1, gate1, post1 = Steps(sem("pre1"), PRE1), Steps(sem("gate1"), GATE1), Steps(sem("post1"), POST1)
        shift = Steps(sem("shift"), SHIFT)
        s_made = sem("s_made")
        s_read = sem("s_read")
        t_made = sem("t_made")
        exp_done = sem("exp_done")
        pv_done = sem("pv_done")
        ot_made = sem("ot_made")
        o_moved = [sem(f"o_moved{g}") for g in range(NG)]
        den_in = sem("den_in")
        v_put = sem("v_put")
        stack_out = sem("stack_out")
        stack_in = [sem(f"stack_in{g}") for g in range(NG)]
        shift_out = sem("shift_out")
        shift_in = sem("shift_in")
        c_made = sem("c_made")
        c_sb = sem("c_sb")
        z_made = sem("z_made")
        z_sb = sem("z_sb")
        hc_made = sem("hc_made")
        y_made = sem("y_made")
        g1_made = sem("g1_made")
        x1_made = sem("x1_made")
        c1_made = sem("c1_made")
        gelu_done = sem("gelu_done")
        act_x = sem("act_x")
        a1_done = sem("a1_done")
        y1_made = sem("y1_made")
        out_sem = sem("out_sem")

        def wait_apart(eng, *waits):
            waits = [(sem, value if isinstance(value, int) else eng.to_reg(value)) for sem, value in waits]
            if not all(isinstance(value, int) for _, value in waits):
                eng.wait_ge(consts, 2)
            for sem, value in waits:
                eng.wait_ge(sem, value)

        V = {}
        n = 0
        for name, w in VEC:
            V[name] = n
            n += w

        def col(name, i=0):
            return vec[:, V[name] + i:V[name] + i + 1]

        def before(b, u):
            return b * UNITS + (u - 1 if u else 0)

        def s_turned_bank(b):
            return bank[1] if isinstance(b, int) and b == NB - 1 else ps_a

        def c_bank(b, e):
            return ps_b if e < 2 or (isinstance(b, int) and b == NB - 1) else ps_a

        def half(b, u):
            return u % 2 if past(b, 2) else 0

        def bank_before(b, u):
            return before(b, u) if past(b, 2) else b * UNITS + u

        def out_bank(b):
            return bank[1] if isinstance(b, int) and b == 0 else ps_q

        def s_use(b, pos):
            if isinstance(b, int) and b == 0:
                return pos if pos < 2 else pos - 1
            if isinstance(b, int) and b == NB:
                return b * (SLOTS + NG) - 1
            return b * (SLOTS + NG) + pos - 1

        def s_pos(s):
            return (s // 16) * 17 + s % 16 + (1 if s % 16 >= 2 else 0)

        def turn_use(b, g):
            return (b, 17 * g + 19) if g < NG - 1 else (b + 1, 2)

        def s_bank(b, pos):
            return ps_s[s_use(b, pos) % 2] if isinstance(b, int) else ps_s[(pos + 1) % 2]

        program = nc.Block()
        block = program.__enter__()

        @block.sync
        def _(sp):
            xr = d["x"].rearrange("b (t p) d -> b p t d", p=P)
            sp.dma_start(x_all[:, 0], xr[0]).then_inc(x_first, 16)
            for dst, src in ((ident[:], d["ident"]), (w_qkv0[:], d["w_qkv0"]), (vec[:], d["vec"])):
                sp.dma_start(dst, src).then_inc(w_first, 16)
            early = [
                     (w_in0[:], d["w_in0"]), (w_dt[:], d["w_dt"]), (w_out0[:], d["w_out0"]), (w_o0[:], d["w_o0"]),
                     (w_gate0[:], d["w_gate0"]), (head_of[:], d["head_of"]), (pick_f[:], d["pick"]),
                     (rows[:], d["rows"].partition_broadcast(P))]
            for dst, src in early:
                sp.dma_start(dst, src).then_inc(w_early, 16)
            sp.wait_ge(consts, 1)
            for k in range(3):
                sp.dma_start(b2_f[32 * k:32 * k + E0, 0, :], d["b2"]).then_inc(w_early, 16)
                sp.dma_start(b2_f[32 * k:32 * k + E1, 1, :], d["fc2_b"]).then_inc(w_early, 16)
            for b in range(1, NB):
                sp.dma_start(x_all[:, b], xr[b]).then_inc(x_rest, 16)
            late = [(w1[:], d["w1"]), (w2[:], d["w2"]), (block1[:], d["block1"])]
            for dst, src in late:
                sp.dma_start(dst, src).then_inc(w_late, 16)

            def stacks_out(b):
                wait_apart(sp, (pre.sem, pre.after("k3", b)), *[(stack_in[g], 32 * b) for g in range(NG) if past(b, 1)])
                for j, parts in ((0, ((0, 0, 3), (3, 0, 2), (5, 0, 1))), (1, ((0, 0, 0), (1, 0, 0), (2, 0, 0), (3, 1, 0), (4, 1, 0), (5, 2, 0)))):
                    for to, first, n in parts:
                        n = n or 1
                        sp.dma_start(stack[j][:, to:to + n, :], qk_p[:, j, first:first + n, :]).then_inc(stack_out, 16)

            def stacks_in(b, g):
                wait_apart(sp, (stack_out, 16 * 9 * (b + 1)), *[(t_made, SLOTS * (b - 1) + 16 * (g + 1))] * past(b, 1))
                for j, dst in ((0, qs), (1, ks)):
                    src = stack[j].rearrange("(h d) s n -> h (d s) n", h=NH)[4 * g:4 * g + 4].rearrange("h r n -> r h n")
                    sp.dma_start(dst[0:KROWS, 4 * g:4 * g + 4, :], src).then_inc(stack_in[g], 16)

            def shift_rows(b, g):
                n = b * NG + g
                sp.wait_ge(s_read, s_use(*turn_use(b, g)) + 1)
                if past(n, 1):
                    sp.wait_ge(shift_in, 16 * n)
                sp.dma_start(shift_d.rearrange("a r n -> (a r) n"), smax_t[:]).then_inc(shift_out, 16)
                wait_apart(sp, (shift_out, 16 * (n + 1)))
                sp.dma_start(qs[KROWS:KROWS + 2, 4 * g:4 * g + 4, :], shift_d).then_inc(shift_in, 16)

            def outputs(b, g):
                wait_apart(sp, (ot_made, b * NG + g + 1), *[(post.sem, post.after("on", b - 1))] * past(b, 1))
                for r in range(4):
                    sp.dma_start(o_num[32 * g + 8 * r:32 * g + 8 * r + 8, :], oT[32 * r:32 * r + 8, :]).then_inc(o_moved[g], 16)
                    sp.dma_start(o_den_c[8 * (4 * g + r):8 * (4 * g + r + 1), :], oT[32 * r + 8:32 * r + 9, :]).then_inc(o_moved[g], 16)

            def body(b, full, previous, following):
                for s in range(SLOTS):
                    if previous and s == 2:
                        shift_rows(b - 1, NG - 1)
                    if full and s in (18, 34, 50):
                        shift_rows(b, s // 16 - 1)
                    for g in range(NG):
                        for alive, n, pos in ((previous, b - 1, s + SLOTS), (full, b, s)):
                            if alive and pos == AT[f"out{g}"]:
                                outputs(n, g)
                        for alive, n, pos in ((full, b, s), (following, b + 1, s - SLOTS)):
                            if alive and pos == AT[f"stacks_in{g}"]:
                                stacks_in(n, g)
                    if isinstance(b, int) and b == NB and s + SLOTS == AT["load1"]:
                        sp.wait_ge(t_made, SLOTS * NB - 16)
                        sp.dma_start(fc1[:, 0:12], d["fc1"][:, 0:12]).then_inc(w_up1, 16)
                        sp.dma_start(sfc1, d["sfc1"]).then_inc(w_up1, 16)
                        for dst, src in ((fc2, "fc2"), (sfc2, "sfc2")):
                            sp.dma_start(dst, d[src]).then_inc(w_down1, 16)
                    if isinstance(b, int) and b == NB and s + SLOTS == AT["load1_end"]:
                        sp.wait_ge(t_made, SLOTS * NB)
                        sp.dma_start(fc1[:, 12:E1], d["fc1"][:, 12:E1]).then_inc(w_up1_end, 16)
                    if isinstance(b, int) and b == NB - 1 and s == 0:
                        sp.wait_ge(ssm.sem, ssm.after("s", b))
                        for dst, src in ((w_qkv1, "w_qkv1"), (w_proj1, "w_proj1"), (w_gate1, "w_gate1")):
                            sp.dma_start(dst, d[src]).then_inc(w_attn1, 16)
                    if previous and s + SLOTS == AT["rd"]:
                        sp.wait_ge(post.sem, post.after("rd", b - 1))
                        sp.dma_start(o_den[:], o_den_c[:]).then_inc(den_in, 16)
                    if following and s - SLOTS == AT["stacks_out"]:
                        stacks_out(b + 1)

            sp.wait_ge(consts, 2)
            stacks_out(0)
            stacks_in(0, 0)
            stacks_in(0, 1)
            body(0, True, False, True)
            body(1, True, True, True)
            with sp.Fori(2, NB - 1) as b:
                body(b, True, True, True)
            body(NB - 1, True, True, False)
            body(NB, False, True, False)
            with sp.Fori(0, NB) as b:
                sp.wait_ge(post1.sem, post1.after("out", b))
                sp.dma_start(out.rearrange("b (t p) d -> b p t d", p=P)[b], x_all[:, b]).then_inc(out_sem, 16)
            sp.wait_ge(out_sem, 16 * NB)

        @block.tensor
        def _(pe):
            pe.wait_ge(w_first, 16 * 3)

            def turn(dst, src):
                for t in range(T):
                    mm = pe.transpose(dst[:, t * P:(t + 1) * P], src[:, t * P:(t + 1) * P], ident[:])
                return mm

            def flat(ap):
                return ap.rearrange("p t n -> p (t n)")

            def ssm_at(b, s):
                if s == AT["u0"]:
                    if past(b, 1):
                        pe.wait_ge(ssm.sem, ssm.after("s", b - 1))
                    pe.wait_ge(pre.sem, pre.after("v_sb", b))
                    pe.matmul(ps_a[:], w_in0[:, 0:P], xT[:], start=True, stop=True).then_inc(ssm.sem, 1)
                if s == AT["u1"]:
                    pe.wait_ge(ssm.sem, ssm.after("u0_sb", b))
                    pe.matmul(ps_a[:], w_in0[:, P:2 * P], xT[:], start=True, stop=True).then_inc(ssm.sem, 1)
                if s in (AT["z0"], AT["z1"]):
                    j = 0 if s == AT["z0"] else 1
                    pe.wait_ge(ssm.sem, ssm.after(("c13", "gu0")[j], b))
                    pe.matmul(ps_a[:], w_dt[:, 0, j * P:(j + 1) * P], uc[:, 0, :], start=True, stop=False)
                    pe.matmul(ps_a[:], w_dt[:, 1, j * P:(j + 1) * P], uc[:, 1, :], start=False, stop=True).then_inc(ssm.sem, 1)
                if s == AT["p"]:
                    pe.wait_ge(ssm.sem, ssm.after("gu1", b))
                    pe.matmul(ps_a[:], w_out0[:, 0, :], gu[:, 0, :], start=True, stop=False)
                    pe.matmul(ps_a[:], w_out0[:, 1, :], gu[:, 1, :], start=False, stop=True).then_inc(ssm.sem, 1)
                if s == AT["res"]:
                    pe.wait_ge(ssm.sem, ssm.after("scan", b))
                    pe.matmul(ps_a[:], w_in0[:, 2 * P:3 * P], xT[:], start=True, stop=True).then_inc(ssm.sem, 1)

            def pre_at(b, s):
                if s == AT["turn"]:
                    pe.wait_ge(pre.sem, pre.after("xn", b))
                    if past(b, 1):
                        pe.wait_ge(ssm.sem, ssm.after("s", b - 1))
                    if past(b, 3):
                        pe.wait_ge(tail.sem, tail.after("s_tok", b - 3))
                        pe.wait_ge(c_sb, (b - 2) * E0)
                    turn(ps_a, flat(xn)).then_inc(pre.sem, 1)
                if s == AT["q"]:
                    pe.wait_ge(pre.sem, pre.after("xT_kept", b))
                    pe.matmul(ps_a[:], w_qkv0[:, 0:P], xT[:], start=True, stop=True).then_inc(pre.sem, 1)
                if s == AT["k"]:
                    pe.wait_ge(pre.sem, pre.after("qr", b))
                    pe.matmul(ps_a[:], w_qkv0[:, P:2 * P], xT[:], start=True, stop=True).then_inc(pre.sem, 1)
                if s == AT["v"]:
                    pe.wait_ge(pre.sem, pre.after("kr", b))
                    for t in range(T):
                        mm = pe.matmul(ps_a[:, t * P:(t + 1) * P], xT[:, t * P:(t + 1) * P], w_qkv0[:, 2 * P:3 * P], start=True, stop=True)
                    mm.then_inc(pre.sem, 1)

            def scores(b, s):
                h, t = s // T, s % T
                u = s_use(b, s_pos(s))
                if s % 16 == 0:
                    pe.wait_ge(stack_in[s // 16], 32 * (b + 1))
                if past(b, 1) or u >= 2:
                    pe.wait_ge(s_read, u - 1)
                pe.matmul(s_bank(b, s_pos(s))[:], qs[0:KROWS, h, t * P:(t + 1) * P], ks[0:KROWS, h, :],
                          start=True, stop=True).then_inc(s_made, 1)

            def shift_turn(b, g):
                at, pos = turn_use(b, g)
                u = s_use(at, pos)
                pe.wait_ge(shift.sem, shift.after("lo", b * NG + g))
                pe.wait_ge(s_read, u - 1)
                for t in range(T):
                    mm = pe.transpose(s_bank(at, pos)[0:8, :].bitcast(BF16)[:, t * P:(t + 1) * P],
                                      smax_p[:, t].rearrange("p a r -> p (a r)"), identb[:])
                mm.then_inc(s_made, 1)

            def transposed(b, v):
                g, t, r = v // 16, v % 16 // 4, v % 4
                h = 4 * g + r
                if v % 16 == 0:
                    pe.wait_ge(shift_in, 16 * (b * NG + g + 1))
                if past(b, 1) or v >= 2:
                    pe.wait_ge(exp_done, b * SLOTS + v - 1)
                pe.matmul(ps_t[v % 2][:], ks[:, h, t * P:(t + 1) * P], qs[:, h, :], start=True, stop=True).then_inc(t_made, 1)

            def weighted(b, q):
                g, t = q // 4, q % 4
                pe.wait_ge(exp_done, b * SLOTS + 4 * q + 4)
                if t == 0:
                    pe.wait_ge(v_put, b * NG + g + 1)
                    if past(b, 1) or g >= 1:
                        pe.wait_ge(ot_made, b * NG + g)
                for r in range(4):
                    mm = pe.matmul(ps_o[32 * r:32 * r + 32, :], v_aug[:, t, 4 * g + r, :], probs[:, (4 * q + r) % 8, :],
                                   start=(t == 0), stop=(t == 3))
                mm.then_inc(pv_done, 1)

            def post_at(b, s):
                if s == AT["den"]:
                    pe.wait_ge(den_in, 16 * (b + 1))
                    if past(b, 1):
                        pe.wait_ge(tail.sem, tail.after("z2", b - 1))
                    pe.matmul(ps_b[:], head_of[:], o_den[:], start=True, stop=True).then_inc(post.sem, 1)
                if s == AT["proj"]:
                    pe.wait_ge(post.sem, post.after("on", b))
                    pe.matmul(ps_b[:], w_o0[:], o_n[:], start=True, stop=True).then_inc(post.sem, 1)
                if s == AT["turn1"]:
                    pe.wait_ge(post.sem, post.after("r1", b))
                    turn(ps_b, r1[:]).then_inc(post.sem, 1)
                if s == AT["turn2"]:
                    pe.wait_ge(post.sem, post.after("z", b))
                    turn(ps_b, flat(z1)).then_inc(post.sem, 1)
                if s == AT["logits"]:
                    pe.wait_ge(post.sem, post.after("x1", b))
                    for t in range(T):
                        mm = pe.matmul(ps_b[:, 12 * t:12 * t + 12], x1T[:, t * P:(t + 1) * P], w_gate0[:], start=True, stop=True)
                    mm.then_inc(post.sem, 1)
                if s == AT["cturn"]:
                    pe.wait_ge(post.sem, post.after("p3", b))
                    for t in range(T):
                        mm = pe.transpose(ps_b[0:96, :].bitcast(BF16)[:, t * P:(t + 1) * P], cpb[:, t], identb[:])
                    mm.then_inc(post.sem, 1)

            def ssm_left(b):
                if isinstance(b, int) and b == NB - 2:
                    pe.wait_ge(gate1.sem, gate1.after("cT", 0))
                else:
                    pe.wait_ge(ssm.sem, ssm.after("s", b + 2))

            def expert_c(b, e):
                if e == 0:
                    pe.wait_ge(post.sem, post.after("cT", b))
                    pe.wait_ge(w_late, 16 * 3)
                elif c_bank(b, e) is ps_b:
                    pe.wait_ge(z_sb, (b * E0 + e) * 2)
                else:
                    if e == 2:
                        ssm_left(b)
                    pe.wait_ge(c_sb, b * E0 + e)
                    if C_AT[e] >= AT["s_tok"] > C_AT[e - 1]:
                        pe.wait_ge(tail.sem, tail.after("s_tok", b))
                pe.matmul(c_bank(b, e)[:], pick[:, e, :], cT[:], start=True, stop=True).then_inc(c_made, 1)

            def expert_z(b, k):
                e, c = k // 2, k % 2
                if k == 0 and past(b, 1):
                    pe.wait_ge(post.sem, post.after("r2", b - 1))
                if c == 0 and c_bank(b, e) is ps_b:
                    pe.wait_ge(c_sb, b * E0 + e + 1)
                else:
                    pe.wait_ge(z_sb, b * 2 * E0 + k)
                pe.matmul(ps_b[:], w1[:, e, c * P:(c + 1) * P], x1T[:], start=True, stop=True).then_inc(z_made, 1)

            def expert_y(b, k):
                e, c = k // 2, k % 2
                pe.wait_ge(hc_made, b * 2 * E0 + k + 1)
                pe.matmul(ps_y[:], w2[:, e, c, :], hc[:, k % 2, :], start=(k == 0), stop=False).then_inc(y_made, 1)

            def post_end(b):
                for j in range(3):
                    mm = pe.matmul(ps_y[:], b2_p[:, 0, j, :], cT[:], start=False, stop=(j == 2))
                mm.then_inc(post.sem, 1)

            def experts_at(b, s):
                for k in range(2 * E0):
                    if s == Y_AT[k]:
                        expert_y(b, k)
                for e in range(E0):
                    if s == C_AT[e]:
                        expert_c(b, e)
                for k in range(2 * E0):
                    if s == Z_AT[k]:
                        expert_z(b, k)
                if s == AT["y"]:
                    post_end(b)
                if s == AT["turn3"]:
                    pe.wait_ge(post.sem, post.after("r2", b))
                    turn(ps_b, r2[:]).then_inc(post.sem, 1)

            def tail_at(b, s):
                if s == AT["s_turn"]:
                    pe.wait_ge(tail.sem, tail.after("s_near", b))
                    if isinstance(b, int) and b == NB - 1:
                        pe.wait_ge(post1.sem, post1.after("out", 0))
                    else:
                        ssm_left(b)
                        pe.wait_ge(c_sb, b * E0 + sum(at < AT["s_turn"] for at in C_AT))
                    turn(s_turned_bank(b), s_near[:]).then_inc(tail.sem, 1)

            def token_major(w):
                for t in range(T):
                    mm = pe.matmul(ps_p[:, t * P:(t + 1) * P], xT[:, t * P:(t + 1) * P], w, start=True, stop=True)
                return mm

            def pre1_at(b, u):
                if u == 2:
                    pe.wait_ge(pre1.sem, pre1.after("xn", b))
                    if isinstance(b, int) and b < 2:
                        pe.wait_ge(ssm.sem, ssm.after("s", NB - 1))
                        pe.wait_ge(tail.sem, tail.after("s_tok", NB - 3 + b))
                        pe.wait_ge(c_sb, (NB - 2 + b) * E0)
                    turn(ps_p, xn[:].rearrange("p t n -> p (t n)")).then_inc(pre1.sem, 1)
                if u == 3:
                    pe.wait_ge(pre1.sem, pre1.after("xT_kept", b))
                    if isinstance(b, int) and b == 0:
                        pe.wait_ge(w_attn1, 16 * 3)
                    for t in range(T):
                        mm = pe.matmul(ps_p[:, E1 * t:E1 * (t + 1)], xT[:, t * P:(t + 1) * P], w_gate1[:], start=True, stop=True)
                    mm.then_inc(gate1.sem, 1)
                if u == 4:
                    pe.wait_ge(gate1.sem, gate1.after("lsub", b))
                    pe.matmul(ps_p[:], w_qkv1[:, 0:P], xT[:], start=True, stop=True).then_inc(pre1.sem, 1)
                if u == 5:
                    pe.wait_ge(pre1.sem, pre1.after("q_sb", b))
                    token_major(w_qkv1[:, P:2 * P]).then_inc(pre1.sem, 1)
                if u == 6:
                    pe.wait_ge(pre1.sem, pre1.after("k_sb", b))
                    token_major(w_qkv1[:, 2 * P:3 * P]).then_inc(pre1.sem, 1)
                if u == 7:
                    pe.wait_ge(pre1.sem, pre1.after("v_sb", b))
                    if isinstance(b, int) and b == 0:
                        pe.wait_ge(ready1, 1)
                    for t in range(T):
                        mm = pe.matmul(ps_p[:, 0:P + 1], kT[:, t, :], vT[:, t, 0:P + 1], start=(t == 0), stop=(t == T - 1))
                    mm.then_inc(pre1.sem, 1)
                if u == 9:
                    pe.wait_ge(pre1.sem, pre1.after("ks_sb", b))
                    pe.matmul(ps_p[:], ksum[:], qT[:], start=True, stop=True).then_inc(pre1.sem, 1)
                if u == 12:
                    pe.wait_ge(pre1.sem, pre1.after("rd1", b))
                    pe.matmul(ps_p[:], kv[:], qT[:], start=True, stop=True).then_inc(pre1.sem, 1)
                if u == 13:
                    pe.wait_ge(pre1.sem, pre1.after("o", b))
                    pe.matmul(ps_p[:], w_proj1[:], o_n1[:], start=True, stop=True).then_inc(pre1.sem, 1)
                if u == 15:
                    pe.wait_ge(pre1.sem, pre1.after("s", b))
                    pe.wait_ge(gate1.sem, gate1.after("p3", b))
                    for t in range(T):
                        mm = pe.transpose(ps_p[0:96, :].bitcast(BF16)[:, t * P:(t + 1) * P], cpb1[:, t], identb[:])
                    mm.then_inc(gate1.sem, 1)

            def up_at(b, u):
                if u < E1:
                    wx, wg = fc1[:, u, 0:F1], fc1[:, u, F1:2 * F1]
                else:
                    wx, wg = sfc1[:, (u - E1) * P:(u - E1 + 1) * P], sfc1[:, (u - E1 + 2) * P:(u - E1 + 3) * P]
                if u == 0:
                    pe.wait_ge(gate1.sem, gate1.after("cT", b))
                if u == 0 and not past(b, 1):
                    pe.wait_ge(w_up1, 16 * 2)
                    pe.wait_ge(ot_made, NG * NB)
                if u == 12 and not past(b, 1):
                    pe.wait_ge(w_up1_end, 16)
                if past(b, 1) or u >= 1:
                    pe.wait_ge(gelu_done, bank_before(b, u))
                pe.matmul(ps_g[half(b, u)][:], wg, xT_all[:, b, :], start=True, stop=True).then_inc(g1_made, 1)
                if past(b, 1) or u >= 1:
                    pe.wait_ge(act_x, bank_before(b, u))
                pe.matmul(ps_x[half(b, u)][:], wx, xT_all[:, b, :], start=True, stop=True).then_inc(x1_made, 1)
                if u < E1:
                    if past(b, 1) or u >= 1:
                        pe.wait_ge(a1_done, b * E1 + u)
                    pe.matmul(ps_c[:], pick[:, u, :], cT1, start=True, stop=True).then_inc(c1_made, 1)

            def down_at(b, u):
                if u < E1:
                    pe.wait_ge(a1_done, b * E1 + u + 1)
                else:
                    pe.wait_ge(act_x, b * UNITS + u + 1)
                if u == 0:
                    if past(b, 1):
                        pe.wait_ge(post1.sem, post1.after("v", b - 1))
                    else:
                        pe.wait_ge(ready1, 2)
                w = fc2[:, u, :] if u < E1 else sfc2[:, u - E1, :]
                pe.matmul(ps_y1[:], w, hc1[:, u % 2, :], start=(u == 0), stop=(u == UNITS - 1)).then_inc(y1_made, 1)

            def biases(b):
                for j in range(3):
                    pe.matmul(ps_y1[:], b2_p[:, 1, j, :], cT1, start=False, stop=False)

            def end1_at(b, u):
                if u == 2:
                    pe.wait_ge(post1.sem, post1.after("ws", b))
                    turn(out_bank(b), ws1).then_inc(post1.sem, 1)

            def unit1(b, u, full, previous, following):
                if full:
                    up_at(b, u)
                if full and u >= 1:
                    down_at(b, u - 1)
                if previous and u == 0:
                    down_at(b - 1, UNITS - 1)
                if full and u == E1 - 1:
                    biases(b)
                if following:
                    pre1_at(b + 1, u)
                if previous:
                    end1_at(b - 1, u)

            def body1(b, full, previous, following):
                for u in range(UNITS):
                    unit1(b, u, full, previous, following)

            def layer1_at(pos):
                for u in range(UNITS):
                    if pos == PRE1_AT[u]:
                        pre1_at(0, u)
                for n, at in enumerate(UNIT1_AT):
                    if pos == at:
                        unit1(n // UNITS, n % UNITS, True, n >= UNITS, True)

            def body(b, full, previous, before, following):
                alive = [(n, b - n) for n in range(3) if (full, previous, before)[n]]
                for s in range(SLOTS):
                    for n, batch in alive:
                        if LAG <= s + SLOTS * n < LAG + SLOTS:
                            transposed(batch, s + SLOTS * n - LAG)
                    if full:
                        scores(b, s)
                    for n, batch in alive:
                        q, rest = divmod(s + SLOTS * n - LAG - 6, 4)
                        if rest == 0 and 0 <= q < 16:
                            weighted(batch, q)
                    if isinstance(b, int) and b == 0:
                        ssm_at(0, s - LATE0)
                    if following:
                        ssm_at(b + 1, s - SLOTS)
                    if following:
                        pre_at(b + 1, s - SLOTS)
                    for n, batch in alive[::-1]:
                        tail_at(batch, s + SLOTS * n)
                        post_at(batch, s + SLOTS * n)
                        experts_at(batch, s + SLOTS * n)
                    if isinstance(b, int) and b >= NB - 1:
                        layer1_at(s + SLOTS * (b - NB + 1))
                    if full and s in (17, 33, 49):
                        shift_turn(b, s // 16 - 1)
                    if previous and s == 1:
                        shift_turn(b - 1, NG - 1)

            for s in range(-SLOTS, 0):
                pre_at(0, s)
            pe.wait_ge(w_early, 16 * 14)
            pe.matmul(ps_b[:, 0:1], w_o0[:], col("bv"), start=True, stop=True).then_inc(setup_pe, 1)
            pe.wait_ge(consts, 2)
            pe.wait_ge(setup, SETUP["b2"])
            pe.wait_ge(setup_pool, 4)
            for s in range(-SLOTS, 0):
                ssm_at(0, s - LATE0)
            body(0, True, False, False, True)
            body(1, True, True, False, True)
            with pe.Fori(2, NB - 1) as b:
                body(b, True, True, True, True)
            body(NB - 1, True, True, True, False)
            body(NB, False, True, True, False)
            body(NB + 1, False, False, True, False)
            with pe.Fori(2, NB - 1) as b:
                body1(b, True, True, True)
            body1(NB - 1, True, True, False)
            body1(NB, False, True, False)

        @block.scalar
        def _(act):
            act.wait_ge(w_first, 16 * 3)

            def ssm_at(b, s):
                for s0, step, made, i in ((AT["u0_sb"], "u0_sb", "u0", 0), (AT["u1_sb"], "u1_sb", "u1", 1)):
                    if s == s0:
                        act.wait_ge(ssm.sem, ssm.after(made, b))
                        nc.scalar.copy(up[:, i, 3:3 + S], ps_a[:]).then_inc(ssm.sem, 1)
                for i, s0 in ((0, AT["c0"]), (1, AT["c1"])):
                    if s == s0:
                        act.wait_ge(ssm.sem, ssm.after(("u1_sb", "c03")[i], b))
                        nc.scalar.activation(uc[:, i, :], up[:, i, 0:S], ACT.Identity, bias=col("conv_b", i),
                                             scale=col("conv_w", 4 * i)).then_inc(ssm.sem, 1)
                for s0, made, i in ((AT["th0"], "z0", 0), (AT["th1"], "z1", 1)):
                    if s == s0:
                        act.wait_ge(ssm.sem, ssm.after(made, b))
                        if isinstance(b, int) and b == 0 and i == 0:
                            act.wait_ge(setup, SETUP["dt_half"])
                        nc.scalar.activation(th[:], ps_a[:], ACT.Tanh, bias=col("dt_half", i), scale=0.5).then_inc(ssm.sem, 1)

            def pre_at(b, s):
                if s == AT["xT"]:
                    act.wait_ge(pre.sem, pre.after("turn", b))
                    nc.scalar.copy(xT[:], ps_a[:]).then_inc(pre.sem, 1)
                    nc.scalar.copy(xT_all[:, b, :], ps_a[:]).then_inc(pre.sem, 1)
                for s0, made, j in ((AT["q1"], "q", 0), (AT["k1"], "k", 1)):
                    if s == s0:
                        act.wait_ge(pre.sem, pre.after(made, b))
                        if j == 0 and past(b, 1):
                            act.wait_ge(stack_out, 16 * 9 * b)
                        nc.scalar.activation(qk_p[:, j, 0, :], ps_a[:], ACT.Identity, bias=col("bq", j)).then_inc(pre.sem, 1)
                if s == AT["v_sb"]:
                    act.wait_ge(pre.sem, pre.after("v", b))
                    if past(b, 1):
                        act.wait_ge(v_put, NG * b)
                    nc.scalar.copy(v_new[:].rearrange("p t n -> p (t n)"), ps_a[:]).then_inc(pre.sem, 1)

            def exps(b, v):
                act.wait_ge(t_made, b * SLOTS + v + 1)
                if past(b, 1) or v >= 8:
                    act.wait_ge(pv_done, b * 16 + v // 4 - 1)
                nc.scalar.activation(probs[:, v % 8, :], ps_t[v % 2][:], ACT.Exp, scale=SCALE).then_inc(exp_done, 1)

            def group_out(b, g):
                act.wait_ge(pv_done, b * 16 + 4 * g + 4)
                if past(b, 1) or g >= 1:
                    act.wait_ge(o_moved[g - 1], 16 * 8 * (b + (1 if g else 0)))
                nc.scalar.copy(oT[:], ps_o[:]).then_inc(ot_made, 1)

            def post_at(b, s):
                if s == AT["x1"]:
                    act.wait_ge(post.sem, post.after("turn2", b))
                    nc.scalar.activation(x1T[:], ps_b[:], ACT.Identity, bias=col("ln1_b"), scale=col("ln1_g")).then_inc(post.sem, 1)
                if s == AT["gexp"]:
                    act.wait_ge(post.sem, post.after("gsub", b))
                    nc.scalar.activation(g4[:, 1], g4[:, 0], ACT.Exp).then_inc(post.sem, 1)
                if s == AT["eexp"]:
                    act.wait_ge(post.sem, post.after("eabs", b))
                    nc.scalar.activation(g4[:, 5], g4[:, 4], ACT.Exp).then_inc(post.sem, 1)
                if s == AT["cT"]:
                    act.wait_ge(post.sem, post.after("cturn", b))
                    nc.scalar.copy(cT[:], ps_b[0:96, :].bitcast(BF16)[:, 0:S]).then_inc(post.sem, 1)

            def experts_at(b, s):
                for e in range(E0):
                    if s == C_AT[e]:
                        act.wait_ge(c_made, b * E0 + e + 1)
                        if e >= 2 or past(b, 1):
                            act.wait_ge(hc_made, (b * E0 + e - 1) * 2)
                        nc.scalar.copy(cbc[:, e % 2, :], c_bank(b, e)[:]).then_inc(c_sb, 1)
                for k in range(2 * E0):
                    if s == Z_AT[k]:
                        act.wait_ge(z_made, b * 2 * E0 + k + 1)
                        if k >= 2 or past(b, 1):
                            act.wait_ge(hc_made, b * 2 * E0 + k - 1)
                        nc.scalar.activation(hz[:, k % 2, :], ps_b[:], ACT.Relu, bias=col("b1", k)).then_inc(z_sb, 1)

            def tail_at(b, s):
                if s == AT["tanh"]:
                    act.wait_ge(tail.sem, tail.after("bias", b))
                    nc.scalar.activation(tht[:], zg[:], ACT.Tanh, scale=0.5).then_inc(tail.sem, 1)
                if s == AT["s_near"]:
                    nc.scalar.copy(s_near[:], sT_all[:, b, :]).then_inc(tail.sem, 1)
                if s == AT["s_tok"]:
                    act.wait_ge(tail.sem, tail.after("s_turn", b))
                    nc.scalar.copy(s_tok[:], tiles(s_turned_bank(b)[:])).then_inc(tail.sem, 1)

            def pre1_at(b, u):
                if u == 2:
                    act.wait_ge(pre1.sem, pre1.after("turn", b))
                    nc.scalar.copy(xT[:], ps_p[:]).then_inc(pre1.sem, 1)
                    nc.scalar.copy(xT_all[:, b, :], ps_p[:]).then_inc(pre1.sem, 1)
                if u == 6:
                    act.wait_ge(pre1.sem, pre1.after("v", b))
                    nc.scalar.copy(vT[:, :, 0:P], tiles(ps_p[:])).then_inc(pre1.sem, 1)
                if u == 15:
                    act.wait_ge(gate1.sem, gate1.after("cturn", b))
                    nc.scalar.copy(cT1, ps_p[0:96, :].bitcast(BF16)[:, 0:S]).then_inc(gate1.sem, 1)

            def gelu_at(b, u):
                n = b * UNITS + u
                act.wait_ge(g1_made, n + 1)
                if past(b, 1) or u >= 2:
                    act.wait_ge(act_x, before(b, u))
                bias = col("fc1_b", 2 * u + 1) if u < E1 else col("sfc1_b", u - E1 + 2)
                nc.scalar.activation(hz1[:, u % 2, :], ps_g[half(b, u)][:], ACT.Gelu, bias=bias).then_inc(gelu_done, 1)

            def end1_at(b, u):
                if u == 0:
                    act.wait_ge(y1_made, UNITS * (b + 1))
                    nc.scalar.activation(th[:], ps_y1[:], ACT.Tanh, bias=col("sb_half"), scale=0.5).then_inc(post1.sem, 1)

            def unit1(b, u, full, previous, following):
                if full:
                    gelu_at(b, u)
                if previous:
                    end1_at(b - 1, u)
                if following:
                    pre1_at(b + 1, u)

            def body1(b, full, previous, following):
                for u in range(UNITS):
                    unit1(b, u, full, previous, following)

            def layer1_at(pos):
                for u in range(UNITS):
                    if pos == PRE1_AT[u]:
                        pre1_at(0, u)
                for n, at in enumerate(UNIT1_AT):
                    if pos == at:
                        unit1(n // UNITS, n % UNITS, True, n >= UNITS, True)

            def body(b, full, previous, before, following):
                alive = [(n, b - n) for n in range(3) if (full, previous, before)[n]]
                for s in range(SLOTS):
                    for n, batch in alive:
                        if LAG <= s + SLOTS * n < LAG + SLOTS:
                            exps(batch, s + SLOTS * n - LAG)
                    for n, batch in alive:
                        g, rest = divmod(s + SLOTS * n - LAG - 18, 16)
                        if rest == 0 and 0 <= g < NG:
                            group_out(batch, g)
                    if isinstance(b, int) and b == 0:
                        ssm_at(0, s - LATE0)
                    if following:
                        ssm_at(b + 1, s - SLOTS)
                    if following:
                        pre_at(b + 1, s - SLOTS)
                    for n, batch in alive[::-1]:
                        tail_at(batch, s + SLOTS * n)
                        post_at(batch, s + SLOTS * n)
                        experts_at(batch, s + SLOTS * n)
                    if isinstance(b, int) and b >= NB - 1:
                        layer1_at(s + SLOTS * (b - NB + 1))

            for s in range(-SLOTS, 0):
                pre_at(0, s)
            act.wait_ge(w_early, 16 * 14)
            act.wait_ge(consts, 2)
            for s in range(-SLOTS, 0):
                ssm_at(0, s - LATE0)
            body(0, True, False, False, True)
            body(1, True, True, False, True)
            with act.Fori(2, NB - 1) as b:
                body(b, True, True, True, True)
            body(NB - 1, True, True, True, False)
            body(NB, False, True, True, False)
            body(NB + 1, False, False, True, False)
            with act.Fori(2, NB - 1) as b:
                body1(b, True, True, True)
            body1(NB - 1, True, True, False)
            body1(NB, False, True, False)

        @block.vector
        def _(dve):
            v = nc.vector

            def moments(src, i, chain, names, b):
                for t in range(T):
                    ins = v.bn_stats(st6[:, i, t], src(t))
                ins.then_inc(chain.sem, 1)
                wait_apart(dve, (chain.sem, chain.after(names[0], b)))
                for t in range(T):
                    ins = v.bn_aggr(mv[:, i, t], st6[:, i, t])
                ins.then_inc(chain.sem, 1)

            def normal(dst, src, i):
                for t in range(T):
                    ins = v.tensor_scalar(dst[:, t], src(t), mv[:, i, t, 0:1], rstd[:, i, 1, t:t + 1], ALU.subtract, ALU.mult)
                return ins

            def ssm_at(b, s):
                for i, s0 in ((0, AT["c0"]), (1, AT["c1"])):
                    for j in (1, 2, 3):
                        if s == s0 + j:
                            dve.wait_ge(ssm.sem, ssm.after(f"c{i}{j - 1}", b))
                            v.scalar_tensor_tensor(out=uc[:, i, :], in0=up[:, i, j:j + S], scalar=col("conv_w", 4 * i + j),
                                                   in1=uc[:, i, :], op0=ALU.mult, op1=ALU.add).then_inc(ssm.sem, 1)
                for i, s0 in ((0, AT["gu0"]), (1, AT["gu1"])):
                    if s == s0:
                        dve.wait_ge(ssm.sem, ssm.after(f"th{i}", b))
                        v.scalar_tensor_tensor(out=gu[:, i, :], in0=th[:], scalar=3.0, in1=uc[:, i, :], op0=ALU.add,
                                               op1=ALU.mult).then_inc(ssm.sem, 1)
                if s == AT["scan"]:
                    dve.wait_ge(ssm.sem, ssm.after("p", b))
                    v.tensor_tensor_scan(scan[:], decay[:], ps_a[:], 0.0, ALU.mult, ALU.add).then_inc(ssm.sem, 1)
                if s == AT["s"]:
                    dve.wait_ge(ssm.sem, ssm.after("res", b))
                    v.tensor_tensor(sT_all[:, b, :], ps_a[:], scan[:], ALU.add).then_inc(ssm.sem, 1)

            def pre_at(b, s):
                if s == AT["stats"]:
                    if isinstance(b, int) and b == 0:
                        dve.wait_ge(x_first, 16)
                    elif isinstance(b, int) and b == 1:
                        dve.wait_ge(x_rest, 16 * (NB - 1))
                    if past(b, 1):
                        dve.wait_ge(pre.sem, pre.after("k3", b - 1))
                    moments(lambda t: x_all[:, b, t], 0, pre, ["stats"], b)
                if s == AT["xn"]:
                    dve.wait_ge(pre.sem, pre.after("rstd", b))
                    normal(xn, lambda t: x_all[:, b, t], 0).then_inc(pre.sem, 1)
                for s0, made, j in ((AT["qr"], "q1", 0), (AT["kr"], "k1", 1)):
                    if s == s0:
                        dve.wait_ge(pre.sem, pre.after(made, b))
                        v.scalar_tensor_tensor(out=qk_r[:, j, :], in0=ps_a[:], scalar=col("bq", j), in1=qk_p[:, j, 0, :],
                                               op0=ALU.add, op1=ALU.subtract).then_inc(pre.sem, 1)

            def maxima(b, s):
                h, t = s // T, s % T
                dve.wait_ge(s_made, s_use(b, s_pos(s)) + 1)
                v.tensor_reduce(smax[:, h // 4, h % 4, t:t + 1], s_bank(b, s_pos(s))[:], AX, ALU.max).then_inc(s_read, 1)

            def shift_pieces(b, g):
                n = b * NG + g
                dve.wait_ge(s_read, s_use(b, s_pos(16 * g + 15)) + 1)
                v.tensor_scalar(smax_n[:], smax[:, g], -1.0, None, ALU.mult).then_inc(shift.sem, 1)
                dve.wait_ge(shift.sem, shift.after("neg", n))
                hi = smax_p[:].rearrange("p t a r -> p a r t")
                v.tensor_copy(hi[:, 0], smax_n[:]).then_inc(shift.sem, 1)
                dve.wait_ge(shift.sem, shift.after("hi", n))
                v.tensor_tensor(smax_r[:], smax_n[:], hi[:, 0], ALU.subtract).then_inc(shift.sem, 1)
                dve.wait_ge(shift.sem, shift.after("rest", n))
                v.tensor_copy(hi[:, 1], smax_r[:]).then_inc(shift.sem, 1)

            def shift_rows(b, g):
                at, pos = turn_use(b, g)
                n = b * NG + g
                dve.wait_ge(s_made, s_use(at, pos) + 1)
                if past(n, 1):
                    dve.wait_ge(shift_out, 16 * n)
                v.tensor_copy(smax_t[:], s_bank(at, pos)[0:8, :].bitcast(BF16)[:, 0:S]).then_inc(s_read, 1)

            def post_at(b, s):
                def step(name, ins):
                    ins.then_inc(post.sem, 1)
                    dve.wait_ge(post.sem, post.after(name, b))

                if s == AT["rd"]:
                    for g in range(NG):
                        dve.wait_ge(o_moved[g], 16 * 8 * (b + 1))
                    v.reciprocal(o_den_c[:], o_den_c[:]).then_inc(post.sem, 1)
                if s == AT["on"]:
                    dve.wait_ge(post.sem, post.after("den", b))
                    v.tensor_tensor(o_n[:], o_num[:], ps_b[:], ALU.mult).then_inc(post.sem, 1)
                if s == AT["r1"]:
                    dve.wait_ge(post.sem, post.after("proj", b))
                    v.scalar_tensor_tensor(out=r1[:], in0=ps_b[:], scalar=col("bo_all"), in1=xT_all[:, b, :], op0=ALU.add,
                                           op1=ALU.add).then_inc(post.sem, 1)
                if s == AT["stats1"]:
                    dve.wait_ge(post.sem, post.after("turn1", b))
                    moments(lambda t: ps_b[:, t * P:(t + 1) * P], 1, post, ["stats1"], b)
                if s == AT["z"]:
                    if past(b, 1):
                        dve.wait_ge(tail.sem, tail.after("x_new", b - 1))
                    dve.wait_ge(post.sem, post.after("rstd1", b))
                    normal(z1, lambda t: ps_b[:, t * P:(t + 1) * P], 1).then_inc(post.sem, 1)
                if s == AT["group"]:
                    dve.wait_ge(post.sem, post.after("logits", b))
                    step("lg", v.tensor_tensor(gl[:], ps_b[:, 0:48].rearrange("p (t e) -> p t e", t=T),
                                               rows[:, 2:3, 0:12].broadcast_to([P, T, 12]), ALU.add))
                    gr = gl[:, :, 0:4]
                    step("gmax", v.tensor_reduce(gm[:, 0, :], gr, AX, ALU.max))
                    v.tensor_tensor(g4[:, 0], gr, gm[:, 0, :].unsqueeze(2).broadcast_to([P, T, 4]), ALU.subtract).then_inc(post.sem, 1)
                if s == AT["expert"]:
                    dve.wait_ge(post.sem, post.after("gexp", b))
                    step("gsum", v.tensor_reduce(gm[:, 1, :], g4[:, 1], AX, ALU.add))
                    step("gties", v.scalar_tensor_tensor(out=g4[:, 2], in0=g4[:, 0], scalar=0.0,
                                                         in1=rows[:, 2:3, 12:16].broadcast_to([P, T, 4]), op0=ALU.is_equal, op1=ALU.mult))
                    step("gtop", v.tensor_reduce(gm[:, 2, :], g4[:, 2], AX, ALU.max))
                    step("ghot", v.tensor_tensor(g4[:, 3], g4[:, 2], gm[:, 2, :].unsqueeze(2).broadcast_to([P, T, 4]), ALU.is_equal))
                    ex = gl[:, :, 4:12].rearrange("p t (g e) -> p t g e", e=2)
                    step("ediff", v.tensor_tensor(g4[:, 6], ex[:, :, :, 0], ex[:, :, :, 1], ALU.subtract))
                    v.scalar_tensor_tensor(out=g4[:, 4], in0=g4[:, 6], scalar=-1.0, in1=g4[:, 6], op0=ALU.mult,
                                           op1=ALU.min).then_inc(post.sem, 1)
                if s == AT["comb"]:
                    dve.wait_ge(post.sem, post.after("eexp", b))
                    step("eden", v.scalar_tensor_tensor(out=g4[:, 4], in0=g4[:, 5], scalar=1.0,
                                                        in1=gm[:, 1, :].unsqueeze(2).broadcast_to([P, T, 4]), op0=ALU.add, op1=ALU.mult))
                    step("erec", v.reciprocal(g4[:, 5], g4[:, 4]))
                    step("chot", v.tensor_tensor(g4[:, 7], g4[:, 5], g4[:, 3], ALU.mult))
                    step("first", v.scalar_tensor_tensor(out=comb[:, :, :, 0], in0=g4[:, 6], scalar=0.0, in1=g4[:, 7],
                                                         op0=ALU.is_ge, op1=ALU.mult))
                    step("second", v.tensor_tensor(comb[:, :, :, 1], g4[:, 7], comb[:, :, :, 0], ALU.subtract))
                    pieces(comb[:].rearrange("p t g e -> p t (g e)"), E0, step)
                if s == AT["r2"]:
                    dve.wait_ge(post.sem, post.after("y", b))
                    v.tensor_tensor(r2[:], ps_y[:], x1T[:], ALU.add).then_inc(post.sem, 1)
                if s == AT["stats2"]:
                    dve.wait_ge(post.sem, post.after("turn3", b))
                    moments(lambda t: ps_b[:, t * P:(t + 1) * P], 2, post, ["stats2"], b)

            def pieces(c, n, step):
                step("p1", v.tensor_copy(cpb[:, :, 0:n], c))
                step("s1", v.tensor_tensor(cpf[:, 0, :, 0:n], c, cpb[:, :, 0:n], ALU.subtract))
                step("p2", v.tensor_copy(cpb[:, :, 32:32 + n], cpf[:, 0, :, 0:n]))
                step("s2", v.tensor_tensor(cpf[:, 1, :, 0:n], cpf[:, 0, :, 0:n], cpb[:, :, 32:32 + n], ALU.subtract))
                step("p3", v.tensor_copy(cpb[:, :, 64:64 + n], cpf[:, 1, :, 0:n]))

            def tail_at(b, s):
                if s == AT["z2"]:
                    dve.wait_ge(post.sem, post.after("rstd2", b))
                    normal(zt, lambda t: ps_b[:, t * P:(t + 1) * P], 2).then_inc(tail.sem, 1)

            def pre1_at(b, u):
                def step(name, ins, chain=gate1, own=False):
                    ins.then_inc(chain.sem, 1)
                    if own:
                        wait_apart(dve, (chain.sem, chain.after(name, b)))
                    else:
                        dve.wait_ge(chain.sem, chain.after(name, b))

                if u == 0:
                    if past(b, 1):
                        dve.wait_ge(gate1.sem, gate1.after("cT", b - 1))
                    dve.wait_ge(tail.sem, tail.after("x_new", b if isinstance(b, int) and b < 3 else NB - 1))
                    for t in range(T):
                        ins = v.bn_stats(st6[:, 3, t], x_all[:, b, t])
                    step("stats", ins, pre1, own=True)
                    for t in range(T):
                        ins = v.bn_aggr(mv[:, 3, t], st6[:, 3, t])
                    ins.then_inc(pre1.sem, 1)
                if u == 1:
                    dve.wait_ge(pre1.sem, pre1.after("rstd", b))
                    for t in range(T):
                        ins = v.tensor_scalar(xn[:, t], x_all[:, b, t], mv[:, 3, t, 0:1], rstd[:, 3, 1, t:t + 1], ALU.subtract, ALU.mult)
                    ins.then_inc(pre1.sem, 1)
                if u == 3:
                    dve.wait_ge(gate1.sem, gate1.after("logits", b))
                    lp = ps_p[:, 0:T * E1].rearrange("p (t e) -> p t e", t=T)
                    step("lmax", v.tensor_reduce(gm1[:, 0, :], lp, AX, ALU.max))
                    v.tensor_tensor(lg[:, 0, :, 0:E1], lp, spread(gm1[:, 0, :]), ALU.subtract).then_inc(gate1.sem, 1)
                if u == 4:
                    dve.wait_ge(pre1.sem, pre1.after("q", b))
                    v.tensor_scalar(qT[:], ps_p[:], 0.0, None, ALU.max).then_inc(pre1.sem, 1)
                if u == 5:
                    dve.wait_ge(pre1.sem, pre1.after("k", b))
                    v.tensor_scalar(kT[:], tiles(ps_p[:]), 0.0, None, ALU.max).then_inc(pre1.sem, 1)
                if u == 7:
                    dve.wait_ge(pre1.sem, pre1.after("kv", b))
                    v.tensor_tensor(kv[:], ps_p[:, 0:P], block1[:], ALU.mult).then_inc(pre1.sem, 1)
                    v.tensor_scalar(ksum[:], block1[:], ps_p[:, P:P + 1], None, ALU.mult).then_inc(pre1.sem, 1)
                if u == 8:
                    dve.wait_ge(gate1.sem, gate1.after("lexp", b))
                    step("lsum", v.tensor_reduce(gm1[:, 1, :], lg[:, 1, :, 0:E1], AX, ALU.add))
                    step("lrec", v.reciprocal(gm1[:, 2, :], gm1[:, 1, :]))
                    step("score", v.tensor_tensor(lg[:, 2, :, 0:E1], lg[:, 1, :, 0:E1], spread(gm1[:, 2, :]), ALU.mult), own=True)
                    for t in range(T):
                        ins = v.max(m8[:, t], lg[:, 2, t])
                    ins.then_inc(gate1.sem, 1)
                if u == 9:
                    dve.wait_ge(pre1.sem, pre1.after("dn", b))
                    v.tensor_scalar(o_num1[:], ps_p[:], 1e-15, None, ALU.add).then_inc(pre1.sem, 1)
                    dve.wait_ge(gate1.sem, gate1.after("top8", b))
                    step("top3", v.tensor_copy(m8v[:, :, 0:3], m8[:, :, 0:3]), own=True)
                    for t in range(T):
                        ins = v.match_replace(lg[:, 3, t], m8v[:, t], lg[:, 2, t], -2.0)
                    ins.then_inc(gate1.sem, 1)
                if u in (10, 11):
                    c = (u - 10) * 256
                    if u == 10:
                        dve.wait_ge(pre1.sem, pre1.after("dn_eps", b))
                    v.reciprocal(r21[:, c:c + 256], o_num1[:, c:c + 256]).then_inc(pre1.sem, 1)
                if u == 12:
                    dve.wait_ge(pre1.sem, pre1.after("num", b))
                    v.tensor_tensor(o_n1[:], ps_p[:], r21[:], ALU.mult).then_inc(pre1.sem, 1)
                    dve.wait_ge(gate1.sem, gate1.after("rep", b))
                    step("mask", v.tensor_tensor(lg[:, 4, :, 0:E1], lg[:, 3, :, 0:E1], lg[:, 2, :, 0:E1], ALU.not_equal))
                    step("tw", v.tensor_tensor(lg[:, 5, :, 0:E1], lg[:, 4, :, 0:E1], lg[:, 2, :, 0:E1], ALU.mult))
                    step("tsum", v.tensor_reduce(gm1[:, 3, :], lg[:, 5, :, 0:E1], AX, ALU.add))
                    v.tensor_scalar(gm1[:, 4, :], gm1[:, 3, :], 1e-20, None, ALU.add).then_inc(gate1.sem, 1)
                if u == 13:
                    dve.wait_ge(pre1.sem, pre1.after("pr", b))
                    v.tensor_scalar(sT_all[:, b, :], ps_p[:], col("bp"), None, ALU.add).then_inc(pre1.sem, 1)
                    dve.wait_ge(gate1.sem, gate1.after("tsum_eps", b))
                    step("trec", v.reciprocal(gm1[:, 5, :], gm1[:, 4, :]))
                    if not past(b, 1):
                        dve.wait_ge(ready1, 1)
                    step("comb", v.tensor_tensor(lg[:, 4, :, 0:E1], lg[:, 5, :, 0:E1], spread(gm1[:, 5, :]), ALU.mult))
                    v.tensor_copy(cpb1[:, :, 0:E1], lg[:, 4, :, 0:E1]).then_inc(gate1.sem, 1)
                if u == 14:
                    dve.wait_ge(gate1.sem, gate1.after("p1", b))
                    step("s1", v.tensor_tensor(cpf1[:, 0, :, 0:E1], lg[:, 4, :, 0:E1], cpb1[:, :, 0:E1], ALU.subtract))
                    step("p2", v.tensor_copy(cpb1[:, :, 32:32 + E1], cpf1[:, 0, :, 0:E1]))
                    step("s2", v.tensor_tensor(cpf1[:, 1, :, 0:E1], cpf1[:, 0, :, 0:E1], cpb1[:, :, 32:32 + E1], ALU.subtract))
                    v.tensor_copy(cpb1[:, :, 64:64 + E1], cpf1[:, 1, :, 0:E1]).then_inc(gate1.sem, 1)

            def spread(x):
                return x.unsqueeze(2).broadcast_to([P, T, E1])

            def unit_at(b, u):
                n = b * UNITS + u
                dve.wait_ge(gelu_done, n + 1)
                dve.wait_ge(x1_made, n + 1)
                if past(b, 1) or u >= 2:
                    dve.wait_ge(y1_made, before(b, u))
                bias = col("fc1_b", 2 * u) if u < E1 else col("sfc1_b", u - E1)
                mid = cbc1 if u < E1 else hc1
                ins = v.scalar_tensor_tensor(out=mid[:, u % 2, :], in0=ps_x[half(b, u)][:], scalar=bias,
                                             in1=hz1[:, u % 2, :], op0=ALU.add, op1=ALU.mult)
                ins.then_inc(act_x, 1)
                if u < E1:
                    dve.wait_ge(act_x, n + 1)
                    dve.wait_ge(c1_made, b * E1 + u + 1)
                    v.tensor_tensor(hc1[:, u % 2, :], cbc1[:, u % 2, :], ps_c[:], ALU.mult).then_inc(a1_done, 1)

            def end1_at(b, u):
                if u == 0:
                    dve.wait_ge(post1.sem, post1.after("th", b))
                    v.tensor_scalar(scan[:], ps_y1[:], col("sb"), None, ALU.add).then_inc(post1.sem, 1)
                if u == 1:
                    dve.wait_ge(post1.sem, post1.after("v", b))
                    v.scalar_tensor_tensor(out=s_gated, in0=th[:], scalar=1.0, in1=scan[:], op0=ALU.add, op1=ALU.mult).then_inc(post1.sem, 1)
                    dve.wait_ge(post1.sem, post1.after("w", b))
                    v.tensor_tensor(ws1, s_gated, sT_all[:, b, :], ALU.mult).then_inc(post1.sem, 1)
                if u == 2:
                    dve.wait_ge(post1.sem, post1.after("turn", b))
                    v.scalar_tensor_tensor(out=x_all[:, b], in0=tiles(out_bank(b)[:]), scalar=0.5, in1=x_all[:, b], op0=ALU.mult,
                                           op1=ALU.add).then_inc(post1.sem, 1)

            def unit1(b, u, full, previous, following):
                if full:
                    unit_at(b, u)
                if previous:
                    end1_at(b - 1, u)
                if following:
                    pre1_at(b + 1, u)

            def body1(b, full, previous, following):
                for u in range(UNITS):
                    unit1(b, u, full, previous, following)

            def layer1_at(pos):
                for u in range(UNITS):
                    if pos == PRE1_AT[u]:
                        pre1_at(0, u)
                for n, at in enumerate(UNIT1_AT):
                    if pos == at:
                        unit1(n // UNITS, n % UNITS, True, n >= UNITS, True)

            def body(b, full, previous, before, following):
                alive = [(n, b - n) for n in range(3) if (full, previous, before)[n]]
                for s in range(SLOTS):
                    if full:
                        maxima(b, s)
                    if full and s % 16 == 15:
                        shift_pieces(b, s // 16)
                    if full and s in (17, 33, 49):
                        shift_rows(b, s // 16 - 1)
                    if previous and s == 1:
                        shift_rows(b - 1, NG - 1)
                    if isinstance(b, int) and b == 0:
                        ssm_at(0, s - LATE0)
                    if following:
                        ssm_at(b + 1, s - SLOTS)
                    if following:
                        pre_at(b + 1, s - SLOTS)
                    for n, batch in alive[::-1]:
                        tail_at(batch, s + SLOTS * n)
                        post_at(batch, s + SLOTS * n)
                    if isinstance(b, int) and b >= NB - 1:
                        layer1_at(s + SLOTS * (b - NB + 1))

            for s in range(-SLOTS, 0):
                pre_at(0, s)
            dve.wait_ge(w_early, 16 * 14)
            v.tensor_scalar(vec[:, V["dt_half"]:V["dt_half"] + 2], vec[:, V["dt_b"]:V["dt_b"] + 2], -LN2, 0.5, ALU.add, ALU.mult).then_inc(setup, 1)
            v.tensor_scalar(w_out0[:], w_out0[:], 0.25 * GAIN, None, ALU.mult).then_inc(setup, 1)
            dve.wait_ge(setup_pe, 1)
            v.tensor_tensor(col("bo_all"), ps_b[:, 0:1], col("bo"), ALU.add).then_inc(setup, 1)
            v.tensor_scalar(col("sb_half"), col("sb"), 0.5, None, ALU.mult).then_inc(setup, 1)
            v.tensor_copy(b2_p[:, :, 0, :], b2_f[:]).then_inc(setup, 1)
            dve.wait_ge(setup, 5)
            v.tensor_tensor(b2_f[:], b2_f[:], b2_p[:, :, 0, :], ALU.subtract).then_inc(setup, 1)
            dve.wait_ge(setup, 6)
            v.tensor_copy(b2_p[:, :, 1, :], b2_f[:]).then_inc(setup, 1)
            dve.wait_ge(setup, 7)
            v.tensor_tensor(b2_p[:, :, 2, :], b2_f[:], b2_p[:, :, 1, :], ALU.subtract).then_inc(setup, 1)
            dve.wait_ge(setup, SETUP["b2"])
            dve.wait_ge(consts, 2)
            for s in range(-SLOTS, 0):
                ssm_at(0, s - LATE0)
            body(0, True, False, False, True)
            body(1, True, True, False, True)
            with dve.Fori(2, NB - 1) as b:
                body(b, True, True, True, True)
            body(NB - 1, True, True, True, False)
            body(NB, False, True, True, False)
            body(NB + 1, False, False, True, False)
            with dve.Fori(2, NB - 1) as b:
                body1(b, True, True, True)
            body1(NB - 1, True, True, False)
            body1(NB, False, True, False)

        @block.gpsimd
        def _(pool):
            p = nc.gpsimd
            p.memset(b2_f[:], 0.0).then_inc(consts, 1)
            p.memset(mhalf[:], -0.5).then_inc(setup_pool, 1)
            pool.wait_ge(setup_pool, 1)

            def rsqrt(i, chain, first, names, b):
                wait_apart(pool, (chain.sem, chain.after(first, b)))
                p.tensor_scalar(rstd[:, i, 0, :], mv[:, i, :, 1], EPS, None, ALU.add).then_inc(chain.sem, 1)
                pool.wait_ge(chain.sem, chain.after(names[0], b))
                p.tensor_tensor(rstd[:, i, 1, :], rstd[:, i, 0, :], mhalf[:], ALU.pow).then_inc(chain.sem, 1)

            def pre_at(b, s):
                if s == AT["rstd"]:
                    rsqrt(0, pre, "moments", ["eps"], b)
                if s == AT["q2"]:
                    wait_apart(pool, (pre.sem, pre.after("v_sb", b)))
                    for j, name in ((0, "q2"), (1, "k2")):
                        p.tensor_scalar(qk_p[:, j, 1, :], qk_r[:, j, :], 1.0, None, ALU.mult).then_inc(pre.sem, 1)
                        pool.wait_ge(pre.sem, pre.after(name, b))
                        p.tensor_tensor(qk_p[:, j, 2, :], qk_r[:, j, :], qk_p[:, j, 1, :], ALU.subtract).then_inc(pre.sem, 1)

            def values(b, g):
                spent = [(pv_done, 16 * (b - 1) + 4 * g + 4)] if past(b, 1) else []
                wait_apart(pool, (pre.sem, pre.after("v_sb", b)), *spent)
                p.tensor_scalar(v_aug[:, :, 4 * g:4 * g + 4, 0:HD],
                                v_new[:, :, 32 * g:32 * g + 32].rearrange("p t (h d) -> p t h d", d=HD),
                                1.0, None, ALU.mult).then_inc(v_put, 1)

            def post_at(b, s):
                if s == AT["rstd1"]:
                    rsqrt(1, post, "moments1", ["eps1"], b)
                if s == AT["rstd2"]:
                    rsqrt(2, post, "moments2", ["eps2"], b)

            def tail_at(b, s):
                if s == AT["gain"]:
                    pool.wait_ge(tail.sem, tail.after("z2", b))
                    p.tensor_tensor(zg[:], zt[:], rows[:, 0:1, :].broadcast_to([P, T, P]), ALU.mult).then_inc(tail.sem, 1)
                    pool.wait_ge(tail.sem, tail.after("gain", b))
                    p.tensor_tensor(zg[:], zg[:], rows[:, 1:2, :].broadcast_to([P, T, P]), ALU.add).then_inc(tail.sem, 1)
                if s == AT["w"]:
                    wait_apart(pool, (tail.sem, tail.after("tanh", b)))
                    p.tensor_scalar(tht[:], tht[:], 0.5, 0.5, ALU.mult, ALU.add).then_inc(tail.sem, 1)
                    pool.wait_ge(tail.sem, tail.after("half", b))
                    p.tensor_tensor(zt[:], tht[:], zg[:], ALU.mult).then_inc(tail.sem, 1)
                if s == AT["ws"]:
                    pool.wait_ge(tail.sem, tail.after("w", b))
                    p.tensor_tensor(zg[:], zt[:], s_tok[:], ALU.mult).then_inc(tail.sem, 1)
                    pool.wait_ge(tail.sem, tail.after("ws", b))
                    p.tensor_tensor(x_all[:, b], x_all[:, b], zg[:], ALU.add).then_inc(tail.sem, 1)

            def experts_at(b, s):
                for k in range(2 * E0):
                    if s == Z_AT[k]:
                        pool.wait_ge(z_sb, b * 2 * E0 + k + 1)
                        if past(b, 1) or k >= 2:
                            pool.wait_ge(y_made, b * 2 * E0 + k - 1)
                        p.tensor_tensor(hc[:, k % 2, :], hz[:, k % 2, :], cbc[:, k // 2 % 2, :], ALU.mult).then_inc(hc_made, 1)

            def pre1_at(b, u):
                if u == 0:
                    wait_apart(pool, (pre1.sem, pre1.after("moments", b)))
                    p.tensor_scalar(rstd[:, 3, 0, :], mv[:, 3, :, 1], EPS, None, ALU.add).then_inc(pre1.sem, 1)
                    pool.wait_ge(pre1.sem, pre1.after("eps", b))
                    p.tensor_tensor(rstd[:, 3, 1, :], rstd[:, 3, 0, :], mhalf[:], ALU.pow).then_inc(pre1.sem, 1)
                if u == 3:
                    pool.wait_ge(gate1.sem, gate1.after("lsub", b))
                    p.tensor_tensor(lg[:, 1, :, 0:E1], ebase[:, :, 0:E1], lg[:, 0, :, 0:E1], ALU.pow).then_inc(gate1.sem, 1)

            def unit1(b, u, following):
                if following:
                    pre1_at(b + 1, u)

            def body1(b, following):
                for u in range(UNITS):
                    unit1(b, u, following)

            def layer1_at(pos):
                if pos == AT["ones1"]:
                    pool.wait_ge(ssm.sem, ssm.after("s", NB - 1))
                    p.memset(cpb1[:], 0.0)
                    p.memset(z_tok[:, :, P:P + 1], 1.0).then_inc(ready1, 1)
                if pos == AT["scale1"]:
                    pool.wait_ge(w_down1, 16 * 2)
                    p.tensor_tensor(fc2, fc2, vec[:, V["mult"]:V["mult"] + E1].unsqueeze(2).broadcast_to([P, E1, P]), ALU.mult)
                    p.tensor_tensor(sfc2, sfc2, vec[:, V["s_mult"]:V["s_mult"] + 2].unsqueeze(2).broadcast_to([P, 2, P]), ALU.mult)\
                        .then_inc(ready1, 1)
                for u in range(UNITS):
                    if pos == PRE1_AT[u]:
                        pre1_at(0, u)
                for n, at in enumerate(UNIT1_AT):
                    if pos == at:
                        unit1(n // UNITS, n % UNITS, True)

            def body(b, full, previous, before, following):
                alive = [(n, b - n) for n in range(3) if (full, previous, before)[n]]
                for s in range(SLOTS):
                    for n, batch in alive[::-1]:
                        tail_at(batch, s + SLOTS * n)
                        post_at(batch, s + SLOTS * n)
                        experts_at(batch, s + SLOTS * n)
                    if isinstance(b, int) and b >= NB - 1:
                        layer1_at(s + SLOTS * (b - NB + 1))
                    for g in range(NG):
                        if full and s == AT[f"values{g}"]:
                            values(b, g)
                        if following and s - SLOTS == AT[f"values{g}"]:
                            values(b + 1, g)
                    if following:
                        pre_at(b + 1, s - SLOTS)

            for s in range(-SLOTS, AT["rstd"] + 1):
                pre_at(0, s)
            p.memset(decay[:], DECAY)
            p.memset(up[:, :, 0:3], 0.0)
            p.memset(cpb[:], 0.0)
            p.memset(ebase[:], 2.718281828459045)
            p.memset(lg[:], -1.0)
            p.memset(m8v[:], -1.0)
            p.memset(v_aug[:], 0.0).then_inc(setup_pool, 1)
            pool.wait_ge(setup_pool, 2)
            p.memset(ks[32:KROWS + 2], 1.0).then_inc(setup_pool, 1)
            pool.wait_ge(setup_pool, 3)
            p.memset(v_aug[:, :, :, HD:HD + 1], 1.0).then_inc(consts, 1)
            for s in range(AT["rstd"] + 1, 0):
                pre_at(0, s)
            values(0, 0)
            values(0, 1)
            pool.wait_ge(w_first, 16 * 3)
            pool.wait_ge(w_early, 16 * 14)
            p.tensor_scalar(identb[:], ident[:], 1.0, None, ALU.mult)
            p.tensor_scalar(pick[:], pick_f[:].unsqueeze(2).broadcast_to([96, 16, P]), 1.0, None, ALU.mult).then_inc(setup_pool, 1)
            body(0, True, False, False, True)
            body(1, True, True, False, True)
            with pool.Fori(2, NB - 1) as b:
                body(b, True, True, True, True)
            body(NB - 1, True, True, True, False)
            body(NB, False, True, True, False)
            body(NB + 1, False, False, True, False)
            with pool.Fori(2, NB - 1) as b:
                body1(b, True)
        program.__exit__(None, None, None)


def lay_out(i):
    import numpy as np

    def c(a):
        return np.ascontiguousarray(a)

    def chunks(a, n):
        return a.reshape(n, P, -1).transpose(1, 0, 2)

    a = {k: np.asarray(v) for k, v in i.items()}
    f = np.float32
    vec = np.zeros((P, 96), f)
    given = {
        "conv_w": chunks(a["L0_attn_conv_w"].reshape(256, 4), 2).reshape(P, 8),
        "conv_b": chunks(a["L0_attn_conv_b"][:, None], 2).reshape(P, 2),
        "dt_b": chunks(a["L0_attn_dt_proj_b"][:, None], 2).reshape(P, 2),
        "bq": a["L0_ffn_in_proj_b"].reshape(3, P).T[:, 0:2],
        "bv": a["L0_ffn_in_proj_b"].reshape(3, P).T[:, 2:3],
        "bo": a["L0_ffn_out_proj_b"][:, None],
        "ln1_g": a["L0_ffn_ln1_g"][:, None],
        "ln1_b": a["L0_ffn_ln1_b"][:, None],
        "b1": a["L0_ffn_b1"].reshape(16, P).T,
        "bp": a["L1_attn_b_proj"][:, None],
        "fc1_b": a["L1_ffn_fc1_b"].reshape(30, P).T,
        "mult": a["L1_ffn_geglu_mult"].T,
        "sfc1_b": a["L1_ffn_s_fc1_b"].reshape(4, P).T,
        "s_mult": a["L1_ffn_s_geglu_mult"].reshape(2, P).T,
        "sb": a["L1_ffn_s_fc2_b"][:, None],
    }
    n = 0
    for name, w in VEC:
        if name in given:
            vec[:, n:n + w] = given[name]
        n += w
    rows = np.zeros((1, 3, P), f)
    rows[0, 0], rows[0, 1] = a["L0_ffn_ln2_g"], a["L0_ffn_ln2_b"]
    rows[0, 2, 0:12] = np.concatenate([a["L0_ffn_b_group"], a["L0_ffn_b_expert"].reshape(8)])
    rows[0, 2, 12:16] = (4, 3, 2, 1)
    eye = np.eye(P, dtype=f)
    return {
        "x": c(a["L0_attn_x"]),
        "ident": eye,
        "vec": vec,
        "rows": rows.reshape(3 * P),
        "head_of": c(np.repeat(np.eye(NH, dtype=f), HD, axis=1)),
        "pick": c(np.tile(np.eye(32, 16, dtype=f), (3, 1))),
        "block1": c(np.kron(np.eye(4, dtype=f), np.ones((32, 32), f))),
        "w_in0": c(a["L0_attn_in_proj_w"].T),
        "w_dt": c(chunks(a["L0_attn_dt_proj_w"].T, 2)),
        "w_out0": c(chunks(a["L0_attn_out_proj_w"].T, 2)),
        "w_qkv0": c(a["L0_ffn_in_proj_w"].T),
        "w_o0": c(a["L0_ffn_out_proj_w"].T),
        "w_gate0": c(np.concatenate([a["L0_ffn_w_group"], a["L0_ffn_w_expert"].transpose(1, 0, 2).reshape(P, 8)], axis=1)),
        "w1": c(a["L0_ffn_w1"].transpose(1, 0, 2)),
        "w2": c(a["L0_ffn_w2"].reshape(E0, 2, P, P).transpose(2, 0, 1, 3)),
        "b2": c(a["L0_ffn_b2"]),
        "w_qkv1": c(a["L1_attn_W_qkv"].T),
        "w_proj1": c(a["L1_attn_W_proj"].T),
        "w_gate1": c(a["L1_ffn_gate_w"].T),
        "fc1": c(a["L1_ffn_fc1_w"].transpose(2, 0, 1)),
        "fc2": c(a["L1_ffn_fc2_w"].transpose(2, 0, 1)),
        "fc2_b": c(a["L1_ffn_fc2_b"]),
        "sfc1": c(a["L1_ffn_s_fc1_w"].T),
        "sfc2": c(chunks(a["L1_ffn_s_fc2_w"].T, 2)),
    }


def kernel(**inputs):
    import concourse.bacc as bacc
    from concourse.bass_utils import run_bass_kernel_spmd

    nc = bacc.Bacc("TRN2", target_bir_lowering=False, num_devices=1)
    arrays = lay_out(inputs)
    d = {n: nc.dram_tensor("in_" + n, a.shape, mybir.dt.from_np(a.dtype), kind="ExternalInput").ap() for n, a in arrays.items()}
    out = nc.dram_tensor("out", [NB, S, P], F32, kind="ExternalOutput").ap()
    build(nc, d, out)
    return run_bass_kernel_spmd(nc, [{"in_" + n: a for n, a in arrays.items()}], core_ids=[0]).results[0]["out"]
```
